# Optimizing a Trainium2 kernel written in Bass

```python
import numpy as np
import jax
import jax.numpy as jnp

def _softmax(x, axis=-1):
    return jax.nn.softmax(x, axis=axis)

def _gelu(x):
    return jax.nn.gelu(x, approximate=True)

def _silu(x):
    return jax.nn.silu(x)

def _sigmoid(x):
    return jax.nn.sigmoid(x)

def _layernorm(x, axis=-1, eps=1e-05):
    m = jnp.mean(x, axis=axis, keepdims=True)
    v = jnp.var(x, axis=axis, keepdims=True)
    return (x - m) / jnp.sqrt(v + eps)

def _scatter_add(tgt, idx, src, axis=0):
    return tgt.at[idx].add(src)

def _segment_sum(src, seg, n):
    return jax.ops.segment_sum(src, seg, n)
kernel_name = 'mk_gps_d2_gnn_r8_aada1c'

def setup_inputs(seed: int=0):
    np.random.seed(seed)
    _w = jnp.asarray

    def _rec_inputs():
        import jax
        import jax.numpy as jnp
        _gk = jax.random.key(seed)
        x = -0.0002928 + 1 * jax.random.normal(jax.random.fold_in(_gk, 1), (1024, 512), jnp.float32)
        src = jax.random.randint(jax.random.fold_in(_gk, 2), (16384,), 0, 1024, jnp.int32)
        dst = jnp.minimum((1024 * jax.random.uniform(jax.random.fold_in(_gk, 3), (16384,)) ** 2.0).astype(jnp.int32), 8191)
        _o = jnp.argsort(dst, stable=True)
        src = src[_o]
        dst = dst[_o]
        return (x, src, dst)
    x, src, dst = _rec_inputs()

    def _L0_gnn_setup():
        import jax, jax.numpy as jnp
        import numpy as np
        NEG = -1000000.0
        key = jax.random.key(seed)
        ks = jax.random.split(key, 8)
        N, D_IN, D_Q, D_K, E = (1024, 512, 512, 512, 32768)
        s = 1.0 / np.sqrt(D_IN)
        return {'x': jax.random.normal(ks[0], (N, D_IN), dtype=jnp.float32), 'edge_index': jax.random.randint(ks[1], (2, E), 0, N, dtype=jnp.int64), 'Wq': jax.random.normal(ks[2], (D_IN, D_Q), dtype=jnp.float32) * s, 'bq': jax.random.normal(ks[3], (D_Q,), dtype=jnp.float32) * 0.01, 'Wk': jax.random.normal(ks[4], (D_IN, D_K), dtype=jnp.float32) * s, 'bk': jax.random.normal(ks[5], (D_K,), dtype=jnp.float32) * 0.01, 'Wv': jax.random.normal(ks[6], (D_IN, D_K), dtype=jnp.float32) * s, 'bv': jax.random.normal(ks[7], (D_K,), dtype=jnp.float32) * 0.01}
    _L0_gnn_all = _L0_gnn_setup()
    _L0_gnn_in = {k: v for k, v in _L0_gnn_all.items() if k in ('Wq', 'bq', 'Wk', 'bk', 'Wv', 'bv')}
    del _L0_gnn_all

    def _L0_mix_setup():
        import jax, jax.numpy as jnp
        import numpy as np
        DIM = 512
        HEADS = 8
        DIM_HEAD = 64
        KEY_RATIO = 4
        INNER = HEADS * DIM_HEAD
        B, N = (8, 2048)
        key = jax.random.key(seed)
        ks = jax.random.split(key, 8)
        s_in = 1.0 / np.sqrt(DIM)
        s_h = 1.0 / np.sqrt(DIM_HEAD)
        s_out = 1.0 / np.sqrt(INNER)
        return {'x': jax.random.normal(ks[0], (B, N, DIM), dtype=jnp.float32), 'W_in': jax.random.uniform(ks[1], (DIM, INNER), jnp.float32, -s_in, s_in), 'b_in': jax.random.uniform(ks[2], (INNER,), jnp.float32, -s_in, s_in), 'W_q': jax.random.uniform(ks[3], (DIM_HEAD, KEY_RATIO), jnp.float32, -s_h, s_h), 'W_k': jax.random.uniform(ks[4], (DIM_HEAD, KEY_RATIO), jnp.float32, -s_h, s_h), 'W_v': jax.random.uniform(ks[5], (DIM_HEAD, DIM_HEAD), jnp.float32, -s_h, s_h), 'W_out': jax.random.uniform(ks[6], (INNER, DIM), jnp.float32, -s_out, s_out), 'b_out': jax.random.uniform(ks[7], (DIM,), jnp.float32, -s_out, s_out)}
    _L0_mix_all = _L0_mix_setup()
    _L0_mix_in = {k: v for k, v in _L0_mix_all.items() if k in ('W_in', 'b_in', 'W_q', 'W_k', 'W_v', 'W_out', 'b_out')}
    del _L0_mix_all

    def _L0_ffn_setup():
        import jax, jax.numpy as jnp
        import numpy as np
        IN_FEATURES = 512
        FEATURES = 512
        BATCH, SEQ = (8, 1024)

        def _ste(x_orig, y_proc):
            return x_orig + jax.lax.stop_gradient(y_proc - x_orig)
        key = jax.random.key(seed)
        kx, kw = jax.random.split(key)
        x = jax.random.normal(kx, (BATCH, SEQ, IN_FEATURES), dtype=jnp.float32)
        weight = jax.random.normal(kw, (IN_FEATURES, FEATURES), dtype=jnp.float32) / np.sqrt(IN_FEATURES)
        bias = jnp.zeros((FEATURES,), dtype=jnp.float32)
        return {'x': x, 'weight': weight, 'bias': bias}
    _L0_ffn_all = _L0_ffn_setup()
    _L0_ffn_in = {k: v for k, v in _L0_ffn_all.items() if k in ('weight', 'bias')}
    del _L0_ffn_all

    def _L1_gnn_setup():
        import jax, jax.numpy as jnp
        import numpy as np
        D = 512
        H = 8
        DH = D // H
        F = 256
        L = 2
        N = 2500
        E = 40000
        EPS = 1e-05

        def _xavier(key, shape):
            fan_out, fan_in = (shape[-2], shape[-1])
            lim = float(np.sqrt(6.0 / (fan_in + fan_out)))
            return jax.random.uniform(key, shape, jnp.float32, -lim, lim)

        def _batchnorm(x, g, b):
            mu = jnp.mean(x, axis=0)
            var = jnp.mean(jnp.square(x - mu), axis=0)
            return (x - mu) * jax.lax.rsqrt(var + EPS) * g + b

        def _layernorm(x, g, b):
            mu = jnp.mean(x, axis=-1, keepdims=True)
            var = jnp.mean(jnp.square(x - mu), axis=-1, keepdims=True)
            return (x - mu) * jax.lax.rsqrt(var + EPS) * g + b
        key = jax.random.key(seed)
        ks = jax.random.split(key, 12)
        src = jax.random.normal(ks[0], (N, D), jnp.float32)
        edge_index = jax.random.randint(ks[1], (2, E), 0, N)
        return {'src': src, 'edge_index': edge_index, 'Wq': _xavier(ks[2], (L, D, D)), 'bq': jnp.zeros((L, D), jnp.float32), 'Wk': _xavier(ks[3], (L, D, D)), 'Wv': _xavier(ks[4], (L, D, D)), 'Wo': _xavier(ks[5], (L, D, D)), 'bo': jnp.zeros((L, D), jnp.float32), 'W1': _xavier(ks[6], (L, F, D)), 'b1': jnp.zeros((L, F), jnp.float32), 'W2': _xavier(ks[7], (L, D, F)), 'b2': jnp.zeros((L, D), jnp.float32), 'g1': jnp.ones((L, D), jnp.float32), 'beta1': jnp.zeros((L, D), jnp.float32), 'g2': jnp.ones((L, D), jnp.float32), 'beta2': jnp.zeros((L, D), jnp.float32), 'ln_g': jnp.ones((D,), jnp.float32), 'ln_b': jnp.zeros((D,), jnp.float32)}
    _L1_gnn_all = _L1_gnn_setup()
    _L1_gnn_in = {k: v for k, v in _L1_gnn_all.items() if k in ('Wq', 'bq', 'Wk', 'Wv', 'Wo', 'bo', 'W1', 'b1', 'W2', 'b2', 'g1', 'beta1', 'g2', 'beta2', 'ln_g', 'ln_b')}
    del _L1_gnn_all

    def _L1_mix_setup():
        import jax, jax.numpy as jnp
        import numpy as np
        DIM = 512
        HEADS = 8
        HEAD_DIM = DIM // HEADS
        B, N = (4, 1024)
        key = jax.random.key(seed)
        k1, k2, k3, k4 = jax.random.split(key, 4)
        x = jax.random.normal(k1, (B, N, DIM), dtype=jnp.float32)
        Wqkv = jax.random.normal(k2, (DIM, 3 * DIM), dtype=jnp.float32) * DIM ** (-0.5)
        Wout = jax.random.normal(k3, (DIM, DIM), dtype=jnp.float32) * DIM ** (-0.5)
        bout = jax.random.normal(k4, (DIM,), dtype=jnp.float32) * 0.01
        return {'x': x, 'Wqkv': Wqkv, 'Wout': Wout, 'bout': bout}
    _L1_mix_all = _L1_mix_setup()
    _L1_mix_in = {k: v for k, v in _L1_mix_all.items() if k in ('Wqkv', 'Wout', 'bout')}
    del _L1_mix_all

    def _L1_ffn_setup():
        import jax, jax.numpy as jnp
        import numpy as np
        MARK_AX = 0
        OP_AND = 1
        OP_OR = 2
        OP_XOR = 3
        ALU_LO = 16
        ALU_HI = 32
        AX_CARRY_LO = 48
        AX_CARRY_HI = 64
        OUTPUT_LO = 80
        OUTPUT_HI = 96
        NIB_A = 0
        NIB_B = 1
        OP_START = 16
        RESULT = 64
        GE_DIM = 160
        N_ROWS = 8
        B, S, D = (8, 512, 512)

        def _decode_nibble(x_bd, start):
            bits = x_bd[..., start:start + 16] > 0.5
            return jnp.argmax(bits, axis=-1).astype(x_bd.dtype)

        def _mlp2(x, w1, b1, w2, b2):
            h = jax.nn.relu(jnp.einsum('bsrd,de->bsre', x, w1) + b1)
            return jnp.einsum('bsrd,de->bsre', h, w2) + b2

        def _forward(x_bd, and_w1, and_b1, and_w2, and_b2, or_w1, or_b1, or_w2, or_b2, xor_w1, xor_b1, xor_w2, xor_b2):
            a_lo = _decode_nibble(x_bd, ALU_LO)
            a_hi = _decode_nibble(x_bd, ALU_HI)
            b_lo = _decode_nibble(x_bd, AX_CARRY_LO)
            b_hi = _decode_nibble(x_bd, AX_CARRY_HI)
            Bsz, Ssz, _ = x_bd.shape
            x_ge = jnp.zeros((Bsz, Ssz, N_ROWS, GE_DIM), x_bd.dtype)
            x_ge = x_ge.at[..., 0, NIB_A].set(a_lo).at[..., 1, NIB_A].set(a_hi)
            x_ge = x_ge.at[..., 0, NIB_B].set(b_lo).at[..., 1, NIB_B].set(b_hi)
            x_ge = x_ge.at[..., :, OP_START + 28].set(x_bd[..., OP_OR, None])
            x_ge = x_ge.at[..., :, OP_START + 29].set(x_bd[..., OP_XOR, None])
            x_ge = x_ge.at[..., :, OP_START + 30].set(x_bd[..., OP_AND, None])
            y_and = _mlp2(x_ge, and_w1, and_b1, and_w2, and_b2)
            y_or = _mlp2(x_ge, or_w1, or_b1, or_w2, or_b2)
            y_xor = _mlp2(x_ge, xor_w1, xor_b1, xor_w2, xor_b2)
            is_and = x_bd[..., OP_AND] > 0.5
            is_or = x_bd[..., OP_OR] > 0.5
            is_xor = x_bd[..., OP_XOR] > 0.5
            sel = jnp.where(is_and[..., None, None], y_and, jnp.where(is_or[..., None, None], y_or, y_xor))
            active = (x_bd[..., MARK_AX] >= 0.5) & (is_and | is_or | is_xor)
            res_lo = jnp.clip(jnp.round(sel[..., 0, RESULT]), 0, 15).astype(jnp.int32)
            res_hi = jnp.clip(jnp.round(sel[..., 1, RESULT]), 0, 15).astype(jnp.int32)
            amask = active.astype(x_bd.dtype)[..., None]
            add_lo = 2.0 * jax.nn.one_hot(res_lo, 16, dtype=x_bd.dtype) * amask
            add_hi = 2.0 * jax.nn.one_hot(res_hi, 16, dtype=x_bd.dtype) * amask
            out = x_bd.at[..., OUTPUT_LO:OUTPUT_LO + 16].add(add_lo)
            out = out.at[..., OUTPUT_HI:OUTPUT_HI + 16].add(add_hi)
            return out
        key = jax.random.key(seed)
        ks = jax.random.split(key, 7)
        inp = {'x_bd': jax.random.uniform(ks[0], (B, S, D), dtype=jnp.float32)}
        for i, op in enumerate(['and', 'or', 'xor']):
            inp[op + '_w1'] = jax.random.normal(ks[1 + 2 * i], (GE_DIM, GE_DIM), jnp.float32) * 0.08
            inp[op + '_b1'] = jnp.zeros((GE_DIM,), jnp.float32)
            inp[op + '_w2'] = jax.random.normal(ks[2 + 2 * i], (GE_DIM, GE_DIM), jnp.float32) * 0.08
            inp[op + '_b2'] = jnp.zeros((GE_DIM,), jnp.float32)
        return inp
    _L1_ffn_all = _L1_ffn_setup()
    _L1_ffn_in = {k: v for k, v in _L1_ffn_all.items() if k in ('and_w1', 'and_b1', 'and_w2', 'and_b2', 'or_w1', 'or_b1', 'or_w2', 'or_b2', 'xor_w1', 'xor_b1', 'xor_w2', 'xor_b2')}
    del _L1_ffn_all
    return {'x': x, 'src': src, 'dst': dst, 'L0_gnn_Wq': _L0_gnn_in['Wq'], 'L0_gnn_bq': _L0_gnn_in['bq'], 'L0_gnn_Wk': _L0_gnn_in['Wk'], 'L0_gnn_bk': _L0_gnn_in['bk'], 'L0_gnn_Wv': _L0_gnn_in['Wv'], 'L0_gnn_bv': _L0_gnn_in['bv'], 'L0_mix_W_in': _L0_mix_in['W_in'], 'L0_mix_b_in': _L0_mix_in['b_in'], 'L0_mix_W_q': _L0_mix_in['W_q'], 'L0_mix_W_k': _L0_mix_in['W_k'], 'L0_mix_W_v': _L0_mix_in['W_v'], 'L0_mix_W_out': _L0_mix_in['W_out'], 'L0_mix_b_out': _L0_mix_in['b_out'], 'L0_ffn_weight': _L0_ffn_in['weight'], 'L0_ffn_bias': _L0_ffn_in['bias'], 'L1_gnn_Wq': _L1_gnn_in['Wq'], 'L1_gnn_bq': _L1_gnn_in['bq'], 'L1_gnn_Wk': _L1_gnn_in['Wk'], 'L1_gnn_Wv': _L1_gnn_in['Wv'], 'L1_gnn_Wo': _L1_gnn_in['Wo'], 'L1_gnn_bo': _L1_gnn_in['bo'], 'L1_gnn_W1': _L1_gnn_in['W1'], 'L1_gnn_b1': _L1_gnn_in['b1'], 'L1_gnn_W2': _L1_gnn_in['W2'], 'L1_gnn_b2': _L1_gnn_in['b2'], 'L1_gnn_g1': _L1_gnn_in['g1'], 'L1_gnn_beta1': _L1_gnn_in['beta1'], 'L1_gnn_g2': _L1_gnn_in['g2'], 'L1_gnn_beta2': _L1_gnn_in['beta2'], 'L1_gnn_ln_g': _L1_gnn_in['ln_g'], 'L1_gnn_ln_b': _L1_gnn_in['ln_b'], 'L1_mix_Wqkv': _L1_mix_in['Wqkv'], 'L1_mix_Wout': _L1_mix_in['Wout'], 'L1_mix_bout': _L1_mix_in['bout'], 'L1_ffn_and_w1': _L1_ffn_in['and_w1'], 'L1_ffn_and_b1': _L1_ffn_in['and_b1'], 'L1_ffn_and_w2': _L1_ffn_in['and_w2'], 'L1_ffn_and_b2': _L1_ffn_in['and_b2'], 'L1_ffn_or_w1': _L1_ffn_in['or_w1'], 'L1_ffn_or_b1': _L1_ffn_in['or_b1'], 'L1_ffn_or_w2': _L1_ffn_in['or_w2'], 'L1_ffn_or_b2': _L1_ffn_in['or_b2'], 'L1_ffn_xor_w1': _L1_ffn_in['xor_w1'], 'L1_ffn_xor_b1': _L1_ffn_in['xor_b1'], 'L1_ffn_xor_w2': _L1_ffn_in['xor_w2'], 'L1_ffn_xor_b2': _L1_ffn_in['xor_b2']}

def reference(x, src, dst, L0_gnn_Wq, L0_gnn_bq, L0_gnn_Wk, L0_gnn_bk, L0_gnn_Wv, L0_gnn_bv, L0_mix_W_in, L0_mix_b_in, L0_mix_W_q, L0_mix_W_k, L0_mix_W_v, L0_mix_W_out, L0_mix_b_out, L0_ffn_weight, L0_ffn_bias, L1_gnn_Wq, L1_gnn_bq, L1_gnn_Wk, L1_gnn_Wv, L1_gnn_Wo, L1_gnn_bo, L1_gnn_W1, L1_gnn_b1, L1_gnn_W2, L1_gnn_b2, L1_gnn_g1, L1_gnn_beta1, L1_gnn_g2, L1_gnn_beta2, L1_gnn_ln_g, L1_gnn_ln_b, L1_mix_Wqkv, L1_mix_Wout, L1_mix_bout, L1_ffn_and_w1, L1_ffn_and_b1, L1_ffn_and_w2, L1_ffn_and_b2, L1_ffn_or_w1, L1_ffn_or_b1, L1_ffn_or_w2, L1_ffn_or_b2, L1_ffn_xor_w1, L1_ffn_xor_b1, L1_ffn_xor_w2, L1_ffn_xor_b2):
    import jax
    import jax.numpy as jnp

    def _L0_gnn_ref(x, edge_index, Wq, bq, Wk, bk, Wv, bv):
        import jax, jax.numpy as jnp
        import numpy as np
        NEG = -1000000.0
        q = x @ Wq + bq
        k = x @ Wk + bk
        v = x @ Wv + bv
        N = x.shape[0]
        adj = jnp.zeros((N, N), dtype=x.dtype).at[edge_index[0], edge_index[1]].set(1.0)
        a = q @ k.T / jnp.sqrt(jnp.asarray(q.shape[-1], dtype=x.dtype))
        a = a * adj + (1.0 - adj) * NEG
        attn = jax.nn.softmax(a, axis=-1)
        return attn @ v

    def _L0_mix_ref(x, W_in, b_in, W_q, W_k, W_v, W_out, b_out):
        import jax, jax.numpy as jnp
        import numpy as np
        DIM = 512
        HEADS = 8
        DIM_HEAD = 64
        KEY_RATIO = 4
        INNER = HEADS * DIM_HEAD
        B, N = (8, 2048)
        Bx, Nx, _ = x.shape
        x_mid = x @ W_in + b_in
        x_mid = x_mid.reshape(Bx, Nx, HEADS, DIM_HEAD).transpose(0, 2, 1, 3)
        q = jnp.einsum('bhnd,dr->bhnr', x_mid, W_q)
        k = jnp.einsum('bhnd,dr->bhnr', x_mid, W_k)
        v = jnp.einsum('bhnd,dc->bhnc', x_mid, W_v)
        q = jax.nn.softmax(q, axis=-1)
        k = jax.nn.softmax(k, axis=-2)
        kv = jnp.einsum('bhnr,bhnc->bhrc', k, v)
        qkv = jnp.einsum('bhnr,bhrc->bhnc', q, kv)
        qkv = qkv.transpose(0, 2, 1, 3).reshape(Bx, Nx, INNER)
        return qkv @ W_out + b_out

    def _L0_ffn_ref(x, weight, bias):
        import jax, jax.numpy as jnp
        import numpy as np
        IN_FEATURES = 512
        FEATURES = 512
        BATCH, SEQ = (8, 1024)

        def _ste(x_orig, y_proc):
            return x_orig + jax.lax.stop_gradient(y_proc - x_orig)
        weight_centered = weight - jnp.mean(weight)
        weight_bin = jnp.sign(weight_centered)
        weight_bin_ste = _ste(weight, weight_bin)
        scale_gamma = jnp.mean(jnp.abs(weight))
        effective_weight = weight_bin_ste * scale_gamma
        y = jnp.dot(x, effective_weight) + bias
        act_clipped = jnp.clip(y, -1.0, 1.0)
        quant_dequant = jnp.round(act_clipped * 7.0) / 7.0
        return _ste(y, quant_dequant)

    def _L1_gnn_ref(src, edge_index, Wq, bq, Wk, Wv, Wo, bo, W1, b1, W2, b2, g1, beta1, g2, beta2, ln_g, ln_b):
        import jax, jax.numpy as jnp
        import numpy as np
        D = 512
        H = 8
        DH = D // H
        F = 256
        L = 2
        N = 2500
        E = 40000
        EPS = 1e-05

        def _xavier(key, shape):
            fan_out, fan_in = (shape[-2], shape[-1])
            lim = float(np.sqrt(6.0 / (fan_in + fan_out)))
            return jax.random.uniform(key, shape, jnp.float32, -lim, lim)

        def _batchnorm(x, g, b):
            mu = jnp.mean(x, axis=0)
            var = jnp.mean(jnp.square(x - mu), axis=0)
            return (x - mu) * jax.lax.rsqrt(var + EPS) * g + b

        def _layernorm(x, g, b):
            mu = jnp.mean(x, axis=-1, keepdims=True)
            var = jnp.mean(jnp.square(x - mu), axis=-1, keepdims=True)
            return (x - mu) * jax.lax.rsqrt(var + EPS) * g + b
        n = src.shape[0]
        scaling = float(DH) ** (-0.5)
        tgt = edge_index[1]
        srcidx = edge_index[0]
        x = src
        for l in range(L):
            q = ((x @ Wq[l].T + bq[l]) * scaling).reshape(n, H, DH)
            k = (x @ Wk[l].T).reshape(n, H, DH)
            v = (x @ Wv[l].T).reshape(n, H, DH)
            scores = jnp.einsum('ehd,ehd->eh', q[tgt], k[srcidx])
            m = jax.ops.segment_max(scores, tgt, num_segments=n)
            p = jnp.exp(scores - m[tgt])
            s = jax.ops.segment_sum(p, tgt, num_segments=n)
            w = p / (s[tgt] + 1e-16)
            agg = jax.ops.segment_sum(w[:, :, None] * v[srcidx], tgt, num_segments=n)
            attn = agg.reshape(n, D) @ Wo[l].T + bo[l]
            x = _batchnorm(x + attn, g1[l], beta1[l])
            ff = jax.nn.relu(x @ W1[l].T + b1[l]) @ W2[l].T + b2[l]
            x = _batchnorm(x + ff, g2[l], beta2[l])
        return _layernorm(x, ln_g, ln_b)

    def _L1_mix_ref(x, Wqkv, Wout, bout):
        import jax, jax.numpy as jnp
        import numpy as np
        DIM = 512
        HEADS = 8
        HEAD_DIM = DIM // HEADS
        B, N = (4, 1024)
        b, n, d = x.shape
        h, hd = (HEADS, HEAD_DIM)
        qkv = x @ Wqkv
        q, k, v = jnp.split(qkv, 3, axis=-1)

        def to_heads(t):
            return t.reshape(b, n, h, hd).transpose(0, 2, 1, 3)
        q, k, v = (to_heads(q), to_heads(k), to_heads(v))
        q = jax.nn.elu(q) + 1.0
        k = jax.nn.elu(k) + 1.0
        kv = jnp.einsum('bhnd,bhne->bhde', k, v)
        z = 1.0 / (jnp.einsum('bhnd,bhd->bhn', q, k.sum(axis=2)) + 1e-06)
        out = jnp.einsum('bhnd,bhde->bhne', q, kv) * z[..., None]
        out = out.transpose(0, 2, 1, 3).reshape(b, n, d)
        return out @ Wout + bout

    def _L1_ffn_ref(x_bd, and_w1, and_b1, and_w2, and_b2, or_w1, or_b1, or_w2, or_b2, xor_w1, xor_b1, xor_w2, xor_b2):
        import jax, jax.numpy as jnp
        import numpy as np
        MARK_AX = 0
        OP_AND = 1
        OP_OR = 2
        OP_XOR = 3
        ALU_LO = 16
        ALU_HI = 32
        AX_CARRY_LO = 48
        AX_CARRY_HI = 64
        OUTPUT_LO = 80
        OUTPUT_HI = 96
        NIB_A = 0
        NIB_B = 1
        OP_START = 16
        RESULT = 64
        GE_DIM = 160
        N_ROWS = 8
        B, S, D = (8, 512, 512)

        def _decode_nibble(x_bd, start):
            bits = x_bd[..., start:start + 16] > 0.5
            return jnp.argmax(bits, axis=-1).astype(x_bd.dtype)

        def _mlp2(x, w1, b1, w2, b2):
            h = jax.nn.relu(jnp.einsum('bsrd,de->bsre', x, w1) + b1)
            return jnp.einsum('bsrd,de->bsre', h, w2) + b2

        def _forward(x_bd, and_w1, and_b1, and_w2, and_b2, or_w1, or_b1, or_w2, or_b2, xor_w1, xor_b1, xor_w2, xor_b2):
            a_lo = _decode_nibble(x_bd, ALU_LO)
            a_hi = _decode_nibble(x_bd, ALU_HI)
            b_lo = _decode_nibble(x_bd, AX_CARRY_LO)
            b_hi = _decode_nibble(x_bd, AX_CARRY_HI)
            Bsz, Ssz, _ = x_bd.shape
            x_ge = jnp.zeros((Bsz, Ssz, N_ROWS, GE_DIM), x_bd.dtype)
            x_ge = x_ge.at[..., 0, NIB_A].set(a_lo).at[..., 1, NIB_A].set(a_hi)
            x_ge = x_ge.at[..., 0, NIB_B].set(b_lo).at[..., 1, NIB_B].set(b_hi)
            x_ge = x_ge.at[..., :, OP_START + 28].set(x_bd[..., OP_OR, None])
            x_ge = x_ge.at[..., :, OP_START + 29].set(x_bd[..., OP_XOR, None])
            x_ge = x_ge.at[..., :, OP_START + 30].set(x_bd[..., OP_AND, None])
            y_and = _mlp2(x_ge, and_w1, and_b1, and_w2, and_b2)
            y_or = _mlp2(x_ge, or_w1, or_b1, or_w2, or_b2)
            y_xor = _mlp2(x_ge, xor_w1, xor_b1, xor_w2, xor_b2)
            is_and = x_bd[..., OP_AND] > 0.5
            is_or = x_bd[..., OP_OR] > 0.5
            is_xor = x_bd[..., OP_XOR] > 0.5
            sel = jnp.where(is_and[..., None, None], y_and, jnp.where(is_or[..., None, None], y_or, y_xor))
            active = (x_bd[..., MARK_AX] >= 0.5) & (is_and | is_or | is_xor)
            res_lo = jnp.clip(jnp.round(sel[..., 0, RESULT]), 0, 15).astype(jnp.int32)
            res_hi = jnp.clip(jnp.round(sel[..., 1, RESULT]), 0, 15).astype(jnp.int32)
            amask = active.astype(x_bd.dtype)[..., None]
            add_lo = 2.0 * jax.nn.one_hot(res_lo, 16, dtype=x_bd.dtype) * amask
            add_hi = 2.0 * jax.nn.one_hot(res_hi, 16, dtype=x_bd.dtype) * amask
            out = x_bd.at[..., OUTPUT_LO:OUTPUT_LO + 16].add(add_lo)
            out = out.at[..., OUTPUT_HI:OUTPUT_HI + 16].add(add_hi)
            return out
        return _forward(x_bd, and_w1, and_b1, and_w2, and_b2, or_w1, or_b1, or_w2, or_b2, xor_w1, xor_b1, xor_w2, xor_b2)
    edge_index = jnp.stack([src, dst])
    xn = _layernorm(x, axis=-1)
    x = x + _L0_gnn_ref(xn, edge_index, L0_gnn_Wq, L0_gnn_bq, L0_gnn_Wk, L0_gnn_bk, L0_gnn_Wv, L0_gnn_bv) + _L0_mix_ref(xn[None], L0_mix_W_in, L0_mix_b_in, L0_mix_W_q, L0_mix_W_k, L0_mix_W_v, L0_mix_W_out, L0_mix_b_out)[0]
    x = x + _L0_ffn_ref(_layernorm(x, axis=-1)[None], L0_ffn_weight, L0_ffn_bias)[0]
    xn = _layernorm(x, axis=-1)
    x = x + _L1_gnn_ref(xn, edge_index, L1_gnn_Wq, L1_gnn_bq, L1_gnn_Wk, L1_gnn_Wv, L1_gnn_Wo, L1_gnn_bo, L1_gnn_W1, L1_gnn_b1, L1_gnn_W2, L1_gnn_b2, L1_gnn_g1, L1_gnn_beta1, L1_gnn_g2, L1_gnn_beta2, L1_gnn_ln_g, L1_gnn_ln_b) + _L1_mix_ref(xn[None], L1_mix_Wqkv, L1_mix_Wout, L1_mix_bout)[0]
    x = x + _L1_ffn_ref(_layernorm(x, axis=-1)[None], L1_ffn_and_w1, L1_ffn_and_b1, L1_ffn_and_w2, L1_ffn_and_b2, L1_ffn_or_w1, L1_ffn_or_b1, L1_ffn_or_w2, L1_ffn_or_b2, L1_ffn_xor_w1, L1_ffn_xor_b1, L1_ffn_xor_w2, L1_ffn_xor_b2)[0]
    return x

_drawn_inputs = setup_inputs


def setup_inputs(seed=0):
    import zlib

    import numpy as np

    out = dict(_drawn_inputs(seed))
    spreads = {'L0_ffn_bias': (0.0, 0.1),
     'L1_gnn_bq': (0.0, 0.305),
     'L1_gnn_bo': (0.0, 2.0),
     'L1_gnn_b1': (0.0, 0.285),
     'L1_gnn_b2': (0.0, 2.0),
     'L1_gnn_g1': (1.0, 0.2),
     'L1_gnn_beta1': (0.0, 0.1),
     'L1_gnn_g2': (1.0, 0.2),
     'L1_gnn_beta2': (0.0, 0.1),
     'L1_gnn_ln_g': (1.0, 0.2),
     'L1_gnn_ln_b': (0.0, 0.1),
     'L1_ffn_and_b1': (0.0, 2.0),
     'L1_ffn_and_b2': (0.0, 0.8),
     'L1_ffn_or_b1': (0.0, 2.0),
     'L1_ffn_or_b2': (0.0, 2.0),
     'L1_ffn_xor_b1': (0.0, 2.0),
     'L1_ffn_xor_b2': (0.0, 0.1)}
    factors = {'L0_gnn_bq': 5.398,
     'L0_gnn_bk': 200.0,
     'L0_gnn_bv': 2.861,
     'L0_mix_W_in': 3.624,
     'L0_mix_b_in': 3.168,
     'L0_mix_W_q': 8.0,
     'L0_mix_W_k': 4.251,
     'L1_mix_bout': 8.0,
     'L1_ffn_and_w1': 200.0,
     'L1_ffn_and_w2': 200.0,
     'L1_ffn_or_w1': 200.0,
     'L1_ffn_or_w2': 200.0,
     'L1_ffn_xor_w2': 200.0,
     'L1_ffn_xor_w1': 64.0}
    for name, (base, spread) in spreads.items():
        noise = np.random.default_rng([zlib.crc32(name.encode()), seed]).standard_normal(out[name].shape)
        drawn = base * np.exp(spread * noise) if base else spread * noise
        out[name] = jnp.asarray(drawn.astype(out[name].dtype))
    for name, factor in factors.items():
        out[name] = (out[name] * factor).astype(out[name].dtype)
    return out
```

```python
import numpy as np
import concourse.bass as bass
from concourse import mybir
from contextlib import ExitStack

N = 1024
D = 512
E = 16384
P = 128
TT = N // P
FC = D // P
EC = E // P
H = 8
DH = D // H
R = 4
L = 2
F2 = 256
GE = 160
EPS = 1e-5
NO_EDGE = -1e30
NEG = -1e6
MAGIC = 1.5 * 2.0 ** 23
RING = 4
SHIFT = P

UNITS = H * TT
LAG = 2


def attention_order():
    order = [("q", 0), ("k", 0)]
    for n in range(UNITS + LAG + 1):
        if n % 16 == 8 and n // 16 + 1 < H // 2:
            order += [("q", n // 16 + 1), ("k", n // 16 + 1)]
        if n < UNITS:
            order.append(("score", n))
        m = n - LAG
        if 0 <= m < UNITS:
            order.append(("turn", m))
            if m % 8 == 7:
                order.append(("rsum", m // 8))
        if m >= 8 and m % 8 == 0:
            order += [("rsum_bc", m // 8 - 1), ("agg", m // 8 - 1)]
    return order


def job_table():
    jobs = []

    def add(name, count, engines):
        for i in range(count):
            jobs.append(((name, i), engines[i % len(engines)]))

    A, V = "act", "dve"
    add("bounds", 1, [V])
    add("xT0", FC, [V, A])
    add("counts", TT, [A])
    add("adjT", TT, [V, A])
    for name in ("q0", "k0", "v0"):
        add(name, 4, [V, A])
    for n in range(TT + LAG + 1):
        if n < TT:
            jobs.append((("score0", n), V))
        if 0 <= n - LAG < TT:
            jobs.append((("turn0", n - LAG), A))
        if n - LAG >= 1:
            jobs.append((("attn0", n - LAG - 1), V))
    for name in ("wqk", "bq0", "bk0", "klog", "qlog", "ekt", "kx", "kxT", "xmT", "kvT", "mixM", "qsT"):
        add(name, 1, [V])
    add("mixout", 4, [V])
    add("wsum", 1, [V])
    add("xT1", FC, [V, A])
    add("ffn", 4, [V])
    add("xT2", FC, [V, A])
    add("k1", 4, [V])
    add("v1", 4, [A])
    add("kv1", 1, [V])
    add("q1", 4, [V])
    add("mixM1", 2, [V, A])
    add("den", 4, [V])
    add("mixout1", 4, [V])
    for l in range(L):
        add(f"gv{l}", 4, [V, A])
        for step, i in attention_order():
            engine = {"q": V, "k": A, "score": V, "turn": (V, A)[i % 2], "rsum": V, "rsum_bc": A, "agg": V}[step]
            jobs.append(((f"{step}{l}g", i), engine))
        add(f"wo{l}", FC, [V])
        add(f"h{l}", 2, [A])
        add(f"f{l}", FC, [V])
    add("gT", 4, [V, A])
    add("fT", 4, [V])
    add("hid", 16, [V])
    return jobs


JOBS = job_table()
INDEX = {name: j for j, (name, _) in enumerate(JOBS)}
EVAC_COUNT = {}
_seen = {"act": 0, "dve": 0}
for _name, _engine in JOBS:
    _seen[_engine] += 1
    EVAC_COUNT[_name] = _seen[_engine]

COLS = {}


def _col(name, n):
    COLS[name] = (sum(w for _, w in COLS.values()), n)


for _n in ("bq", "bk", "b_in"):
    _col(_n, FC)
for _l in range(L):
    for _n in ("gbq", "gbo", "gb2", "g1", "be1", "g2", "be2"):
        _col(f"{_n}{_l}", FC)
    _col(f"gb1{_l}", 2)
NCOL = sum(w for _, w in COLS.values())
ROWS = ["L0_gnn_bv", "L0_mix_b_out", "L0_ffn_bias", "L1_mix_bout", "L1_gnn_ln_g", "L1_gnn_ln_b"]

WEIGHTS = ["q0", "k0", "v0", "winT", "win", "wout", "ffn", "k1", "v1", "q1", "wout1"]
for _l in range(L):
    WEIGHTS += [f"gv{_l}", f"gq{_l}", f"gk{_l}", f"go{_l}", f"w12{_l}"]
WSLOTS = 3


def build(nc, a, out):
    fp32, bf16, fp16, i32 = mybir.dt.float32, mybir.dt.bfloat16, mybir.dt.float16, mybir.dt.int32
    ALU = mybir.AluOpType
    ACT = mybir.ActivationFunctionType
    AX = mybir.AxisListType
    ctx = ExitStack()
    with ctx:
        def sb(name, shape, dt=fp32):
            return ctx.enter_context(nc.sbuf_tensor(name, shape, dt))

        def sem(name):
            return ctx.enter_context(nc.semaphore(name))

        X = sb("X", [P, TT, D])
        XN = sb("XN", [P, TT, D])
        XT = sb("XT", [P, FC, N])
        QZ = sb("QZ", [P, 2, 2, N])
        KR = sb("KR", [P, 2, N])
        AG = sb("AG", [P, FC, N])
        MASK = sb("MASK", [P, TT, N])
        PT = sb("PT", [P, 12288])
        SM = sb("SM", [P, 2, N])
        W = sb("W", [P, WSLOTS, FC * D])
        BC = sb("BC", [P, 2, D])
        ident = sb("ident", [P, P])
        ones = sb("ones", [P, P])
        sel = sb("sel", [8, 4, P])
        cols = sb("cols", [P, NCOL])
        st = sb("st", [P, TT, 6])
        mv = sb("mv", [P, TT, 2])
        rstd = sb("rstd", [P, TT])
        nm = sb("nm", [P, 8])
        ls = sb("ls", [P, 2, 8])
        rl = sb("rl", [P, 8])
        tiny = sb("tiny", [P, 16])

        psum = ctx.enter_context(nc.psum_tensor("slots", [P, 4, N], fp32))

        flat = lambda t: t[:].rearrange("p a b -> p (a b)")
        qz = QZ[:].rearrange("p a b c -> p (a b c)")
        ag, kr = flat(AG), flat(KR)
        iota = PT[:, 0:512].bitcast(fp16)
        srcrow = PT[:, 512:2560].bitcast(bf16).rearrange("p (r n) -> p r n", r=RING)
        dstrow = PT[:, 2560:2816].bitcast(bf16).rearrange("p (r n) -> p r n", r=RING)
        idx_i = PT[:, 2816:3200].bitcast(i32)
        dst_f, src_f, drow_f = PT[:, 3200:3328], PT[:, 3328:3456], PT[:, 3456:3584]
        zeros = PT[:, 3584:3584 + 256].bitcast(bf16)
        cmin, cmax = PT[:, 3840:3841], PT[:, 3841:3842]
        brow = PT[0:1, 3842:3842 + 256]
        lo8 = ag[0:1, 0:1024].rearrange("p (t c) -> p t c", t=TT)
        c8 = ag[0:1, 1024:2048].rearrange("p (t c) -> p t c", t=TT)
        relA = ag[0:1, 2048:3072].rearrange("p (t c) -> p t c", t=TT)
        relB = ag[0:1, 3072:4096].rearrange("p (t c) -> p t c", t=TT)
        bnd = PT[0:1, 4100:4132]
        bnd_i = PT[0:1, 4132:4164].bitcast(i32)
        QT0, KT0 = qz.rearrange("p (c n) -> p c n", c=FC), AG
        V0 = PT[:, 0:4096].rearrange("p (t d) -> p t d", t=TT)
        adj0 = PT[:, 4096:8192].bitcast(bf16).rearrange("p (t n) -> p t n", t=TT)
        negm = PT[:, 8192:10240].rearrange("p (r n) -> p r n", r=2)
        P0T = PT[:, 10240:12288].rearrange("p (r s n) -> p r s n", r=2, s=TT)
        o = [0]

        def part(n, rows=P):
            o[0] += n
            return qz[0:rows, o[0] - n:o[0]]

        bdqk = part(256).rearrange("p (c n) -> p c n", c=FC)
        bdv = part(128)
        wqk = part(256).rearrange("p (c n) -> p c n", c=FC)
        b_bc = part(512).rearrange("p (c n) -> p c n", c=FC)
        bq_bc = part(32)
        bk_col = part(1, 32)
        part(7)
        ql = part(256).rearrange("p (t n) -> p t n", t=TT)
        qm = part(64)
        qr = part(64)
        ek = part(256).rearrange("p (t n) -> p t n", t=TT)
        kx = part(512, 32)
        kxT = part(128).rearrange("p (c n) -> p c n", c=FC)
        xmT = part(128).rearrange("p (c n) -> p c n", c=FC)
        hm = part(128).rearrange("p (c n) -> p c n", c=FC)
        kvT = part(128).rearrange("p (c n) -> p c n", c=FC)
        mixM = part(512, 32)
        kmax, ksum, krec = part(1, 32), part(1, 32), part(1, 32)
        ekT, qsT = KR[0:32, 0, :], KR[0:32, 1, :]
        K1 = PT[:, 0:4096].rearrange("p (t d) -> p t d", t=TT)
        V1 = PT[:, 4096:8192].rearrange("p (t d) -> p t d", t=TT)
        kvT1 = PT[:, 8192:8704].rearrange("p (c n) -> p c n", c=FC)
        KS1 = PT[:, 8704:9216].rearrange("p (c n) -> p c n", c=FC)
        M1 = PT[:, 9216:11264].rearrange("p (c n) -> p c n", c=FC)
        blk = PT[:, 11264:11392]
        QT1, Z1 = QT0, AG
        PTr = PT[:, :].rearrange("p (b s n) -> p b s n", b=3, s=TT)
        GV = XN
        rbc = BC[:, 0, :]
        rT = BC[0:8, 1, 0:128]
        G = PT[:, 0:4096].rearrange("p (t d) -> p t d", t=TT)
        W1s = qz[0:6, 0:480]
        w2bc = qz[:, 512:992]
        b2bc = qz[:, 992:995]
        Fx = qz[:, 1024:1152].rearrange("p (t r j) -> p t r j", t=TT, r=2)
        FT = qz[0:6, 2048:4096]
        bits = ag[:, 0:512].rearrange("p (t j n) -> p t j n", t=TT, j=4)
        m16 = ag[:, 512:544].rearrange("p (t j) -> p t j", t=TT)
        i16 = ag[:, 544:560]
        i16m = ag[:, 560:576]
        flags = ag[:, 576:608].rearrange("p (t j) -> p t j", t=TT)
        ysel = ag[:, 608:656].rearrange("p (t r k) -> p t r k", t=TT, r=2)
        pick = ag[:, 656:680].rearrange("p (t k) -> p t k", t=TT)
        res = ag[:, 688:704].rearrange("p (t r) -> p t r", t=TT)
        act_on = ag[:, 704:712]
        oneh = ag[:, 768:1024].rearrange("p (t r n) -> p t r n", t=TT, r=2)
        hidb = [ag[:, 1024:1504], ag[:, 1536:2016]]
        yk = ag[:, 2048:2096].rearrange("p (t r k) -> p t r k", t=TT, r=2)

        psum_full, dve_evacuated, act_evacuated = sem("psum_full"), sem("dve_evacuated"), sem("act_evacuated")
        w_loaded = [sem(f"w_loaded{s}") for s in range(WSLOTS)]
        row_loaded = [sem(f"row_loaded{s}") for s in range(2)]
        x_loaded, idx_loaded, cols_loaded, bd_loaded, nib_loaded = (
            sem(n) for n in ("x_loaded", "idx_loaded", "cols_loaded", "bd_loaded", "nib_loaded"))
        const_made, bd_cleared, blk_made, q_cleared, i16_made = (
            sem(n) for n in ("const_made", "bd_cleared", "blk_made", "q_cleared", "i16_made"))
        pool_link, dve_link, act_link = sem("pool_link"), sem("dve_link"), sem("act_link")
        bounds_made, onehot_ready, onehot_used, mm_bounds = (
            sem(n) for n in ("bounds_made", "onehot_ready", "onehot_used", "minmax_made"))
        counts_floored, logs_taken, mask_made = sem("counts_floored"), sem("logs_taken"), sem("mask_made")
        negm_made, masked0, probs0, x_biased = sem("negm_made"), sem("masked0"), sem("probs0"), sem("x_biased")
        rows_normed, var_ready, std_ready = sem("rows_normed"), sem("var_ready"), sem("std_ready")
        mix_bias, mix_kexp, mix_krdy, mix_kscaled, mix_qs, mix_qe = (
            sem(n) for n in ("b_broadcast", "keys_max_ready", "keys_exp", "mix_kscaled", "mix_queries_ready", "mix_qexp"))
        wstat, wsign, wmean, ffn_row = sem("w_sums"), sem("w_signs"), sem("w_mean"), sem("ffn_row_used")
        kneg, kexp, x1_biased = sem("min_ready"), sem("elu_exp"), sem("x1_biased")
        probs, recips, bn_ready, state_ready = sem("probs"), sem("recips"), sem("bn_var_ready"), sem("state_ready")
        hid_ready, stored = sem("features_ready"), sem("stored")

        slot_of = lambda name, i: psum[:, INDEX[(name, i)] % 4, :]

        def evacuated(name, i):
            engine = JOBS[INDEX[(name, i)]][1]
            return (dve_evacuated if engine == "dve" else act_evacuated), EVAC_COUNT[(name, i)]

        def full(eng, name, i):
            eng.wait_ge(psum_full, INDEX[(name, i)] + 1)
            return slot_of(name, i)

        def done(eng, name, i):
            eng.wait_ge(*evacuated(name, i))

        def col(name, c=None):
            at, w = COLS[name]
            return cols[:, at:at + w] if c is None else cols[:, at + c:at + c + 1]

        def wtile(name):
            s = WEIGHTS.index(name) % WSLOTS
            return W[:, s, :].rearrange("p (k n) -> p k n", k=FC)

        def w_ready(eng, name):
            n = WEIGHTS.index(name)
            eng.wait_ge(w_loaded[n % WSLOTS], 16 * (n // WSLOTS + 1))

        def row(name):
            return BC[:, ROWS.index(name) % 2, :]

        def row_ready(eng, name):
            n = ROWS.index(name)
            eng.wait_ge(row_loaded[n % 2], 16 * (n // 2 + 1))

        LAST_USE = {
            "q0": ("q0", 3), "k0": ("k0", 3), "v0": ("v0", 3), "winT": ("wqk", 0), "win": ("xmT", 0),
            "wout": ("mixM", 0), "ffn": ("ffn", 3), "k1": ("k1", 3), "v1": ("v1", 3), "q1": ("q1", 3),
            "wout1": ("mixM1", 1)}
        for l in range(L):
            LAST_USE.update({f"gv{l}": (f"gv{l}", 3), f"gq{l}": (f"q{l}g", 3), f"gk{l}": (f"k{l}g", 3),
                             f"go{l}": (f"wo{l}", 3), f"w12{l}": (f"f{l}", 3)})

        block = ctx.enter_context(nc.Block())

        @block.sync
        def _(sp):
            sp.dma_start(idx_i, a["idx"]).then_inc(idx_loaded, 16)
            sp.dma_start(X[:], a["x"].rearrange("(t p) d -> p t d", p=P)).then_inc(x_loaded, 16)
            sp.dma_start(cols[:], a["cols"]).then_inc(cols_loaded, 16)

            def load_row(n):
                sp.dma_start(BC[:, n % 2, :], a["rows"][n:n + 1, :].broadcast_to([P, D])).then_inc(row_loaded[n % 2], 16)

            def load_weight(name):
                n = WEIGHTS.index(name)
                if n >= WSLOTS:
                    sp.wait_ge(psum_full, INDEX[LAST_USE[WEIGHTS[n - WSLOTS]]] + 1)
                if name.startswith("w12"):
                    l = int(name[-1])
                    sp.dma_start(W[:, n % WSLOTS, :], a["w12"][l]).then_inc(w_loaded[n % WSLOTS], 16)
                else:
                    sp.dma_start(wtile(name), a[name].rearrange("(k p) n -> p k n", p=P)).then_inc(w_loaded[n % WSLOTS], 16)

            load_row(0)
            load_row(1)
            for name in WEIGHTS[:5]:
                load_weight(name)
            sp.wait_ge(bd_cleared, 1)
            for h in range(H):
                p0, c = (h % 2) * DH, h // 2
                sp.dma_start(bdqk[p0:p0 + DH, c, R * h:R * h + R], a["mq"]).then_inc(bd_loaded, 16)
                sp.dma_start(bdqk[p0:p0 + DH, c, 32 + R * h:32 + R * h + R], a["mk"]).then_inc(bd_loaded, 16)
            for e in range(2):
                sp.dma_start(bdv[e * DH:(e + 1) * DH, e * DH:(e + 1) * DH], a["mv"]).then_inc(bd_loaded, 16)
            sp.wait_ge(x_biased, TT)
            load_row(2)
            load_row(3)
            for name in WEIGHTS[5:]:
                load_weight(name)
            sp.wait_ge(*evacuated("f1", 3))
            load_row(4)
            load_row(5)
            for k in range(3):
                c0 = GE * k
                for r0, n, at in ((0, 2, 0), (44, 3, 2)):
                    sp.dma_start(W1s[at:at + n, c0:c0 + GE], a["nw1"][k, r0:r0 + n, :]).then_inc(nib_loaded, 16)
                sp.dma_start(W1s[5:6, c0:c0 + GE], a["nb1"][k:k + 1, :]).then_inc(nib_loaded, 16)
                sp.dma_start(w2bc[:, c0:c0 + GE], a["nw2"][k:k + 1, :].broadcast_to([P, GE])).then_inc(nib_loaded, 16)
            sp.dma_start(b2bc, a["nb2"].broadcast_to([P, 3])).then_inc(nib_loaded, 16)
            sp.wait_ge(stored, 16)

        @block.gpsimd
        def _(pool):
            links = [0]

            def link(ins):
                links[0] += 1
                ins.then_inc(pool_link, 1)
                pool.wait_ge(pool_link, links[0])

            link(nc.gpsimd.memset(ident[:], 0.0))
            nc.gpsimd.affine_select(out=ident[:], in_=ident[:], compare_op=ALU.not_equal, fill=1.0, base=0,
                                    pattern=[[-1, P]], channel_multiplier=1).then_inc(const_made, 1)
            nc.gpsimd.iota(iota, [[1, N]], base=0, channel_multiplier=0,
                           allow_small_or_imprecise_dtypes=True).then_inc(const_made, 1)
            nc.gpsimd.iota(lo8, [[P, TT], [0, P]], base=0, channel_multiplier=0,
                           allow_small_or_imprecise_dtypes=True).then_inc(const_made, 1)
            nc.gpsimd.iota(c8, [[0, TT], [1, P]], base=0, channel_multiplier=0,
                           allow_small_or_imprecise_dtypes=True).then_inc(const_made, 1)
            nc.gpsimd.memset(zeros, 0.0).then_inc(const_made, 1)
            nc.gpsimd.memset(ones[:], 1.0).then_inc(const_made, 1)
            link(nc.gpsimd.memset(sel[:], 0.0))
            nc.gpsimd.affine_select(out=sel[:].rearrange("k i (e m) -> k i e m", e=2),
                                    in_=sel[:].rearrange("k i (e m) -> k i e m", e=2),
                                    compare_op=ALU.not_equal, fill=1.0, base=0,
                                    pattern=[[-1, 4], [-4, 2], [0, DH]], channel_multiplier=1).then_inc(const_made, 1)
            pool.wait_ge(rows_normed, 1)
            row_ready(pool, "L0_gnn_bv")
            row_ready(pool, "L0_mix_b_out")
            for t in range(TT):
                link(nc.gpsimd.tensor_tensor(X[:, t, :], X[:, t, :], row("L0_gnn_bv"), ALU.add))
                nc.gpsimd.tensor_tensor(X[:, t, :], X[:, t, :], row("L0_mix_b_out"), ALU.add).then_inc(x_biased, 1)
            for t in range(TT):
                pool.wait_ge(psum_full, INDEX[("adjT", 7)] + 1)
                if t >= 2:
                    link(nc.gpsimd.tensor_tensor(MASK[:, t - 2, :], MASK[:, t - 2, :], KR[:, t % 2, :], ALU.add))
                nc.gpsimd.tensor_scalar(KR[:, t % 2, :], MASK[:, t, :], 1.0, None, ALU.max).then_inc(counts_floored, 1)
                nc.gpsimd.tensor_scalar(MASK[:, t, :], MASK[:, t, :], 0.5, NO_EDGE, ALU.is_lt, ALU.mult).then_inc(mask_made, 1)
                pool.wait_ge(mask_made, t + 1)
                pool.wait_ge(logs_taken, t + 1)
            for t in range(TT - 2, TT):
                last = nc.gpsimd.tensor_tensor(MASK[:, t, :], MASK[:, t, :], KR[:, t % 2, :], ALU.add)
                last.then_inc(mask_made, 1)
            for i in range(TT):
                done(pool, "adjT", 6)
                done(pool, "adjT", 7)
                if i >= 2:
                    pool.wait_ge(masked0, i - 1)
                nc.gpsimd.tensor_scalar(negm[:, i % 2, :], adj0[:, i, :], -NEG, NEG, ALU.mult, ALU.add).then_inc(negm_made, 1)
            pool.wait_ge(psum_full, INDEX[("score0", TT - 1)] + 1)
            nc.gpsimd.memset(bdqk, 0.0)
            link(nc.gpsimd.memset(bdv, 0.0))
            link(nc.gpsimd.memset(hm, 1.0))
            hm4 = hm.rearrange("p c (h r) -> p c h r", r=R)
            link(nc.gpsimd.affine_select(out=hm4, in_=hm4, compare_op=ALU.is_ge, fill=0.0, base=0,
                                         pattern=[[P, FC], [-DH, H], [0, R]], channel_multiplier=1))
            nc.gpsimd.affine_select(out=hm4, in_=hm4, compare_op=ALU.is_ge, fill=0.0, base=DH - 1,
                                    pattern=[[-P, FC], [DH, H], [0, R]], channel_multiplier=-1).then_inc(bd_cleared, 1)
            pool.wait_ge(rows_normed, 3)
            link(nc.gpsimd.memset(blk, 0.0))
            link(nc.gpsimd.memset(blk[0:DH, 0:DH], 1.0))
            nc.gpsimd.memset(blk[DH:P, DH:P], 1.0).then_inc(blk_made, 1)
            pool.wait_ge(blk_made, 1)
            row_ready(pool, "L1_mix_bout")
            for t in range(TT):
                nc.gpsimd.tensor_tensor(X[:, t, :], X[:, t, :], row("L1_mix_bout"), ALU.add).then_inc(x1_biased, 1)
            pool.wait_ge(x1_biased, TT)
            pool.wait_ge(psum_full, INDEX[("mixout1", 3)] + 1)
            for b in range(2):
                link(nc.gpsimd.memset(QZ[DH:P, b, 0, :], 0.0))
                nc.gpsimd.memset(QZ[0:DH, b, 1, :], 0.0).then_inc(q_cleared, 1)
                pool.wait_ge(q_cleared, b + 1)
            pool.wait_ge(*evacuated("f1", 3))
            nc.gpsimd.iota(i16, [[1, 16]], base=0, channel_multiplier=0,
                           allow_small_or_imprecise_dtypes=True).then_inc(i16_made, 1)
            nc.gpsimd.iota(i16m, [[1, 16]], base=-16, channel_multiplier=0,
                           allow_small_or_imprecise_dtypes=True).then_inc(i16_made, 1)
            nc.gpsimd.memset(Fx, 1.0).then_inc(i16_made, 1)

        @block.scalar
        def _(act):
            def copy_out(dst, name, i, view=None):
                src = full(act, name, i)
                src = src if view is None else view(src)
                nc.scalar.activation(dst, src, ACT.Copy).then_inc(act_evacuated, 1)

            def take_std(n):
                act.wait_ge(var_ready, n)
                nc.scalar.activation(rstd[:], rstd[:], ACT.Sqrt).then_inc(std_ready, 1)

            def xT(n):
                for c in (1, 3):
                    copy_out(XT[:, c, :], f"xT{n}", c)

            take_std(1)
            xT(0)
            for t in range(TT):
                copy_out(MASK[:, t, :], "counts", t)
            for t in range(1, TT, 2):
                src = full(act, "adjT", t)
                nc.scalar.activation(adj0[:, t, :], src, ACT.Sign).then_inc(act_evacuated, 1)
            for name, dst in (("q0", QT0), ("k0", KT0)):
                if name == "q0":
                    act.wait_ge(cols_loaded, 16)
                for c in (1, 3):
                    src = full(act, name, c)
                    nc.scalar.activation(dst[:, c, :], src, ACT.Identity, bias=col("bq" if name == "q0" else "bk", c),
                                         scale=1.0).then_inc(act_evacuated, 1)
            for j in (1, 3):
                copy_out(V0[:, 2 * j:2 * j + 2, :], "v0", j, lambda s: s.rearrange("p (t d) -> p t d", t=2))
            for t in range(TT):
                act.wait_ge(counts_floored, t + 1)
                nc.scalar.activation(KR[:, t % 2, :], KR[:, t % 2, :], ACT.Ln).then_inc(logs_taken, 1)
            for n in range(TT + LAG + 1):
                if n >= 1 and n - 1 < TT:
                    i = n - 1
                    act.wait_ge(masked0, i + 1)
                    nc.scalar.activation(SM[:, i % 2, :], SM[:, i % 2, :], ACT.Exp, bias=nm[:, i:i + 1], scale=-1.0,
                                         accum_out=ls[:, 0, i:i + 1]).then_inc(probs0, 1)
                i = n - LAG
                if 0 <= i < TT:
                    if i >= 2:
                        act.wait_ge(psum_full, INDEX[("attn0", i - 2)] + 1)
                    copy_out(P0T[:, i % 2, :, :], "turn0", i, lambda s: s.rearrange("p (s n) -> p s n", s=TT))
            act.wait_ge(mix_kexp, 1)
            nc.scalar.activation(ekT, ekT, ACT.Exp, bias=kmax, scale=1.0, accum_out=ksum).then_inc(mix_krdy, 1)
            act.wait_ge(mix_qs, 1)
            nc.scalar.activation(ql, ql, ACT.Exp).then_inc(mix_qe, 1)
            act.wait_ge(wmean, 1)
            wf = wtile("ffn")
            nc.scalar.activation(wf, wf, ACT.Sign, bias=tiny[:, 2:3], scale=1.0).then_inc(wsign, 1)
            take_std(2)
            xT(1)
            take_std(3)
            xT(2)
            for j in range(4):
                act.wait_ge(kneg, j + 1)
                nc.scalar.activation(SM[:, j % 2, :], SM[:, j % 2, :], ACT.Exp).then_inc(kexp, 1)
            for j in range(4):
                copy_out(V1[:, 2 * j:2 * j + 2, :], "v1", j, lambda s: s.rearrange("p (t d) -> p t d", t=2))
            for j in range(4):
                act.wait_ge(kneg, j + 5)
                nc.scalar.activation(SM[:, j % 2, :], SM[:, j % 2, :], ACT.Exp).then_inc(kexp, 1)
            copy_out(M1[:, 2:4, :], "mixM1", 1, lambda s: s.rearrange("p (t d) -> p t d", t=2))

            for l in range(L):
                if l == 0:
                    act.wait_ge(psum_full, INDEX[("xT2", 3)] + 1)
                for j in (1, 3):
                    copy_out(GV[:, 2 * j:2 * j + 2, :], f"gv{l}", j, lambda s: s.rearrange("p (t d) -> p t d", t=2))

                def exp_unit(n):
                    act.wait_ge(*evacuated(f"score{l}g", n))
                    if n % 8 == 0 and n >= 16:
                        act.wait_ge(recips, 8 * l + n // 8 - 1)
                    nc.scalar.activation(SM[:, n % 2, :], SM[:, n % 2, :], ACT.Exp, bias=nm[:, n % 8:n % 8 + 1], scale=-1.0,
                                         accum_out=ls[:, n // 8 % 2, n % 8:n % 8 + 1]).then_inc(probs, 1)

                for step, n in attention_order():
                    if step == "k":
                        if n >= 2:
                            act.wait_ge(psum_full, INDEX[(f"score{l}g", 16 * n - 17)] + 1)
                        copy_out(KR[:, n % 2, :], f"k{l}g", n)
                    elif step == "score" and n >= 1:
                        exp_unit(n - 1)
                    elif step == "turn":
                        if n == UNITS - 2:
                            exp_unit(UNITS - 1)
                        if n % 2 == 1:
                            g, i = n // 4, n % 4
                            if g >= 3:
                                act.wait_ge(psum_full, INDEX[(f"agg{l}g", (g - 3) // 2)] + 1)
                            elif l == 0:
                                act.wait_ge(psum_full, INDEX[("mixout1", 3)] + 1)
                            else:
                                act.wait_ge(psum_full, INDEX[("agg0g", 7)] + 1)
                            copy_out(PTr[:, g % 3, :, i * P:(i + 1) * P], f"turn{l}g", n,
                                     lambda s: s.rearrange("p (s n) -> p s n", s=TT))
                    elif step == "rsum_bc":
                        if n >= 1:
                            done(act, f"agg{l}g", n - 1)
                        src = full(act, f"rsum_bc{l}g", n)
                        nc.scalar.activation(rbc, src[:, 0:D], ACT.Copy).then_inc(act_evacuated, 1)
                take_std(4 + 2 * l)
                for c in range(2):
                    src = full(act, f"h{l}", c)
                    nc.scalar.activation(KR[:, c, :], src, ACT.Relu, bias=col(f"gb1{l}", c), scale=1.0).then_inc(act_evacuated, 1)
                take_std(5 + 2 * l)
            for j in (1, 3):
                copy_out(G[:, 2 * j:2 * j + 2, :], "gT", j, lambda s: s.rearrange("p (t d) -> p t d", t=2))
            take_std(4 + 2 * L)
            take_std(5 + 2 * L)
            act.wait_ge(rows_normed, 5)
            act.dma_start(out.rearrange("(t p) d -> p t d", p=P), X[:]).then_inc(stored, 16)
            act.wait_ge(stored, 16)

        @block.vector
        def _(dve):
            links = [0]

            def link(ins):
                links[0] += 1
                ins.then_inc(dve_link, 1)
                dve.wait_ge(dve_link, links[0])

            rounds = [0]

            def std(n_cols):
                rounds[0] += 1
                nc.vector.tensor_scalar(rstd[:, 0:n_cols], mv[:, 0:n_cols, 1], EPS, None, ALU.add).then_inc(var_ready, 1)
                dve.wait_ge(std_ready, rounds[0])
                link(nc.vector.reciprocal(rstd[:, 0:n_cols], rstd[:, 0:n_cols]))

            def layernorm(dst, src, last_sem):
                for t in range(TT):
                    last = nc.vector.bn_stats(st[:, t, :], src[:, t, :])
                link(last)
                for t in range(TT):
                    last = nc.vector.bn_aggr(mv[:, t, :], st[:, t, :])
                link(last)
                std(TT)
                for t in range(TT):
                    last = nc.vector.tensor_scalar(dst[:, t, :], src[:, t, :], mv[:, t, 0:1], rstd[:, t:t + 1],
                                                   ALU.subtract, ALU.mult)
                if last_sem is None:
                    link(last)
                else:
                    last.then_inc(last_sem, 1)

            def copy_out(dst, name, i, view=None):
                src = full(dve, name, i)
                src = src if view is None else view(src)
                nc.vector.tensor_copy(dst, src).then_inc(dve_evacuated, 1)

            two = lambda s: s.rearrange("p (t d) -> p t d", t=2)

            def xT(n):
                for c in (0, 2):
                    copy_out(XT[:, c, :], f"xT{n}", c)

            dve.wait_ge(idx_loaded, 16)
            nc.vector.tensor_copy(dst_f, idx_i[:, 0:P])
            nc.vector.tensor_copy(src_f, idx_i[:, P:2 * P])
            link(nc.vector.tensor_copy(drow_f, idx_i[:, 2 * P:3 * P]))
            nc.vector.tensor_reduce(cmin, drow_f, AX.X, ALU.min)
            nc.vector.tensor_reduce(cmax, drow_f, AX.X, ALU.max).then_inc(mm_bounds, 1)
            dve.wait_ge(x_loaded, 16)
            layernorm(XN, X, rows_normed)
            src = full(dve, "bounds", 0)
            nc.vector.tensor_copy(brow, src[0:1, 0:2 * P]).then_inc(dve_evacuated, 1)
            dve.wait_ge(*evacuated("bounds", 0))
            dve.wait_ge(const_made, 5)
            lows = brow[:, 0:P].unsqueeze(1).broadcast_to([1, TT, P])
            highs = brow[:, P:2 * P].unsqueeze(1).broadcast_to([1, TT, P])
            nc.vector.tensor_tensor(relA, lows, lo8, ALU.subtract)
            link(nc.vector.tensor_tensor(relB, highs, lo8, ALU.subtract))
            link(nc.vector.tensor_scalar(relB, relB, 0.0, None, ALU.is_ge))
            link(nc.vector.scalar_tensor_tensor(relA, relA, float(P - 1), relB, ALU.is_le, ALU.mult))
            nc.vector.scalar_tensor_tensor(relB, c8, float(P - 1), relA, ALU.subtract, ALU.mult)
            link(nc.vector.tensor_tensor(relA, c8, relA, ALU.mult))
            nc.vector.tensor_reduce(bnd[:, 0:8], relB, AX.X, ALU.min)
            link(nc.vector.tensor_reduce(bnd[:, 8:16], relA, AX.X, ALU.max))
            link(nc.vector.tensor_scalar(bnd[:, 0:8], bnd[:, 0:8], float(P - 1), None, ALU.add))
            link(nc.vector.tensor_tensor(bnd[:, 8:16], bnd[:, 8:16], bnd[:, 0:8], ALU.max))
            link(nc.vector.tensor_scalar(bnd[:, 8:16], bnd[:, 8:16], 1.0, None, ALU.add))
            link(nc.vector.tensor_tensor(bnd[:, 16:24], bnd[:, 8:16], bnd[:, 0:8], ALU.subtract))
            link(nc.vector.memset(bnd[:, 24:25], float(SHIFT)))
            for t in range(1, TT):
                link(nc.vector.tensor_tensor(bnd[:, 24 + t:25 + t], bnd[:, 23 + t:24 + t], bnd[:, 15 + t:16 + t], ALU.add))
            link(nc.vector.tensor_tensor(bnd[:, 24:32], bnd[:, 24:32], bnd[:, 0:8], ALU.subtract))
            nc.vector.tensor_copy(bnd_i, bnd).then_inc(bounds_made, 1)
            xT(0)
            dve.wait_ge(bounds_made, 1)
            dve.sem_inc(onehot_ready, SHIFT)
            for t in range(TT):
                first = dve.value_load(bnd_i[0:1, t:t + 1], min_val=0, max_val=EC - 1)
                end = dve.value_load(bnd_i[0:1, 8 + t:9 + t], min_val=0, max_val=EC)
                before = dve.value_load(bnd_i[0:1, 24 + t:25 + t], min_val=0, max_val=SHIFT + TT * EC)
                with dve.Fori(first, end) as c:
                    b = (c + before) % RING
                    dve.wait_ge(onehot_used, c + before + 1)
                    nc.vector.tensor_scalar(dstrow[:, b, :], iota[:, t * P:(t + 1) * P], dst_f[:, bass.ds(c, 1)], None,
                                            ALU.is_equal)
                    nc.vector.tensor_scalar(srcrow[:, b, :], iota, src_f[:, bass.ds(c, 1)], None,
                                            ALU.is_equal).then_inc(onehot_ready, 1)
            for t in range(0, TT, 2):
                src = full(dve, "adjT", t)
                nc.vector.tensor_scalar(adj0[:, t, :], src, 1.0, None, ALU.min).then_inc(dve_evacuated, 1)
            dve.wait_ge(cols_loaded, 16)
            for name, dst in (("q0", QT0), ("k0", KT0)):
                for c in (0, 2):
                    src = full(dve, name, c)
                    nc.vector.tensor_scalar(dst[:, c, :], src, col("bq" if name == "q0" else "bk", c), None,
                                            ALU.add).then_inc(dve_evacuated, 1)
            for j in (0, 2):
                copy_out(V0[:, 2 * j:2 * j + 2, :], "v0", j, two)
            for n in range(TT + LAG + 1):
                if n < TT:
                    src = full(dve, "score0", n)
                    if n >= 2:
                        dve.wait_ge(psum_full, INDEX[("turn0", n - 2)] + 1)
                    else:
                        dve.wait_ge(*evacuated("adjT", 7))
                    nc.vector.scalar_tensor_tensor(SM[:, n % 2, :], src, float(D) ** -0.5, adj0[:, n, :],
                                                   ALU.mult, ALU.mult).then_inc(dve_evacuated, 1)
                    dve.wait_ge(*evacuated("score0", n))
                    dve.wait_ge(negm_made, n + 1)
                    nc.vector.tensor_tensor_reduce(out=SM[:, n % 2, :], in0=SM[:, n % 2, :], in1=negm[:, n % 2, :],
                                                   scale=-1.0, scalar=3e38, op0=ALU.add, op1=ALU.min,
                                                   accum_out=nm[:, n:n + 1]).then_inc(masked0, 1)
                i = n - LAG - 1
                if i >= 0:
                    dve.wait_ge(probs0, i + 1)
                    link(nc.vector.reciprocal(rl[:, i:i + 1], ls[:, 0, i:i + 1]))
                    dve.wait_ge(x_biased, TT)
                    src = full(dve, "attn0", i)
                    nc.vector.scalar_tensor_tensor(X[:, i, :], src[:, 0:D], rl[:, i:i + 1], X[:, i, :],
                                                   ALU.mult, ALU.add).then_inc(dve_evacuated, 1)
            dve.wait_ge(bd_cleared, 1)
            nc.vector.tensor_copy(b_bc, col("b_in").unsqueeze(2).broadcast_to([P, FC, P])).then_inc(mix_bias, 1)
            quarter = lambda s: s[:, 0:256].rearrange("p (c n) -> p c n", c=FC)
            copy_out(wqk, "wqk", 0, quarter)
            copy_out(bq_bc, "bq0", 0, lambda s: s[:, 0:32])
            copy_out(bk_col, "bk0", 0, lambda s: s[0:32, 0:1])
            src = full(dve, "klog", 0)
            dve.wait_ge(*evacuated("bk0", 0))
            dve.wait_ge(mask_made, TT + 2)
            nc.vector.tensor_scalar(ekT, src[0:32, :], bk_col, None, ALU.add).then_inc(dve_evacuated, 1)
            dve.wait_ge(*evacuated("klog", 0))
            nc.vector.tensor_reduce(kmax, ekT, AX.X, ALU.max, negate=True).then_inc(mix_kexp, 1)
            src = full(dve, "qlog", 0)
            nc.vector.tensor_tensor(ql, src[:, 0:256].rearrange("p (t n) -> p t n", t=TT),
                                    bq_bc.unsqueeze(1).broadcast_to([P, TT, 32]), ALU.add).then_inc(dve_evacuated, 1)
            dve.wait_ge(*evacuated("qlog", 0))
            qlf = ql.rearrange("p t (h r) -> p (t h) r", r=R)
            link(nc.vector.tensor_reduce(qm, qlf, AX.X, ALU.max))
            nc.vector.tensor_tensor(qlf, qlf, qm.unsqueeze(2).broadcast_to([P, TT * H, R]), ALU.subtract).then_inc(mix_qs, 1)
            dve.wait_ge(mix_qe, 1)
            link(nc.vector.tensor_reduce(qr, qlf, AX.X, ALU.add))
            link(nc.vector.reciprocal(qr, qr))
            nc.vector.tensor_tensor(qlf, qlf, qr.unsqueeze(2).broadcast_to([P, TT * H, R]), ALU.mult).then_inc(mix_kscaled, 1)
            dve.wait_ge(mix_krdy, 1)
            link(nc.vector.reciprocal(krec, ksum))
            copy_out(ek, "ekt", 0, lambda s: s[:, 0:256].rearrange("p (t n) -> p t n", t=TT))
            src = full(dve, "kx", 0)
            nc.vector.tensor_scalar(kx, src[0:32, 0:D], krec, None, ALU.mult).then_inc(dve_evacuated, 1)
            four32 = lambda s: s[:, 0:128].rearrange("p (c n) -> p c n", c=FC)
            copy_out(kxT, "kxT", 0, four32)
            src = four32(full(dve, "xmT", 0))
            link(nc.vector.tensor_tensor(xmT, src, col("b_in").unsqueeze(2).broadcast_to([P, FC, 32]), ALU.add))
            nc.vector.tensor_tensor(xmT, xmT, hm, ALU.mult).then_inc(dve_evacuated, 1)
            copy_out(kvT, "kvT", 0, four32)
            copy_out(mixM, "mixM", 0, lambda s: s[0:32, 0:D])
            copy_out(qsT, "qsT", 0, lambda s: s[0:32, :])
            for j in range(4):
                src = two(full(dve, "mixout", j))
                nc.vector.tensor_tensor(X[:, 2 * j:2 * j + 2, :], src, X[:, 2 * j:2 * j + 2, :], ALU.add).then_inc(dve_evacuated, 1)
            dve.wait_ge(*evacuated("mixout", 3))
            w_ready(dve, "ffn")
            wfl = W[:, WEIGHTS.index("ffn") % WSLOTS, :]
            nc.vector.tensor_reduce(tiny[:, 0:1], wfl, AX.X, ALU.add)
            nc.vector.tensor_reduce(tiny[:, 1:2], wfl, AX.X, ALU.add, apply_absolute_value=True).then_inc(wstat, 1)
            src = full(dve, "wsum", 0)
            nc.vector.tensor_scalar(tiny[:, 2:3], src[:, 0:1], -1.0 / (D * D), None, ALU.mult).then_inc(wmean, 1)
            nc.vector.tensor_scalar(tiny[:, 3:4], src[:, 1:2], 1.0 / (D * D), None, ALU.mult).then_inc(dve_evacuated, 1)
            dve.wait_ge(psum_full, INDEX[("kx", 0)] + 1)
            layernorm(XN, X, rows_normed)
            xT(1)
            row_ready(dve, "L0_ffn_bias")
            fb = row("L0_ffn_bias").unsqueeze(1).broadcast_to([P, 2, D])
            dve.wait_ge(psum_full, INDEX[("turn0", 7)] + 1)
            for j in range(4):
                y = two(SM[:, j % 2, :])
                xs = X[:, 2 * j:2 * j + 2, :]
                src = two(full(dve, "ffn", j))
                dve.wait_ge(*evacuated("wsum", 0))
                nc.vector.scalar_tensor_tensor(y, src, tiny[:, 3:4], fb, ALU.mult, ALU.add).then_inc(dve_evacuated, 1)
                dve.wait_ge(*evacuated("ffn", j))
                link(nc.vector.tensor_scalar(y, y, -1.0, 1.0, ALU.max, ALU.min))
                link(nc.vector.tensor_scalar(y, y, 7.0, MAGIC, ALU.mult, ALU.add))
                link(nc.vector.tensor_scalar(y, y, MAGIC, 1.0 / 7.0, ALU.subtract, ALU.mult))
                link(nc.vector.tensor_tensor(xs, xs, y, ALU.add))
            dve.wait_ge(psum_full, INDEX[("xT1", 3)] + 1)
            layernorm(XN, X, rows_normed)
            xT(2)

            def elu1(dst, name, j, n):
                src = full(dve, name, j)
                nc.vector.tensor_scalar(SM[:, n % 2, :], src, 0.0, None, ALU.min).then_inc(kneg, 1)
                dve.wait_ge(kexp, n + 1)
                nc.vector.scalar_tensor_tensor(dst, src, 0.0, SM[:, n % 2, :], ALU.max, ALU.add).then_inc(dve_evacuated, 1)

            for j in range(4):
                elu1(K1[:, 2 * j:2 * j + 2, :].rearrange("p t d -> p (t d)"), "k1", j, j)
            dve.wait_ge(blk_made, 1)
            src = full(dve, "kv1", 0)
            blk4 = blk.unsqueeze(1).broadcast_to([P, FC, P])
            nc.vector.tensor_tensor(kvT1, src[:, 0:D].rearrange("p (c n) -> p c n", c=FC), blk4, ALU.mult)
            nc.vector.tensor_tensor(KS1, src[:, D:2 * D].rearrange("p (c n) -> p c n", c=FC), blk4, ALU.mult).then_inc(dve_evacuated, 1)
            for j in range(4):
                elu1(QT1[:, j, :], "q1", j, 4 + j)
            copy_out(M1[:, 0:2, :], "mixM1", 0, two)
            for j in range(4):
                src = full(dve, "den", j)
                link(nc.vector.tensor_scalar(Z1[:, j, :], src, 1e-6, None, ALU.add))
                link(nc.vector.reciprocal(Z1[:, j, :], Z1[:, j, :]))
                nc.vector.tensor_tensor(QT1[:, j, :], QT1[:, j, :], Z1[:, j, :], ALU.mult).then_inc(dve_evacuated, 1)
            dve.wait_ge(x1_biased, TT)
            for j in range(4):
                src = two(full(dve, "mixout1", j))
                nc.vector.tensor_tensor(X[:, 2 * j:2 * j + 2, :], src, X[:, 2 * j:2 * j + 2, :], ALU.add).then_inc(dve_evacuated, 1)

            def batchnorm(g, be):
                for c in range(FC):
                    nc.vector.bn_stats(st[:, 2 * c, :], XT[:, c, 0:D])
                    last = nc.vector.bn_stats(st[:, 2 * c + 1, :], XT[:, c, D:N])
                link(last)
                for c in range(FC):
                    last = nc.vector.bn_aggr(mv[:, c, :], st[:, 2 * c:2 * c + 2, :])
                link(last)
                std(FC)
                link(nc.vector.tensor_tensor(tiny[:, 4:8], rstd[:, 0:FC], col(g), ALU.mult))
                link(nc.vector.tensor_tensor(tiny[:, 8:12], mv[:, 0:FC, 0], tiny[:, 4:8], ALU.mult))
                link(nc.vector.tensor_tensor(tiny[:, 8:12], col(be), tiny[:, 8:12], ALU.subtract))
                for c in range(FC):
                    last = nc.vector.tensor_scalar(XT[:, c, :], XT[:, c, :], tiny[:, 4 + c:5 + c], tiny[:, 8 + c:9 + c],
                                                   ALU.mult, ALU.add)
                last.then_inc(state_ready, 1)

            for l in range(L):
                if l == 0:
                    dve.wait_ge(psum_full, INDEX[("xT2", 3)] + 1)
                for j in (0, 2):
                    copy_out(GV[:, 2 * j:2 * j + 2, :], f"gv{l}", j, two)
                dve.wait_ge(q_cleared, 2)
                for step, n in attention_order():
                    if step == "q":
                        if n >= 2:
                            dve.wait_ge(psum_full, INDEX[(f"score{l}g", 16 * n - 17)] + 1)
                        src = full(dve, f"q{l}g", n)
                        nc.vector.tensor_scalar(QZ[0:DH, n % 2, 0, :], src[0:DH, :], col(f"gbq{l}", n)[0:DH], DH ** -0.5,
                                                ALU.add, ALU.mult)
                        nc.vector.tensor_scalar(QZ[DH:P, n % 2, 1, :], src[DH:P, :], col(f"gbq{l}", n)[DH:P], DH ** -0.5,
                                                ALU.add, ALU.mult).then_inc(dve_evacuated, 1)
                    elif step == "score":
                        src = full(dve, f"score{l}g", n)
                        if n >= 2:
                            dve.wait_ge(psum_full, INDEX[(f"turn{l}g", n - 2)] + 1)
                        nc.vector.tensor_tensor_reduce(out=SM[:, n % 2, :], in0=src, in1=MASK[:, n % 4 + 4 * (n // 8 % 2), :],
                                                       scale=-1.0, scalar=-0.1 * NO_EDGE, op0=ALU.add, op1=ALU.min,
                                                       accum_out=nm[:, n % 8:n % 8 + 1]).then_inc(dve_evacuated, 1)
                    elif step == "turn":
                        if n % 2 == 0:
                            g, i = n // 4, n % 4
                            if g >= 3:
                                dve.wait_ge(psum_full, INDEX[(f"agg{l}g", (g - 3) // 2)] + 1)
                            copy_out(PTr[:, g % 3, :, i * P:(i + 1) * P], f"turn{l}g", n,
                                     lambda s: s.rearrange("p (s n) -> p s n", s=TT))
                        if n % 8 == 7:
                            b = n // 8
                            dve.wait_ge(probs, UNITS * l + n + 1)
                            if b >= 1:
                                dve.wait_ge(psum_full, INDEX[(f"rsum{l}g", b - 1)] + 1)
                            link(nc.vector.tensor_scalar(rl[:], ls[:, b % 2, :], 1e-16, None, ALU.add))
                            nc.vector.reciprocal(rl[:], rl[:]).then_inc(recips, 1)
                    elif step == "rsum":
                        src = full(dve, f"rsum{l}g", n)
                        if n >= 1:
                            dve.wait_ge(psum_full, INDEX[(f"rsum_bc{l}g", n - 1)] + 1)
                        nc.vector.tensor_copy(rT, src[0:8, 0:P]).then_inc(dve_evacuated, 1)
                    elif step == "agg":
                        src = full(dve, f"agg{l}g", n)
                        done(dve, f"rsum_bc{l}g", n)
                        nc.vector.tensor_tensor(AG[:, n // 2, (n % 2) * D:(n % 2 + 1) * D], src[:, 0:D], rbc,
                                                ALU.mult).then_inc(dve_evacuated, 1)
                for c in range(FC):
                    src = full(dve, f"wo{l}", c)
                    nc.vector.scalar_tensor_tensor(XT[:, c, :], src, col(f"gbo{l}", c), XT[:, c, :],
                                                   ALU.add, ALU.add).then_inc(dve_evacuated, 1)
                dve.wait_ge(*evacuated(f"wo{l}", 3))
                batchnorm(f"g1{l}", f"be1{l}")
                for c in range(FC):
                    src = full(dve, f"f{l}", c)
                    nc.vector.scalar_tensor_tensor(XT[:, c, :], src, col(f"gb2{l}", c), XT[:, c, :],
                                                   ALU.add, ALU.add).then_inc(dve_evacuated, 1)
                dve.wait_ge(*evacuated(f"f{l}", 3))
                batchnorm(f"g2{l}", f"be2{l}")

            for j in (0, 2):
                copy_out(G[:, 2 * j:2 * j + 2, :], "gT", j, two)
            dve.wait_ge(*evacuated("gT", 2))
            dve.wait_ge(*evacuated("gT", 3))
            layernorm(G, G, None)
            row_ready(dve, "L1_gnn_ln_g")
            row_ready(dve, "L1_gnn_ln_b")
            lg = row("L1_gnn_ln_g").unsqueeze(1).broadcast_to([P, TT, D])
            lb = row("L1_gnn_ln_b").unsqueeze(1).broadcast_to([P, TT, D])
            link(nc.vector.tensor_tensor(G, G, lg, ALU.mult))
            link(nc.vector.tensor_tensor(X[:], X[:], G, ALU.add))
            link(nc.vector.tensor_tensor(X[:], X[:], lb, ALU.add))
            layernorm(XN, X, rows_normed)
            dve.wait_ge(rows_normed, 4)
            dve.wait_ge(i16_made, 3)
            nc.vector.tensor_scalar(flags[:, :, 0:1], XN[:, :, 0:1], 0.5, None, ALU.is_ge)
            nc.vector.tensor_scalar(flags[:, :, 1:4], XN[:, :, 1:4], 0.5, None, ALU.is_gt)
            link(nc.vector.tensor_scalar(bits, XN[:, :, 16:80].rearrange("p t (j n) -> p t j n", j=4), 0.5, None, ALU.is_gt))
            bf = bits.rearrange("p t j n -> p (t j) n")
            link(nc.vector.tensor_tensor(bf, bf, i16m.unsqueeze(1).broadcast_to([P, TT * 4, 16]), ALU.mult))
            mf = m16.rearrange("p t j -> p (t j)")
            link(nc.vector.tensor_reduce(mf, bf, AX.X, ALU.min))
            b0 = bits[:, :, 0, 0:4]
            link(nc.vector.tensor_scalar(b0, m16, 0.0, None, ALU.is_lt))
            nc.vector.scalar_tensor_tensor(Fx[:, :, :, 0], m16[:, :, 0:2], 16.0, b0[:, :, 0:2], ALU.add, ALU.mult)
            nc.vector.scalar_tensor_tensor(Fx[:, :, :, 1], m16[:, :, 2:4], 16.0, b0[:, :, 2:4], ALU.add, ALU.mult)
            for r in range(2):
                nc.vector.tensor_copy(Fx[:, :, r, 2:4], XN[:, :, 2:4])
                last = nc.vector.tensor_copy(Fx[:, :, r, 4:5], XN[:, :, 1:2])
            last.then_inc(hid_ready, 1)
            for q in range(4):
                src = full(dve, "fT", q)
                nc.vector.tensor_copy(FT[:, q * D:(q + 1) * D], src[0:6, 0:D]).then_inc(dve_evacuated, 1)
            dve.wait_ge(nib_loaded, 16 * 13)
            for n in range(16):
                t, r = n // 2, n % 2
                src = full(dve, "hid", n)
                nc.vector.scalar_tensor_tensor(hidb[n % 2], src[:, 0:3 * GE], 0.0, w2bc, ALU.max, ALU.mult).then_inc(dve_evacuated, 1)
                dve.wait_ge(*evacuated("hid", n))
                last = nc.vector.tensor_reduce(yk[:, t, r, :], hidb[n % 2].rearrange("p (k e) -> p k e", k=3), AX.X, ALU.add)
            link(last)
            ykf = yk.rearrange("p t r k -> p (t r) k")
            link(nc.vector.tensor_tensor(ykf, ykf, b2bc.unsqueeze(1).broadcast_to([P, 2 * TT, 3]), ALU.add))
            nc.vector.tensor_copy(pick[:, :, 0:1], flags[:, :, 1:2])
            nc.vector.scalar_tensor_tensor(pick[:, :, 1:2], flags[:, :, 1:2], 0.5, flags[:, :, 2:3], ALU.is_lt, ALU.mult)
            link(nc.vector.tensor_tensor(pick[:, :, 2:3], flags[:, :, 1:2], flags[:, :, 2:3], ALU.max))
            nc.vector.tensor_tensor(act_on.unsqueeze(2), pick[:, :, 2:3], flags[:, :, 3:4], ALU.max)
            link(nc.vector.tensor_scalar(pick[:, :, 2:3], pick[:, :, 2:3], 0.5, None, ALU.is_lt))
            link(nc.vector.tensor_tensor(act_on.unsqueeze(2), act_on.unsqueeze(2), flags[:, :, 0:1], ALU.mult))
            for r in range(2):
                last = nc.vector.tensor_tensor(ysel[:, :, r, :], yk[:, :, r, :], pick, ALU.mult)
            link(last)
            resf = res.rearrange("p t r -> p (t r)")
            link(nc.vector.tensor_reduce(resf, ysel.rearrange("p t r k -> p (t r) k"), AX.X, ALU.add))
            link(nc.vector.tensor_scalar(resf, resf, 0.0, 15.0, ALU.max, ALU.min))
            link(nc.vector.tensor_scalar(resf, resf, MAGIC, MAGIC, ALU.add, ALU.subtract))
            onef = oneh.rearrange("p t r n -> p (t r) n")
            link(nc.vector.tensor_tensor(onef, resf.unsqueeze(2).broadcast_to([P, 2 * TT, 16]),
                                         i16.unsqueeze(1).broadcast_to([P, 2 * TT, 16]), ALU.is_equal))
            onet = oneh.rearrange("p t r n -> p t (r n)")
            link(nc.vector.scalar_tensor_tensor(onet, onet, 2.0, act_on.unsqueeze(2).broadcast_to([P, TT, 32]),
                                                ALU.mult, ALU.mult))
            link(nc.vector.tensor_tensor(XN[:, :, 80:112], XN[:, :, 80:112], onet, ALU.add))
            nc.vector.tensor_tensor(X[:], X[:], XN[:], ALU.add).then_inc(rows_normed, 1)

        @block.tensor
        def _(pe):
            waited = {}

            def wait(s, v):
                if waited.get(id(s), 0) < v:
                    pe.wait_ge(s, v)
                    waited[id(s)] = v

            def begin(name, i):
                j = INDEX[(name, i)]
                if j >= 4:
                    wait(*evacuated(*JOBS[j - 4][0]))
                return slot_of(name, i)

            def need(name, *idx):
                for i in idx:
                    wait(*evacuated(name, i))

            def mm(o_, lhsT, rhs, start, stop):
                return nc.tensor.matmul(o_, lhsT, rhs, start=start, stop=stop)

            def end(ins):
                ins.then_inc(psum_full, 1)

            def halves(slot, lhsT_of, rhs_of, n_k):
                for hf in range(2):
                    for k in range(n_k):
                        last = mm(slot[:, hf * D:(hf + 1) * D], lhsT_of(k), rhs_of(k)[:, hf * D:(hf + 1) * D], k == 0, k == n_k - 1)
                return last

            def feature_major(name, w, src, count=FC, n_k=FC, first=0):
                for c in range(first, first + count):
                    slot = begin(name, c)
                    end(halves(slot, lambda k: w[:, k, c * P:(c + 1) * P], lambda k: src[:, k, :], n_k))

            def token_major(name, w, src):
                for j in range(4):
                    slot = begin(name, j)
                    for hf in range(2):
                        t = 2 * j + hf
                        for k in range(FC):
                            last = mm(slot[:, hf * D:(hf + 1) * D], src[:, k, t * P:(t + 1) * P], w[:, k, :], k == 0, k == FC - 1)
                    end(last)

            def turn(slot_part, src):
                rows, n = src.shape[0], src.shape[1]
                return nc.tensor.transpose(slot_part, src, ident[0:rows, 0:rows])

            def xT(n):
                pe.wait_ge(rows_normed, n + 1)
                for c in range(FC):
                    slot = begin(f"xT{n}", c)
                    for t in range(TT):
                        last = turn(slot[:, t * P:(t + 1) * P], XN[:, t, c * P:(c + 1) * P])
                    end(last)

            pe.wait_ge(const_made, 7)
            pe.wait_ge(mm_bounds, 1)
            slot = begin("bounds", 0)
            mm(slot[0:1, 0:P], cmin, ident[:], True, True)
            end(mm(slot[0:1, P:2 * P], cmax, ident[:], True, True))
            xT(0)
            pe.sem_inc(onehot_used, SHIFT + RING)
            pe.wait_ge(bounds_made, 1)
            for t in range(TT):
                slot = begin("counts", t)
                first = pe.value_load(bnd_i[0:1, t:t + 1], min_val=0, max_val=EC - 1)
                last_ = pe.value_load(bnd_i[0:1, 8 + t:9 + t], min_val=0, max_val=EC)
                before = pe.value_load(bnd_i[0:1, 24 + t:25 + t], min_val=0, max_val=SHIFT + TT * EC)
                for hf in range(2):
                    mm(slot[:, hf * D:(hf + 1) * D], zeros[:, 0:P], zeros, True, False)
                with pe.Fori(first, last_) as c:
                    b = (c + before) % RING
                    pe.wait_ge(onehot_ready, c + before + 1)
                    mm(slot[:, 0:D], dstrow[:, b, :], srcrow[:, b, 0:D], False, False)
                    mm(slot[:, D:N], dstrow[:, b, :], srcrow[:, b, D:N], False, False).then_inc(onehot_used, 1)
                for hf in range(2):
                    last = mm(slot[:, hf * D:(hf + 1) * D], zeros[:, 0:P], zeros, False, True)
                end(last)
            need("counts", *range(TT))
            for t in range(TT):
                slot = begin("adjT", t)
                for s in range(TT):
                    last = turn(slot[:, s * P:(s + 1) * P], MASK[:, s, t * P:(t + 1) * P])
                end(last)
            need("xT0", *range(FC))
            for name, order in (("q0", feature_major), ("k0", feature_major), ("v0", token_major)):
                w_ready(pe, name)
                order(name, wtile(name), XT)
            need("q0", 2, 3)
            need("k0", 2, 3)
            for n in range(TT + LAG + 1):
                if n < TT:
                    slot = begin("score0", n)
                    end(halves(slot, lambda k: QT0[:, k, n * P:(n + 1) * P], lambda k: KT0[:, k, :], FC))
                i = n - LAG
                if 0 <= i < TT:
                    slot = begin("turn0", i)
                    pe.wait_ge(probs0, i + 1)
                    for s in range(TT):
                        last = turn(slot[:, s * P:(s + 1) * P], SM[:, i % 2, s * P:(s + 1) * P])
                    end(last)
                i = n - LAG - 1
                if i >= 0:
                    slot = begin("attn0", i)
                    need("v0", 2, 3)
                    need("turn0", i)
                    for s in range(TT):
                        last = mm(slot[:, 0:D], P0T[:, i % 2, s, :], V0[:, s, :], s == 0, s == TT - 1)
                    end(last)
            w_ready(pe, "winT")
            pe.wait_ge(bd_loaded, 16 * 18)
            wt = wtile("winT")
            slot = begin("wqk", 0)
            for c in range(FC):
                for k in range(FC):
                    last = mm(slot[:, 64 * c:64 * c + 64], wt[:, k, c * P:(c + 1) * P], bdqk[:, k, :], k == 0, k == FC - 1)
            end(last)
            pe.wait_ge(mix_bias, 1)
            slot = begin("bq0", 0)
            for k in range(FC):
                last = mm(slot[:, 0:32], b_bc[:, k, :], bdqk[:, k, 0:32], k == 0, k == FC - 1)
            end(last)
            slot = begin("bk0", 0)
            for k in range(FC):
                last = mm(slot[0:32, 0:1], bdqk[:, k, 32:64], col("b_in", k), k == 0, k == FC - 1)
            end(last)
            need("wqk", 0)
            slot = begin("klog", 0)
            end(halves(slot[0:32, :], lambda k: wqk[:, k, 32:64], lambda k: XT[:, k, :], FC))
            slot = begin("qlog", 0)
            for t in range(TT):
                for k in range(FC):
                    last = mm(slot[:, 32 * t:32 * t + 32], XT[:, k, t * P:(t + 1) * P], wqk[:, k, 0:32], k == 0, k == FC - 1)
            end(last)
            slot = begin("ekt", 0)
            pe.wait_ge(mix_krdy, 1)
            for t in range(TT):
                last = turn(slot[:, 32 * t:32 * t + 32], ekT[:, t * P:(t + 1) * P])
            end(last)
            slot = begin("kx", 0)
            need("ekt", 0)
            for t in range(TT):
                last = mm(slot[0:32, 0:D], ek[:, t, :], XN[:, t, :], t == 0, t == TT - 1)
            end(last)
            slot = begin("kxT", 0)
            need("kx", 0)
            for c in range(FC):
                last = turn(slot[:, 32 * c:32 * c + 32], kx[:, c * P:(c + 1) * P])
            end(last)
            slot = begin("xmT", 0)
            need("kxT", 0)
            w_ready(pe, "win")
            wi = wtile("win")
            for c in range(FC):
                for k in range(FC):
                    last = mm(slot[:, 32 * c:32 * c + 32], wi[:, k, c * P:(c + 1) * P], kxT[:, k, :], k == 0, k == FC - 1)
            end(last)
            slot = begin("kvT", 0)
            need("xmT", 0)
            for c in range(FC):
                last = mm(slot[:, 32 * c:32 * c + 32], bdv, xmT[:, c, :], True, True)
            end(last)
            slot = begin("mixM", 0)
            need("kvT", 0)
            w_ready(pe, "wout")
            for c in range(FC):
                last = mm(slot[0:32, 0:D], kvT[:, c, :], wtile("wout")[:, c, :], c == 0, c == FC - 1)
            end(last)
            slot = begin("qsT", 0)
            pe.wait_ge(mix_kscaled, 1)
            for t in range(TT):
                last = turn(slot[0:32, t * P:(t + 1) * P], ql[:, t, :])
            end(last)
            for j in range(4):
                slot = begin("mixout", j)
                need("mixM", 0)
                need("qsT", 0)
                for hf in range(2):
                    t = 2 * j + hf
                    last = mm(slot[:, hf * D:(hf + 1) * D], qsT[:, t * P:(t + 1) * P], mixM, True, True)
                end(last)
            slot = begin("wsum", 0)
            pe.wait_ge(wstat, 1)
            end(mm(slot[:, 0:2], ones[:], tiny[:, 0:2], True, True))
            xT(1)
            need("xT1", 2, 3)
            pe.wait_ge(wsign, 1)
            token_major("ffn", wtile("ffn"), XT)
            xT(2)
            need("xT2", 2, 3)
            for name in ("k1", "v1"):
                w_ready(pe, name)
                token_major(name, wtile(name), XT)
            pe.wait_ge(blk_made, 1)
            need("k1", 3)
            need("v1", 3)
            slot = begin("kv1", 0)
            for c in range(FC):
                cs = slice(c * P, (c + 1) * P)
                for t in range(TT):
                    mm(slot[:, cs], V1[:, t, cs], K1[:, t, cs], t == 0, t == TT - 1)
                for t in range(TT):
                    last = mm(slot[:, D + c * P:D + (c + 1) * P], K1[:, t, cs], ones[:], t == 0, t == TT - 1)
            end(last)
            w_ready(pe, "q1")
            feature_major("q1", wtile("q1"), XT)
            w_ready(pe, "wout1")
            need("kv1", 0)
            for j in range(2):
                slot = begin("mixM1", j)
                for hf in range(2):
                    c = 2 * j + hf
                    last = mm(slot[:, hf * D:(hf + 1) * D], kvT1[:, c, :], wtile("wout1")[:, c, :], True, True)
                end(last)
            for c in range(FC):
                slot = begin("den", c)
                need("q1", c)
                end(halves(slot, lambda k: KS1[:, c, :], lambda k: QT1[:, c, :], 1))
            need("den", 3)
            need("mixM1", 0, 1)
            token_major("mixout1", M1, QT1)
            for l in range(L):
                if l:
                    pe.wait_ge(state_ready, 2 * l)
                w_ready(pe, f"gv{l}")
                token_major(f"gv{l}", wtile(f"gv{l}"), XT)
                w_ready(pe, f"gq{l}")
                w_ready(pe, f"gk{l}")
                for step, n in attention_order():
                    slot = begin(f"{step}{l}g", n)
                    if step in "qk":
                        w = wtile(f"g{step}{l}")
                        end(halves(slot, lambda k: w[:, k, n * P:(n + 1) * P], lambda k: XT[:, k, :], FC))
                    elif step == "score":
                        pair, hf, e, i = n // 16, n // 8 % 2, n // 4 % 2, n % 4
                        need(f"q{l}g", pair)
                        need(f"k{l}g", pair)
                        t = 4 * hf + i
                        end(halves(slot, lambda k: QZ[:, pair % 2, e, t * P:(t + 1) * P], lambda k: KR[:, pair % 2, :], 1))
                    elif step == "turn":
                        wait(probs, UNITS * l + n + 1)
                        for s in range(TT):
                            last = turn(slot[:, s * P:(s + 1) * P], SM[:, n % 2, s * P:(s + 1) * P])
                        end(last)
                    elif step == "rsum":
                        wait(recips, 8 * l + n + 1)
                        end(turn(slot[0:8, 0:P], rl[:]))
                    elif step == "rsum_bc":
                        need(f"rsum{l}g", n)
                        for i in range(4):
                            last = mm(slot[:, i * P:(i + 1) * P], sel[:, i, :], rT, True, True)
                        end(last)
                    elif step == "agg":
                        need(f"gv{l}", 2, 3)
                        need(f"turn{l}g", 8 * n + 6, 8 * n + 7)
                        for s in range(TT):
                            for e in range(2):
                                g = 2 * n + e
                                head = 2 * (n // 2) + e
                                last = mm(slot[e * DH:(e + 1) * DH, 0:D], GV[:, s, head * DH:(head + 1) * DH],
                                          PTr[:, g % 3, s, :], s == 0, s == TT - 1)
                        end(last)
                need(f"agg{l}g", 7)
                w_ready(pe, f"go{l}")
                feature_major(f"wo{l}", wtile(f"go{l}"), AG)
                w_ready(pe, f"w12{l}")
                ws = W[:, WEIGHTS.index(f"w12{l}") % WSLOTS, :]
                pe.wait_ge(state_ready, 2 * l + 1)
                feature_major(f"h{l}", ws[:, 0:1024].rearrange("p (k n) -> p k n", k=FC), XT, count=2)
                need(f"h{l}", 0, 1)
                feature_major(f"f{l}", ws[:, 1024:2048].rearrange("p (k n) -> p k n", k=2), KR, n_k=2)
            pe.wait_ge(state_ready, 2 * L)
            for j in range(4):
                slot = begin("gT", j)
                for hf in range(2):
                    for c in range(FC):
                        t = 2 * j + hf
                        last = turn(slot[:, hf * D + c * P:hf * D + (c + 1) * P], XT[:, c, t * P:(t + 1) * P])
                end(last)
            pe.wait_ge(hid_ready, 1)
            for q in range(4):
                slot = begin("fT", q)
                for s in range(4):
                    n = 4 * q + s
                    last = turn(slot[0:6, s * P:(s + 1) * P], Fx[:, n // 2, n % 2, 0:6])
                end(last)
            pe.wait_ge(nib_loaded, 16 * 13)
            need("fT", 3)
            for n in range(16):
                slot = begin("hid", n)
                end(mm(slot[:, 0:3 * GE], FT[:, n * P:(n + 1) * P], W1s, True, True))


def kernel(**inputs):
    import concourse.bacc as bacc
    from concourse.bass_utils import run_bass_kernel_spmd

    g = {k: np.asarray(v) for k, v in inputs.items()}

    def chunks(v):
        return v.reshape(-1, P).T

    src, dst = g["src"].reshape(EC, P), g["dst"].reshape(EC, P)
    vec = {"bq": g["L0_gnn_bq"], "bk": g["L0_gnn_bk"], "b_in": g["L0_mix_b_in"]}
    names = {"gbq": "bq", "gbo": "bo", "gb2": "b2", "g1": "g1", "be1": "beta1", "g2": "g2", "be2": "beta2", "gb1": "b1"}
    for l in range(L):
        vec.update({f"{k}{l}": g[f"L1_gnn_{v}"][l] for k, v in names.items()})
    wqkv = g["L1_mix_Wqkv"]
    nets = ("and", "or", "xor")
    arrays = {
        "idx": np.concatenate([dst.T, src.T, dst], axis=1),
        "x": g["x"],
        "cols": np.concatenate([chunks(vec[n]) for n in COLS], axis=1),
        "rows": np.stack([g[n] for n in ROWS]),
        "q0": g["L0_gnn_Wq"], "k0": g["L0_gnn_Wk"], "v0": g["L0_gnn_Wv"],
        "winT": g["L0_mix_W_in"].T, "win": g["L0_mix_W_in"], "wout": g["L0_mix_W_out"],
        "mq": g["L0_mix_W_q"], "mk": g["L0_mix_W_k"], "mv": g["L0_mix_W_v"],
        "ffn": g["L0_ffn_weight"],
        "q1": wqkv[:, 0:D], "k1": wqkv[:, D:2 * D], "v1": wqkv[:, 2 * D:3 * D], "wout1": g["L1_mix_Wout"],
        "nw1": np.stack([g[f"L1_ffn_{k}_w1"] for k in nets]),
        "nb1": np.stack([g[f"L1_ffn_{k}_b1"] for k in nets]),
        "nw2": np.stack([g[f"L1_ffn_{k}_w2"][:, 64] for k in nets]),
        "nb2": np.stack([g[f"L1_ffn_{k}_b2"][64:65] for k in nets], axis=1),
    }
    for l in range(L):
        for k in "qkvo":
            arrays[f"g{k}{l}"] = g[f"L1_gnn_W{k}"][l].T
    fold = lambda w: w.reshape(-1, P, w.shape[1]).transpose(1, 0, 2).reshape(P, -1)
    arrays["w12"] = np.stack([np.concatenate([fold(g["L1_gnn_W1"][l].T), fold(g["L1_gnn_W2"][l].T)], axis=1)
                              for l in range(L)])

    nc = bacc.Bacc("TRN2", target_bir_lowering=False, num_devices=1)
    feed, aps = {}, {}
    for name, v in arrays.items():
        v = np.ascontiguousarray(v)
        feed[f"in_{name}"] = v
        aps[name] = nc.dram_tensor(f"in_{name}", v.shape, mybir.dt.from_np(v.dtype), kind="ExternalInput").ap()
    out = nc.dram_tensor("out_0", (N, D), mybir.dt.float32, kind="ExternalOutput").ap()
    build(nc, aps, out)
    r = run_bass_kernel_spmd(nc, [feed], core_ids=[0])
    return r.results[0]["out_0"]
```

```python
import numpy as np
import concourse.bass as bass
from concourse import mybir
from contextlib import ExitStack

N = 1024
D = 512
E = 16384
P = 128
TT = N // P
FC = D // P
EC = E // P
H = 8
DH = D // H
R = 4
L = 2
F2 = 256
GE = 160
EPS = 1e-5
NO_EDGE = -1e30
NEG = -1e6
MAGIC = 1.5 * 2.0 ** 23
GC = 4
NG = EC // GC
SHIFT = NG

UNITS = H * TT
LAG = 2


def attention_order():
    order = [("q", 0), ("k", 0)]
    for n in range(UNITS + LAG + 1):
        if n % 16 == 8 and n // 16 + 1 < H // 2:
            order += [("q", n // 16 + 1), ("k", n // 16 + 1)]
        if n < UNITS:
            order.append(("score", n))
        m = n - LAG
        if 0 <= m < UNITS:
            order.append(("turn", m))
            if m % 8 == 7:
                order.append(("rsum", m // 8))
        if m >= 8 and m % 8 == 0:
            order += [("rsum_bc", m // 8 - 1), ("agg", m // 8 - 1)]
    return order


def job_table():
    jobs = []

    def add(name, count, engines):
        for i in range(count):
            jobs.append(((name, i), engines[i % len(engines)]))

    A, V = "act", "dve"
    add("bounds", 1, [V])
    add("xT0", FC, [V, A])
    add("counts", TT, [A])
    add("adjT", TT, [V, A])
    for name in ("q0", "k0", "v0"):
        add(name, 4, [V, A])
    for n in range(TT + LAG + 1):
        if n < TT:
            jobs.append((("score0", n), V))
        if 0 <= n - LAG < TT:
            jobs.append((("turn0", n - LAG), A))
        if n - LAG >= 1:
            jobs.append((("attn0", n - LAG - 1), V))
    for name in ("wqk", "bq0", "bk0", "klog", "qlog", "ekt", "kx", "kxT", "xmT", "kvT", "mixM", "qsT"):
        add(name, 1, [V])
    add("wsum", 1, [V])
    add("mixout", 4, [V])
    add("xT1", FC, [V, A])
    add("ffn", 4, [V])
    add("xT2", FC, [V, A])
    add("k1", 4, [V])
    add("v1", 4, [A])
    add("kv1", 1, [V])
    add("q1", 4, [V])
    add("mixM1", 2, [V, A])
    add("den", 1, [V])
    add("gv0", 4, [V, A])
    add("zb", 4, [V])
    add("mixout1", 4, [V])
    for l in range(L):
        if l:
            add(f"gv{l}", 4, [V, A])
        for step, i in attention_order():
            engine = {"q": V, "k": A, "score": V, "turn": (V, A)[i % 2], "rsum": V, "rsum_bc": A, "agg": V}[step]
            jobs.append(((f"{step}{l}g", i), engine))
        add(f"wo{l}", FC, [V])
        add(f"h{l}", 2, [A])
        add(f"f{l}", FC, [V])
    add("gT", 4, [V])
    add("fT", 4, [V])
    add("hid", 16, [V])
    return jobs


JOBS = job_table()
INDEX = {name: j for j, (name, _) in enumerate(JOBS)}
EVAC_COUNT = {}
_seen = {"act": 0, "dve": 0}
for _name, _engine in JOBS:
    _seen[_engine] += 1
    EVAC_COUNT[_name] = _seen[_engine]

COLS = {}


def _col(name, n):
    COLS[name] = (sum(w for _, w in COLS.values()), n)


for _n in ("bq", "bk", "b_in"):
    _col(_n, FC)
for _l in range(L):
    for _n in ("gbq", "gbo", "gb2", "g1", "be1", "g2", "be2"):
        _col(f"{_n}{_l}", FC)
    _col(f"gb1{_l}", 2)
NCOL = sum(w for _, w in COLS.values())
ROWS = ["L0_gnn_bv", "L0_mix_b_out", "L0_ffn_bias", "L1_mix_bout", "L1_gnn_ln_g", "L1_gnn_ln_b"]

WEIGHTS = ["q0", "k0", "v0", "winT", "win", "wout", "ffn", "k1", "v1", "q1", "wout1"]
for _l in range(L):
    WEIGHTS += [f"gv{_l}", f"gq{_l}", f"gk{_l}", f"go{_l}", f"w12{_l}"]
WSLOTS = 3


def build(nc, a, out):
    fp32, bf16, fp16, i32 = mybir.dt.float32, mybir.dt.bfloat16, mybir.dt.float16, mybir.dt.int32
    ALU = mybir.AluOpType
    ACT = mybir.ActivationFunctionType
    AX = mybir.AxisListType
    ctx = ExitStack()
    with ctx:
        def sb(name, shape, dt=fp32):
            return ctx.enter_context(nc.sbuf_tensor(name, shape, dt))

        def sem(name):
            return ctx.enter_context(nc.semaphore(name))

        X = sb("X", [P, TT, D])
        XN = sb("XN", [P, TT, D])
        XT = sb("XT", [P, FC, N])
        QZ = sb("QZ", [P, 2, 2, N])
        KR = sb("KR", [P, 2, N])
        AG = sb("AG", [P, FC, N])
        MASK = sb("MASK", [P, TT, N])
        PT = sb("PT", [P, 12288])
        SM = sb("SM", [P, 2, N])
        W = sb("W", [P, WSLOTS, FC * D])
        BC = sb("BC", [P, 2, D])
        ident = sb("ident", [P, P])
        ones = sb("ones", [P, P])
        sel = sb("sel", [8, 4, P])
        cols = sb("cols", [P, NCOL])
        st = sb("st", [P, TT, 6])
        mv = sb("mv", [P, TT, 2])
        rstd = sb("rstd", [P, TT])
        nm = sb("nm", [P, 8])
        ls = sb("ls", [P, 2, 8])
        rl = sb("rl", [P, 8])
        tiny = sb("tiny", [P, 4])
        bns = sb("bns", [P, 8])

        psum = ctx.enter_context(nc.psum_tensor("slots", [P, 4, N], fp32))

        flat = lambda t: t[:].rearrange("p a b -> p (a b)")
        qz = QZ[:].rearrange("p a b c -> p (a b c)")
        ag, kr = flat(AG), flat(KR)
        iota = PT[:, 0:512].bitcast(fp16)
        srcrow = PT[:, 512:2560].bitcast(bf16).rearrange("p (r n) -> p r n", r=GC)
        dstrow = PT[:, 2560:2816].bitcast(bf16).rearrange("p (r n) -> p r n", r=GC)
        idx_i = PT[:, 2816:3200].bitcast(i32)
        dst_f, src_f, drow_f = PT[:, 3200:3328], PT[:, 3328:3456], PT[:, 3456:3584]
        zeros = PT[:, 3584:3584 + 256].bitcast(bf16)
        cmin, cmax = PT[:, 3840:3841], PT[:, 3841:3842]
        brow = PT[0:1, 3842:3842 + 256]
        lo8, c8, relA, relB = (ag[0:1, 256 * n:256 * n + TT * NG].rearrange("p (t c) -> p t c", t=TT) for n in range(4))
        glow, ghigh = ag[0:1, 1024:1024 + NG], ag[0:1, 1056:1056 + NG]
        bnd = PT[0:1, 4100:4132]
        bnd_i = PT[0:1, 4132:4164].bitcast(i32)
        QT0, KT0 = qz.rearrange("p (c n) -> p c n", c=FC), AG
        V0 = PT[:, 0:4096].rearrange("p (t d) -> p t d", t=TT)
        adj0 = PT[:, 4096:8192].bitcast(bf16).rearrange("p (t n) -> p t n", t=TT)
        negm = PT[:, 8192:10240].rearrange("p (r n) -> p r n", r=2)
        P0T = PT[:, 10240:12288].rearrange("p (r s n) -> p r s n", r=2, s=TT)
        o = [0]

        def part(n, rows=P):
            o[0] += n
            return qz[0:rows, o[0] - n:o[0]]

        bdqk = part(256).rearrange("p (c n) -> p c n", c=FC)
        bdv = part(128)
        wqk = part(256).rearrange("p (c n) -> p c n", c=FC)
        b_bc = part(512).rearrange("p (c n) -> p c n", c=FC)
        bq_bc = part(32)
        bk_col = part(1, 32)
        part(7)
        ql = part(256).rearrange("p (t n) -> p t n", t=TT)
        qm = part(64)
        qr = part(64)
        ek = part(256).rearrange("p (t n) -> p t n", t=TT)
        kx = part(512, 32)
        kxT = part(128).rearrange("p (c n) -> p c n", c=FC)
        xmT = part(128).rearrange("p (c n) -> p c n", c=FC)
        hm = part(128).rearrange("p (c n) -> p c n", c=FC)
        kvT = part(128).rearrange("p (c n) -> p c n", c=FC)
        mixM = part(512, 32)
        kmax, ksum, krec = part(1, 32), part(1, 32), part(1, 32)
        ekT, qsT = KR[0:32, 0, :], KR[0:32, 1, :]
        K1 = PT[:, 0:4096].rearrange("p (t d) -> p t d", t=TT)
        V1 = PT[:, 4096:8192].rearrange("p (t d) -> p t d", t=TT)
        kvT1 = PT[:, 8192:8704].rearrange("p (c n) -> p c n", c=FC)
        KS1 = PT[:, 8704:8736].rearrange("p (c h) -> p c h", c=FC)
        selh = PT[:, 11392:11904].rearrange("p (c n) -> p c n", c=FC)
        M1 = PT[:, 9216:11264].rearrange("p (c n) -> p c n", c=FC)
        blk = PT[:, 11264:11392]
        QT1 = QT0
        zT = AG[:, 0, :]
        PTr = PT[:, :].rearrange("p (b s n) -> p b s n", b=3, s=TT)
        GV = XN
        rbc = BC[:, 0, :]
        rT = BC[0:8, 1, 0:128]
        G = PT[:, 0:4096].rearrange("p (t d) -> p t d", t=TT)
        W1s = qz[:, 0:480]
        w2bc = qz[:, 512:992]
        b2bc = qz[:, 992:995]
        Fx = qz[:, 1024:1152].rearrange("p (t r j) -> p t r j", t=TT, r=2)
        FT = qz[:, 2048:4096]
        bits = ag[:, 0:512].rearrange("p (t j n) -> p t j n", t=TT, j=4)
        m16 = ag[:, 512:544].rearrange("p (t j) -> p t j", t=TT)
        i16 = ag[:, 544:560]
        i16m = ag[:, 560:576]
        flags = ag[:, 576:608].rearrange("p (t j) -> p t j", t=TT)
        ysel = ag[:, 608:656].rearrange("p (t r k) -> p t r k", t=TT, r=2)
        pick = ag[:, 656:680].rearrange("p (t k) -> p t k", t=TT)
        res = ag[:, 688:704].rearrange("p (t r) -> p t r", t=TT)
        act_on = ag[:, 704:712]
        oneh = ag[:, 768:1024].rearrange("p (t r n) -> p t r n", t=TT, r=2)
        hidb = [ag[:, 1024:1504], ag[:, 1536:2016]]
        yk = ag[:, 2048:2096].rearrange("p (t r k) -> p t r k", t=TT, r=2)

        psum_full, dve_evacuated, act_evacuated = sem("psum_full"), sem("dve_evacuated"), sem("act_evacuated")
        w_loaded = [sem(f"w_loaded{s}") for s in range(WSLOTS)]
        row_loaded = [sem(f"row_loaded{s}") for s in range(2)]
        x_loaded, idx_loaded, cols_loaded, bd_loaded, nib_loaded = (
            sem(n) for n in ("x_loaded", "idx_loaded", "cols_loaded", "bd_loaded", "nib_loaded"))
        const_made, bd_cleared, blk_made, q_cleared, i16_made = (
            sem(n) for n in ("const_made", "bd_cleared", "blk_made", "q_cleared", "i16_made"))
        pool_link, dve_link, act_link = sem("pool_link"), sem("dve_link"), sem("act_link")
        bounds_made, onehot_ready, onehot_used, mm_bounds = (
            sem(n) for n in ("bounds_made", "onehot_ready", "onehot_used", "minmax_made"))
        counts_floored, logs_taken, mask_made = sem("counts_floored"), sem("logs_taken"), sem("mask_made")
        negm_made, masked0, probs0, x_biased = sem("negm_made"), sem("masked0"), sem("probs0"), sem("x_biased")
        rows_normed, var_ready, std_ready = sem("rows_normed"), sem("var_ready"), sem("std_ready")
        mix_bias, mix_kexp, mix_krdy, mix_kscaled, mix_qs, mix_qe = (
            sem(n) for n in ("b_broadcast", "keys_max_ready", "keys_exp", "mix_kscaled", "mix_queries_ready", "mix_qexp"))
        wstat, wsign, wmean, ffn_row = sem("w_sums"), sem("w_signs"), sem("w_mean"), sem("ffn_row_used")
        kneg, kexp, x1_biased = sem("min_ready"), sem("elu_exp"), sem("x1_biased")
        probs, recips, bn_ready, state_ready, last_chunk_ready = (
            sem(n) for n in ("probs", "recips", "bn_ready", "state_ready", "last_chunk_ready"))
        hid_ready, stored = sem("features_ready"), sem("stored")
        shift_added, out_summed, nibbles_added, hid_cleared = (
            sem(n) for n in ("shift_added", "out_summed", "nibbles_added", "hid_cleared"))

        slot_of = lambda name, i: psum[:, INDEX[(name, i)] % 4, :]

        def evacuated(name, i):
            engine = JOBS[INDEX[(name, i)]][1]
            return (dve_evacuated if engine == "dve" else act_evacuated), EVAC_COUNT[(name, i)]

        def full(eng, name, i):
            eng.wait_ge(psum_full, INDEX[(name, i)] + 1)
            return slot_of(name, i)

        def done(eng, name, i):
            eng.wait_ge(*evacuated(name, i))

        def col(name, c=None):
            at, w = COLS[name]
            return cols[:, at:at + w] if c is None else cols[:, at + c:at + c + 1]

        def wtile(name):
            s = WEIGHTS.index(name) % WSLOTS
            return W[:, s, :].rearrange("p (k n) -> p k n", k=FC)

        def w_ready(eng, name):
            n = WEIGHTS.index(name)
            eng.wait_ge(w_loaded[n % WSLOTS], 16 * (n // WSLOTS + 1))

        def row(name):
            return BC[:, ROWS.index(name) % 2, :]

        def row_ready(eng, name):
            n = ROWS.index(name)
            eng.wait_ge(row_loaded[n % 2], 16 * (n // 2 + 1))

        LAST_USE = {
            "q0": ("q0", 3), "k0": ("k0", 3), "v0": ("v0", 3), "winT": ("wqk", 0), "win": ("xmT", 0),
            "wout": ("mixM", 0), "ffn": ("ffn", 3), "k1": ("k1", 3), "v1": ("v1", 3), "q1": ("q1", 3),
            "wout1": ("mixM1", 1)}
        for l in range(L):
            LAST_USE.update({f"gv{l}": (f"gv{l}", 3), f"gq{l}": (f"q{l}g", 3), f"gk{l}": (f"k{l}g", 3),
                             f"go{l}": (f"wo{l}", 3), f"w12{l}": (f"f{l}", 3)})

        block = ctx.enter_context(nc.Block())

        @block.sync
        def _(sp):
            sp.dma_start(idx_i, a["idx"]).then_inc(idx_loaded, 16)
            sp.dma_start(X[:], a["x"].rearrange("(t p) d -> p t d", p=P)).then_inc(x_loaded, 16)
            sp.dma_start(cols[:], a["cols"]).then_inc(cols_loaded, 16)

            def load_row(n):
                sp.dma_start(BC[:, n % 2, :], a["rows"][n:n + 1, :].broadcast_to([P, D])).then_inc(row_loaded[n % 2], 16)

            def load_weight(name):
                n = WEIGHTS.index(name)
                if n >= WSLOTS:
                    sp.wait_ge(psum_full, INDEX[LAST_USE[WEIGHTS[n - WSLOTS]]] + 1)
                if name.startswith("w12"):
                    l = int(name[-1])
                    sp.dma_start(W[:, n % WSLOTS, :], a["w12"][l]).then_inc(w_loaded[n % WSLOTS], 16)
                else:
                    sp.dma_start(wtile(name), a[name].rearrange("(k p) n -> p k n", p=P)).then_inc(w_loaded[n % WSLOTS], 16)

            load_row(0)
            load_row(1)
            for name in WEIGHTS[:5]:
                load_weight(name)
            sp.wait_ge(bd_cleared, 1)
            for h in range(H):
                p0, c = (h % 2) * DH, h // 2
                sp.dma_start(bdqk[p0:p0 + DH, c, R * h:R * h + R], a["mq"]).then_inc(bd_loaded, 16)
                sp.dma_start(bdqk[p0:p0 + DH, c, 32 + R * h:32 + R * h + R], a["mk"]).then_inc(bd_loaded, 16)
            for e in range(2):
                sp.dma_start(bdv[e * DH:(e + 1) * DH, e * DH:(e + 1) * DH], a["mv"]).then_inc(bd_loaded, 16)
            sp.wait_ge(x_biased, TT)
            load_row(2)
            load_row(3)
            for name in WEIGHTS[5:]:
                load_weight(name)
            sp.wait_ge(*evacuated(f"agg{L - 1}g", 7))
            load_row(4)
            load_row(5)
            sp.wait_ge(hid_cleared, 1)
            for k in range(3):
                c0 = GE * k
                for r0, n, at in ((0, 2, 0), (44, 3, 2)):
                    sp.dma_start(W1s[at:at + n, c0:c0 + GE], a["nw1"][k, r0:r0 + n, :]).then_inc(nib_loaded, 16)
                sp.dma_start(W1s[5:6, c0:c0 + GE], a["nb1"][k:k + 1, :]).then_inc(nib_loaded, 16)
                sp.dma_start(w2bc[:, c0:c0 + GE], a["nw2"][k:k + 1, :].broadcast_to([P, GE])).then_inc(nib_loaded, 16)
            sp.dma_start(b2bc, a["nb2"].broadcast_to([P, 3])).then_inc(nib_loaded, 16)
            sp.wait_ge(stored, 32)

        @block.gpsimd
        def _(pool):
            links = [0]

            def link(ins):
                links[0] += 1
                ins.then_inc(pool_link, 1)
                pool.wait_ge(pool_link, links[0])

            link(nc.gpsimd.memset(ident[:], 0.0))
            nc.gpsimd.affine_select(out=ident[:], in_=ident[:], compare_op=ALU.not_equal, fill=1.0, base=0,
                                    pattern=[[-1, P]], channel_multiplier=1).then_inc(const_made, 1)
            nc.gpsimd.iota(iota, [[1, N]], base=0, channel_multiplier=0,
                           allow_small_or_imprecise_dtypes=True).then_inc(const_made, 1)
            nc.gpsimd.iota(lo8, [[P, TT], [0, NG]], base=0, channel_multiplier=0,
                           allow_small_or_imprecise_dtypes=True).then_inc(const_made, 1)
            nc.gpsimd.iota(c8, [[0, TT], [1, NG]], base=0, channel_multiplier=0,
                           allow_small_or_imprecise_dtypes=True).then_inc(const_made, 1)
            nc.gpsimd.memset(zeros, 0.0).then_inc(const_made, 1)
            nc.gpsimd.memset(ones[:], 1.0).then_inc(const_made, 1)
            link(nc.gpsimd.memset(sel[:], 0.0))
            nc.gpsimd.affine_select(out=sel[:].rearrange("k i (e m) -> k i e m", e=2),
                                    in_=sel[:].rearrange("k i (e m) -> k i e m", e=2),
                                    compare_op=ALU.not_equal, fill=1.0, base=0,
                                    pattern=[[-1, 4], [-4, 2], [0, DH]], channel_multiplier=1).then_inc(const_made, 1)
            pool.wait_ge(rows_normed, TT)
            row_ready(pool, "L0_gnn_bv")
            row_ready(pool, "L0_mix_b_out")
            for t in range(TT):
                link(nc.gpsimd.tensor_tensor(X[:, t, :], X[:, t, :], row("L0_gnn_bv"), ALU.add))
                nc.gpsimd.tensor_tensor(X[:, t, :], X[:, t, :], row("L0_mix_b_out"), ALU.add).then_inc(x_biased, 1)
            for i in range(TT + 2):
                if i >= 2:
                    pool.wait_ge(logs_taken, i - 1)
                    nc.gpsimd.tensor_tensor(MASK[:, i - 2, :], MASK[:, i - 2, :], KR[:, i % 2, :],
                                            ALU.add).then_inc(mask_made, 1)
                if i < TT:
                    done(pool, "adjT", 6)
                    done(pool, "adjT", 7)
                    if i >= 2:
                        pool.wait_ge(masked0, i - 1)
                        pool.wait_ge(mask_made, i - 1)
                    nc.gpsimd.tensor_scalar(negm[:, i % 2, :], adj0[:, i, :], -NEG, NEG, ALU.mult, ALU.add).then_inc(negm_made, 1)
                    nc.gpsimd.tensor_scalar(KR[:, i % 2, :], MASK[:, i, :], 1.0, None, ALU.max).then_inc(counts_floored, 1)
                    link(nc.gpsimd.tensor_scalar(MASK[:, i, :], MASK[:, i, :], 0.5, NO_EDGE, ALU.is_lt, ALU.mult))
            pool.wait_ge(psum_full, INDEX[("score0", TT - 1)] + 1)
            nc.gpsimd.memset(bdqk, 0.0)
            link(nc.gpsimd.memset(bdv, 0.0))
            link(nc.gpsimd.memset(hm, 1.0))
            hm4 = hm.rearrange("p c (h r) -> p c h r", r=R)
            link(nc.gpsimd.affine_select(out=hm4, in_=hm4, compare_op=ALU.is_ge, fill=0.0, base=0,
                                         pattern=[[P, FC], [-DH, H], [0, R]], channel_multiplier=1))
            nc.gpsimd.affine_select(out=hm4, in_=hm4, compare_op=ALU.is_ge, fill=0.0, base=DH - 1,
                                    pattern=[[-P, FC], [DH, H], [0, R]], channel_multiplier=-1).then_inc(bd_cleared, 1)
            pool.wait_ge(rows_normed, 3 * TT)
            link(nc.gpsimd.memset(blk, 0.0))
            link(nc.gpsimd.memset(blk[0:DH, 0:DH], 1.0))
            link(nc.gpsimd.memset(blk[DH:P, DH:P], 1.0))
            link(nc.gpsimd.memset(zT, 0.0))
            link(nc.gpsimd.memset(selh, 0.0))
            s4 = selh.rearrange("k c (e m) -> k c e m", e=2)
            nc.gpsimd.affine_select(out=s4, in_=s4, compare_op=ALU.not_equal, fill=1.0, base=0,
                                    pattern=[[-2, FC], [-1, 2], [0, DH]], channel_multiplier=1).then_inc(blk_made, 1)
            pool.wait_ge(blk_made, 1)
            row_ready(pool, "L1_mix_bout")
            for t in range(TT):
                nc.gpsimd.tensor_tensor(X[:, t, :], X[:, t, :], row("L1_mix_bout"), ALU.add).then_inc(x1_biased, 1)
            pool.wait_ge(x1_biased, TT)
            pool.wait_ge(psum_full, INDEX[("mixout1", 3)] + 1)
            for b in range(2):
                link(nc.gpsimd.memset(QZ[DH:P, b, 0, :], 0.0))
                nc.gpsimd.memset(QZ[0:DH, b, 1, :], 0.0).then_inc(q_cleared, 1)
                pool.wait_ge(q_cleared, b + 1)
            pool.wait_ge(psum_full, INDEX[(f"score{L - 1}g", UNITS - 1)] + 1)
            link(nc.gpsimd.memset(qz[:, 0:480], 0.0))
            link(nc.gpsimd.memset(FT, 0.0))
            nc.gpsimd.memset(Fx, 1.0).then_inc(hid_cleared, 1)
            pool.wait_ge(hid_cleared, 1)
            row_ready(pool, "L1_gnn_ln_b")
            for t in range(TT):
                nc.gpsimd.tensor_tensor(X[:, t, :], X[:, t, :], row("L1_gnn_ln_b"), ALU.add).then_inc(shift_added, 1)
            pool.wait_ge(shift_added, TT)
            pool.wait_ge(psum_full, INDEX[(f"wo{L - 1}", 3)] + 1)
            nc.gpsimd.iota(i16, [[1, 16]], base=0, channel_multiplier=0,
                           allow_small_or_imprecise_dtypes=True).then_inc(i16_made, 1)
            nc.gpsimd.iota(i16m, [[1, 16]], base=-16, channel_multiplier=0,
                           allow_small_or_imprecise_dtypes=True).then_inc(i16_made, 1)
            for t in range(TT):
                pool.wait_ge(rows_normed, 3 * TT + t + 1)
                nc.gpsimd.tensor_tensor(X[:, t, :], X[:, t, :], XN[:, t, :], ALU.add).then_inc(out_summed, 1)

        @block.scalar
        def _(act):
            def copy_out(dst, name, i, view=None):
                src = full(act, name, i)
                src = src if view is None else view(src)
                nc.scalar.activation(dst, src, ACT.Copy).then_inc(act_evacuated, 1)

            def take_std(n):
                act.wait_ge(var_ready, n)
                nc.scalar.activation(rstd[:], rstd[:], ACT.Sqrt).then_inc(std_ready, 1)

            def xT(n):
                for j in (1, 3):
                    copy_out(XT[:, :, 2 * j * P:2 * (j + 1) * P], f"xT{n}", j, lambda s: s.rearrange("p (c n) -> p c n", c=FC))

            take_std(1)
            xT(0)
            for t in range(TT):
                copy_out(MASK[:, t, :], "counts", t)
            for t in range(1, TT, 2):
                src = full(act, "adjT", t)
                nc.scalar.activation(adj0[:, t, :], src, ACT.Sign).then_inc(act_evacuated, 1)
            for name, dst in (("q0", QT0), ("k0", KT0)):
                if name == "q0":
                    act.wait_ge(cols_loaded, 16)
                for c in (1, 3):
                    src = full(act, name, c)
                    nc.scalar.activation(dst[:, c, :], src, ACT.Identity, bias=col("bq" if name == "q0" else "bk", c),
                                         scale=1.0).then_inc(act_evacuated, 1)
            for j in (1, 3):
                copy_out(V0[:, 2 * j:2 * j + 2, :], "v0", j, lambda s: s.rearrange("p (t d) -> p t d", t=2))
            for n in range(TT + LAG + 1):
                if n < TT:
                    act.wait_ge(counts_floored, n + 1)
                    nc.scalar.activation(KR[:, n % 2, :], KR[:, n % 2, :], ACT.Ln).then_inc(logs_taken, 1)
                if n >= 1 and n - 1 < TT:
                    i = n - 1
                    act.wait_ge(masked0, i + 1)
                    nc.scalar.activation(SM[:, i % 2, :], SM[:, i % 2, :], ACT.Exp, bias=nm[:, i:i + 1], scale=-1.0,
                                         accum_out=ls[:, 0, i:i + 1]).then_inc(probs0, 1)
                i = n - LAG
                if 0 <= i < TT:
                    if i >= 2:
                        act.wait_ge(psum_full, INDEX[("attn0", i - 2)] + 1)
                    copy_out(P0T[:, i % 2, :, :], "turn0", i, lambda s: s.rearrange("p (s n) -> p s n", s=TT))
            act.wait_ge(mix_kexp, 1)
            nc.scalar.activation(ekT, ekT, ACT.Exp, bias=kmax, scale=1.0, accum_out=ksum).then_inc(mix_krdy, 1)
            act.wait_ge(mix_qs, 1)
            nc.scalar.activation(ql, ql, ACT.Exp).then_inc(mix_qe, 1)
            act.wait_ge(wmean, 1)
            wf = wtile("ffn")
            nc.scalar.activation(wf, wf, ACT.Sign, bias=tiny[:, 2:3], scale=1.0).then_inc(wsign, 1)
            take_std(2)
            xT(1)
            take_std(3)
            xT(2)
            for j in range(4):
                act.wait_ge(kneg, j + 1)
                nc.scalar.activation(SM[:, j % 2, :], SM[:, j % 2, :], ACT.Exp).then_inc(kexp, 1)
            for j in range(4):
                copy_out(V1[:, 2 * j:2 * j + 2, :], "v1", j, lambda s: s.rearrange("p (t d) -> p t d", t=2))
            for j in range(4):
                act.wait_ge(kneg, j + 5)
                nc.scalar.activation(SM[:, j % 2, :], SM[:, j % 2, :], ACT.Exp).then_inc(kexp, 1)
            copy_out(M1[:, 2:4, :], "mixM1", 1, lambda s: s.rearrange("p (t d) -> p t d", t=2))

            for l in range(L):
                for j in (1, 3):
                    copy_out(GV[:, 2 * j:2 * j + 2, :], f"gv{l}", j, lambda s: s.rearrange("p (t d) -> p t d", t=2))

                def exp_unit(n):
                    act.wait_ge(*evacuated(f"score{l}g", n))
                    if n % 8 == 0 and n >= 16:
                        act.wait_ge(recips, 8 * l + n // 8 - 1)
                    nc.scalar.activation(SM[:, n % 2, :], SM[:, n % 2, :], ACT.Exp, bias=nm[:, n % 8:n % 8 + 1], scale=-1.0,
                                         accum_out=ls[:, n // 8 % 2, n % 8:n % 8 + 1]).then_inc(probs, 1)

                for step, n in attention_order():
                    if step == "k":
                        if n >= 2:
                            act.wait_ge(psum_full, INDEX[(f"score{l}g", 16 * n - 17)] + 1)
                        copy_out(KR[:, n % 2, :], f"k{l}g", n)
                    elif step == "score" and n >= 1:
                        exp_unit(n - 1)
                    elif step == "turn":
                        if n == UNITS - 2:
                            exp_unit(UNITS - 1)
                        if n % 2 == 1:
                            g, i = n // 4, n % 4
                            if g >= 3:
                                act.wait_ge(psum_full, INDEX[(f"agg{l}g", (g - 3) // 2)] + 1)
                            elif l == 0:
                                act.wait_ge(psum_full, INDEX[("mixout1", 3)] + 1)
                            else:
                                act.wait_ge(psum_full, INDEX[("agg0g", 7)] + 1)
                            copy_out(PTr[:, g % 3, :, i * P:(i + 1) * P], f"turn{l}g", n,
                                     lambda s: s.rearrange("p (s n) -> p s n", s=TT))
                    elif step == "rsum_bc":
                        if n >= 1:
                            done(act, f"agg{l}g", n - 1)
                        src = full(act, f"rsum_bc{l}g", n)
                        nc.scalar.activation(rbc, src[:, 0:D], ACT.Copy).then_inc(act_evacuated, 1)
                def bn_last_chunk(n):
                    take_std(n + 4)
                    act.wait_ge(bn_ready, n + 1)
                    nc.scalar.activation(XT[:, 3, :], XT[:, 3, :], ACT.Identity, bias=bns[:, 7:8],
                                         scale=bns[:, 3:4]).then_inc(last_chunk_ready, 1)

                bn_last_chunk(2 * l)
                for c in range(2):
                    src = full(act, f"h{l}", c)
                    nc.scalar.activation(KR[:, c, :], src, ACT.Relu, bias=col(f"gb1{l}", c), scale=1.0).then_inc(act_evacuated, 1)
                bn_last_chunk(2 * l + 1)
            take_std(4 + 2 * L)
            take_std(5 + 2 * L)
            o_v = out.rearrange("(t p) d -> p t d", p=P)
            act.wait_ge(out_summed, TT)
            act.dma_start(o_v[:, :, 112:D], X[:, :, 112:D]).then_inc(stored, 16)
            act.wait_ge(nibbles_added, 1)
            act.dma_start(o_v[:, :, 0:112], X[:, :, 0:112]).then_inc(stored, 16)
            act.wait_ge(stored, 32)

        @block.vector
        def _(dve):
            links = [0]

            def link(ins):
                links[0] += 1
                ins.then_inc(dve_link, 1)
                dve.wait_ge(dve_link, links[0])

            rounds = [0]

            def std(n_cols):
                rounds[0] += 1
                nc.vector.tensor_scalar(rstd[:, 0:n_cols], mv[:, 0:n_cols, 1], EPS, None, ALU.add).then_inc(var_ready, 1)
                dve.wait_ge(std_ready, rounds[0])
                link(nc.vector.reciprocal(rstd[:, 0:n_cols], rstd[:, 0:n_cols]))

            def row_stats(t, src):
                link(nc.vector.bn_stats(st[:, t, :], src))
                nc.vector.bn_aggr(mv[:, t, :], st[:, t, :]).then_inc(dve_link, 1)
                links[0] += 1

            def normalise():
                dve.wait_ge(dve_link, links[0])
                std(TT)
                for t in range(TT):
                    nc.vector.tensor_scalar(XN[:, t, :], X[:, t, :], mv[:, t, 0:1], rstd[:, t:t + 1],
                                            ALU.subtract, ALU.mult).then_inc(rows_normed, 1)

            def copy_out(dst, name, i, view=None):
                src = full(dve, name, i)
                src = src if view is None else view(src)
                nc.vector.tensor_copy(dst, src).then_inc(dve_evacuated, 1)

            two = lambda s: s.rearrange("p (t d) -> p t d", t=2)

            def xT(n):
                for j in (0, 2):
                    copy_out(XT[:, :, 2 * j * P:2 * (j + 1) * P], f"xT{n}", j, lambda s: s.rearrange("p (c n) -> p c n", c=FC))

            dve.wait_ge(idx_loaded, 16)
            nc.vector.tensor_copy(dst_f, idx_i[:, 0:P])
            nc.vector.tensor_copy(src_f, idx_i[:, P:2 * P])
            link(nc.vector.tensor_copy(drow_f, idx_i[:, 2 * P:3 * P]))
            nc.vector.tensor_reduce(cmin, drow_f, AX.X, ALU.min)
            nc.vector.tensor_reduce(cmax, drow_f, AX.X, ALU.max).then_inc(mm_bounds, 1)
            dve.wait_ge(x_loaded, 16)
            for t in range(TT):
                row_stats(t, X[:, t, :])
            normalise()
            src = full(dve, "bounds", 0)
            nc.vector.tensor_copy(brow, src[0:1, 0:2 * P]).then_inc(dve_evacuated, 1)
            dve.wait_ge(*evacuated("bounds", 0))
            dve.wait_ge(const_made, 5)
            nc.vector.tensor_reduce(glow, brow[:, 0:P].rearrange("p (g c) -> p g c", c=GC), AX.X, ALU.min)
            link(nc.vector.tensor_reduce(ghigh, brow[:, P:2 * P].rearrange("p (g c) -> p g c", c=GC), AX.X, ALU.max))
            nc.vector.tensor_tensor(relA, glow.unsqueeze(1).broadcast_to([1, TT, NG]), lo8, ALU.subtract)
            link(nc.vector.tensor_tensor(relB, ghigh.unsqueeze(1).broadcast_to([1, TT, NG]), lo8, ALU.subtract))
            link(nc.vector.tensor_scalar(relB, relB, 0.0, None, ALU.is_ge))
            link(nc.vector.scalar_tensor_tensor(relA, relA, float(P - 1), relB, ALU.is_le, ALU.mult))
            nc.vector.scalar_tensor_tensor(relB, c8, float(NG - 1), relA, ALU.subtract, ALU.mult)
            link(nc.vector.tensor_tensor(relA, c8, relA, ALU.mult))
            nc.vector.tensor_reduce(bnd[:, 0:8], relB, AX.X, ALU.min)
            link(nc.vector.tensor_reduce(bnd[:, 8:16], relA, AX.X, ALU.max))
            link(nc.vector.tensor_scalar(bnd[:, 0:8], bnd[:, 0:8], float(NG - 1), None, ALU.add))
            link(nc.vector.tensor_tensor(bnd[:, 8:16], bnd[:, 8:16], bnd[:, 0:8], ALU.max))
            link(nc.vector.tensor_scalar(bnd[:, 8:16], bnd[:, 8:16], 1.0, None, ALU.add))
            link(nc.vector.tensor_tensor(bnd[:, 16:24], bnd[:, 8:16], bnd[:, 0:8], ALU.subtract))
            link(nc.vector.memset(bnd[:, 24:25], float(SHIFT)))
            for t in range(1, TT):
                link(nc.vector.tensor_tensor(bnd[:, 24 + t:25 + t], bnd[:, 23 + t:24 + t], bnd[:, 15 + t:16 + t], ALU.add))
            link(nc.vector.tensor_tensor(bnd[:, 24:32], bnd[:, 24:32], bnd[:, 0:8], ALU.subtract))
            nc.vector.tensor_copy(bnd_i, bnd).then_inc(bounds_made, 1)
            xT(0)
            dve.wait_ge(bounds_made, 1)
            dve.sem_inc(onehot_ready, GC * SHIFT)
            for t in range(TT):
                first = dve.value_load(bnd_i[0:1, t:t + 1], min_val=0, max_val=NG - 1)
                end = dve.value_load(bnd_i[0:1, 8 + t:9 + t], min_val=0, max_val=NG)
                before = dve.value_load(bnd_i[0:1, 24 + t:25 + t], min_val=0, max_val=SHIFT + TT * NG)
                with dve.Fori(first, end) as g:
                    for b in range(GC):
                        dve.wait_ge(onehot_used, (g + before) * GC + b + 1)
                        nc.vector.tensor_scalar(dstrow[:, b, :], iota[:, t * P:(t + 1) * P],
                                                dst_f[:, bass.ds(g * GC + b, 1)], None, ALU.is_equal)
                        nc.vector.tensor_scalar(srcrow[:, b, :], iota, src_f[:, bass.ds(g * GC + b, 1)], None,
                                                ALU.is_equal).then_inc(onehot_ready, 1)
            for t in range(0, TT, 2):
                src = full(dve, "adjT", t)
                nc.vector.tensor_scalar(adj0[:, t, :], src, 1.0, None, ALU.min).then_inc(dve_evacuated, 1)
            dve.wait_ge(cols_loaded, 16)
            for name, dst in (("q0", QT0), ("k0", KT0)):
                for c in (0, 2):
                    src = full(dve, name, c)
                    nc.vector.tensor_scalar(dst[:, c, :], src, col("bq" if name == "q0" else "bk", c), None,
                                            ALU.add).then_inc(dve_evacuated, 1)
            for j in (0, 2):
                copy_out(V0[:, 2 * j:2 * j + 2, :], "v0", j, two)
            for n in range(TT + LAG + 1):
                if n < TT:
                    src = full(dve, "score0", n)
                    if n >= 2:
                        dve.wait_ge(psum_full, INDEX[("turn0", n - 2)] + 1)
                    else:
                        dve.wait_ge(*evacuated("adjT", 7))
                    nc.vector.scalar_tensor_tensor(SM[:, n % 2, :], src, float(D) ** -0.5, adj0[:, n, :],
                                                   ALU.mult, ALU.mult).then_inc(dve_evacuated, 1)
                    dve.wait_ge(*evacuated("score0", n))
                    dve.wait_ge(negm_made, n + 1)
                    nc.vector.tensor_tensor_reduce(out=SM[:, n % 2, :], in0=SM[:, n % 2, :], in1=negm[:, n % 2, :],
                                                   scale=-1.0, scalar=3e38, op0=ALU.add, op1=ALU.min,
                                                   accum_out=nm[:, n:n + 1]).then_inc(masked0, 1)
                i = n - LAG - 1
                if i >= 0:
                    dve.wait_ge(probs0, i + 1)
                    link(nc.vector.reciprocal(rl[:, i:i + 1], ls[:, 0, i:i + 1]))
                    dve.wait_ge(x_biased, TT)
                    src = full(dve, "attn0", i)
                    nc.vector.scalar_tensor_tensor(X[:, i, :], src[:, 0:D], rl[:, i:i + 1], X[:, i, :],
                                                   ALU.mult, ALU.add).then_inc(dve_evacuated, 1)
            dve.wait_ge(bd_cleared, 1)
            nc.vector.tensor_copy(b_bc, col("b_in").unsqueeze(2).broadcast_to([P, FC, P])).then_inc(mix_bias, 1)
            quarter = lambda s: s[:, 0:256].rearrange("p (c n) -> p c n", c=FC)
            copy_out(wqk, "wqk", 0, quarter)
            copy_out(bq_bc, "bq0", 0, lambda s: s[:, 0:32])
            copy_out(bk_col, "bk0", 0, lambda s: s[0:32, 0:1])
            src = full(dve, "klog", 0)
            dve.wait_ge(*evacuated("bk0", 0))
            dve.wait_ge(mask_made, TT)
            nc.vector.tensor_scalar(ekT, src[0:32, :], bk_col, None, ALU.add).then_inc(dve_evacuated, 1)
            dve.wait_ge(*evacuated("klog", 0))
            nc.vector.tensor_reduce(kmax, ekT, AX.X, ALU.max, negate=True).then_inc(mix_kexp, 1)
            src = full(dve, "qlog", 0)
            nc.vector.tensor_tensor(ql, src[:, 0:256].rearrange("p (t n) -> p t n", t=TT),
                                    bq_bc.unsqueeze(1).broadcast_to([P, TT, 32]), ALU.add).then_inc(dve_evacuated, 1)
            dve.wait_ge(*evacuated("qlog", 0))
            qlf = ql.rearrange("p t (h r) -> p (t h) r", r=R)
            link(nc.vector.tensor_reduce(qm, qlf, AX.X, ALU.max))
            nc.vector.tensor_tensor(qlf, qlf, qm.unsqueeze(2).broadcast_to([P, TT * H, R]), ALU.subtract).then_inc(mix_qs, 1)
            dve.wait_ge(mix_qe, 1)
            link(nc.vector.tensor_reduce(qr, qlf, AX.X, ALU.add))
            link(nc.vector.reciprocal(qr, qr))
            nc.vector.tensor_tensor(qlf, qlf, qr.unsqueeze(2).broadcast_to([P, TT * H, R]), ALU.mult).then_inc(mix_kscaled, 1)
            dve.wait_ge(mix_krdy, 1)
            link(nc.vector.reciprocal(krec, ksum))
            copy_out(ek, "ekt", 0, lambda s: s[:, 0:256].rearrange("p (t n) -> p t n", t=TT))
            src = full(dve, "kx", 0)
            nc.vector.tensor_scalar(kx, src[0:32, 0:D], krec, None, ALU.mult).then_inc(dve_evacuated, 1)
            four32 = lambda s: s[:, 0:128].rearrange("p (c n) -> p c n", c=FC)
            copy_out(kxT, "kxT", 0, four32)
            src = four32(full(dve, "xmT", 0))
            link(nc.vector.tensor_tensor(xmT, src, col("b_in").unsqueeze(2).broadcast_to([P, FC, 32]), ALU.add))
            nc.vector.tensor_tensor(xmT, xmT, hm, ALU.mult).then_inc(dve_evacuated, 1)
            copy_out(kvT, "kvT", 0, four32)
            copy_out(mixM, "mixM", 0, lambda s: s[0:32, 0:D])
            copy_out(qsT, "qsT", 0, lambda s: s[0:32, :])
            w_ready(dve, "ffn")
            wfl = W[:, WEIGHTS.index("ffn") % WSLOTS, :]
            nc.vector.tensor_reduce(tiny[:, 0:1], wfl, AX.X, ALU.add)
            nc.vector.tensor_reduce(tiny[:, 1:2], wfl, AX.X, ALU.add, apply_absolute_value=True).then_inc(wstat, 1)
            src = full(dve, "wsum", 0)
            nc.vector.tensor_scalar(tiny[:, 2:3], src[:, 0:1], -1.0 / (D * D), None, ALU.mult).then_inc(wmean, 1)
            nc.vector.tensor_scalar(tiny[:, 3:4], src[:, 1:2], 1.0 / (D * D), None, ALU.mult).then_inc(dve_evacuated, 1)
            for j in range(4):
                src = two(full(dve, "mixout", j))
                nc.vector.tensor_tensor(X[:, 2 * j:2 * j + 2, :], src, X[:, 2 * j:2 * j + 2, :], ALU.add).then_inc(dve_evacuated, 1)
                dve.wait_ge(*evacuated("mixout", j))
                for t in (2 * j, 2 * j + 1):
                    row_stats(t, X[:, t, :])
            dve.wait_ge(psum_full, INDEX[("kx", 0)] + 1)
            normalise()
            xT(1)
            row_ready(dve, "L0_ffn_bias")
            fb = row("L0_ffn_bias").unsqueeze(1).broadcast_to([P, 2, D])
            dve.wait_ge(psum_full, INDEX[("turn0", 7)] + 1)
            for j in range(4):
                y = two(SM[:, j % 2, :])
                xs = X[:, 2 * j:2 * j + 2, :]
                src = two(full(dve, "ffn", j))
                dve.wait_ge(*evacuated("wsum", 0))
                nc.vector.scalar_tensor_tensor(y, src, tiny[:, 3:4], fb, ALU.mult, ALU.add).then_inc(dve_evacuated, 1)
                dve.wait_ge(*evacuated("ffn", j))
                link(nc.vector.tensor_scalar(y, y, -1.0, 1.0, ALU.max, ALU.min))
                link(nc.vector.tensor_scalar(y, y, 7.0, MAGIC, ALU.mult, ALU.add))
                link(nc.vector.tensor_scalar(y, y, MAGIC, 1.0 / 7.0, ALU.subtract, ALU.mult))
                link(nc.vector.tensor_tensor(xs, xs, y, ALU.add))
                for t in (2 * j, 2 * j + 1):
                    row_stats(t, X[:, t, :])
            normalise()
            xT(2)

            def elu1(dst, name, j, n):
                src = full(dve, name, j)
                nc.vector.tensor_scalar(SM[:, n % 2, :], src, 0.0, None, ALU.min).then_inc(kneg, 1)
                dve.wait_ge(kexp, n + 1)
                nc.vector.scalar_tensor_tensor(dst, src, 0.0, SM[:, n % 2, :], ALU.max, ALU.add).then_inc(dve_evacuated, 1)

            for j in range(4):
                elu1(K1[:, 2 * j:2 * j + 2, :].rearrange("p t d -> p (t d)"), "k1", j, j)
            dve.wait_ge(blk_made, 1)
            src = full(dve, "kv1", 0)
            blk4 = blk.unsqueeze(1).broadcast_to([P, FC, P])
            nc.vector.tensor_tensor(kvT1, src[:, 0:D].rearrange("p (c n) -> p c n", c=FC), blk4, ALU.mult)
            hm8 = hm.rearrange("p c (h r) -> p c h r", r=R)[:, :, :, 0]
            nc.vector.tensor_tensor(KS1, src[:, D:D + 32].rearrange("p (c h) -> p c h", c=FC), hm8, ALU.mult).then_inc(dve_evacuated, 1)
            for j in range(4):
                elu1(QT1[:, j, :], "q1", j, 4 + j)
            copy_out(M1[:, 0:2, :], "mixM1", 0, two)
            src = full(dve, "den", 0)
            link(nc.vector.tensor_scalar(zT[0:8, :], src[0:8, :], 1e-6, None, ALU.add))
            nc.vector.reciprocal(zT[0:8, :], zT[0:8, :]).then_inc(dve_evacuated, 1)
            for j in (0, 2):
                copy_out(GV[:, 2 * j:2 * j + 2, :], "gv0", j, two)
            for j in range(4):
                src = full(dve, "zb", j)
                nc.vector.tensor_tensor(QT1[:, j, :], QT1[:, j, :], src, ALU.mult).then_inc(dve_evacuated, 1)
            dve.wait_ge(x1_biased, TT)
            for j in range(4):
                src = two(full(dve, "mixout1", j))
                nc.vector.tensor_tensor(X[:, 2 * j:2 * j + 2, :], src, X[:, 2 * j:2 * j + 2, :], ALU.add).then_inc(dve_evacuated, 1)

            def add_branch(name, bias):
                for c in range(FC):
                    src = full(dve, name, c)
                    nc.vector.scalar_tensor_tensor(XT[:, c, :], src, col(bias, c), XT[:, c, :],
                                                   ALU.add, ALU.add).then_inc(dve_evacuated, 1)
                    done(dve, name, c)
                    nc.vector.bn_stats(st[:, 2 * c, :], XT[:, c, 0:D])
                    link(nc.vector.bn_stats(st[:, 2 * c + 1, :], XT[:, c, D:N]))
                    nc.vector.bn_aggr(mv[:, c, :], st[:, 2 * c:2 * c + 2, :]).then_inc(dve_link, 1)
                    links[0] += 1
                dve.wait_ge(dve_link, links[0])

            def batchnorm(g, be):
                std(FC)
                link(nc.vector.tensor_tensor(bns[:, 0:4], rstd[:, 0:FC], col(g), ALU.mult))
                link(nc.vector.tensor_tensor(bns[:, 4:8], mv[:, 0:FC, 0], bns[:, 0:4], ALU.mult))
                nc.vector.tensor_tensor(bns[:, 4:8], col(be), bns[:, 4:8], ALU.subtract).then_inc(bn_ready, 1)
                bn_rounds[0] += 1
                dve.wait_ge(bn_ready, bn_rounds[0])
                for c in range(FC - 1):
                    nc.vector.tensor_scalar(XT[:, c, :], XT[:, c, :], bns[:, c:c + 1], bns[:, 4 + c:5 + c],
                                            ALU.mult, ALU.add).then_inc(state_ready, 1)

            bn_rounds = [0]
            for l in range(L):
                if l:
                    for j in (0, 2):
                        copy_out(GV[:, 2 * j:2 * j + 2, :], f"gv{l}", j, two)
                dve.wait_ge(q_cleared, 2)
                for step, n in attention_order():
                    if step == "q":
                        if n >= 2:
                            dve.wait_ge(psum_full, INDEX[(f"score{l}g", 16 * n - 17)] + 1)
                        src = full(dve, f"q{l}g", n)
                        nc.vector.tensor_scalar(QZ[0:DH, n % 2, 0, :], src[0:DH, :], col(f"gbq{l}", n)[0:DH], DH ** -0.5,
                                                ALU.add, ALU.mult)
                        nc.vector.tensor_scalar(QZ[DH:P, n % 2, 1, :], src[DH:P, :], col(f"gbq{l}", n)[DH:P], DH ** -0.5,
                                                ALU.add, ALU.mult).then_inc(dve_evacuated, 1)
                    elif step == "score":
                        src = full(dve, f"score{l}g", n)
                        if n >= 2:
                            dve.wait_ge(psum_full, INDEX[(f"turn{l}g", n - 2)] + 1)
                        nc.vector.tensor_tensor_reduce(out=SM[:, n % 2, :], in0=src, in1=MASK[:, n % 4 + 4 * (n // 8 % 2), :],
                                                       scale=-1.0, scalar=-0.1 * NO_EDGE, op0=ALU.add, op1=ALU.min,
                                                       accum_out=nm[:, n % 8:n % 8 + 1]).then_inc(dve_evacuated, 1)
                    elif step == "turn":
                        if n % 2 == 0:
                            g, i = n // 4, n % 4
                            if g >= 3:
                                dve.wait_ge(psum_full, INDEX[(f"agg{l}g", (g - 3) // 2)] + 1)
                            copy_out(PTr[:, g % 3, :, i * P:(i + 1) * P], f"turn{l}g", n,
                                     lambda s: s.rearrange("p (s n) -> p s n", s=TT))
                        if n % 8 == 7:
                            b = n // 8
                            dve.wait_ge(probs, UNITS * l + n + 1)
                            if b >= 1:
                                dve.wait_ge(psum_full, INDEX[(f"rsum{l}g", b - 1)] + 1)
                            link(nc.vector.tensor_scalar(rl[:], ls[:, b % 2, :], 1e-16, None, ALU.add))
                            nc.vector.reciprocal(rl[:], rl[:]).then_inc(recips, 1)
                    elif step == "rsum":
                        src = full(dve, f"rsum{l}g", n)
                        if n >= 1:
                            dve.wait_ge(psum_full, INDEX[(f"rsum_bc{l}g", n - 1)] + 1)
                        nc.vector.tensor_copy(rT, src[0:8, 0:P]).then_inc(dve_evacuated, 1)
                    elif step == "agg":
                        src = full(dve, f"agg{l}g", n)
                        done(dve, f"rsum_bc{l}g", n)
                        nc.vector.tensor_tensor(AG[:, n // 2, (n % 2) * D:(n % 2 + 1) * D], src[:, 0:D], rbc,
                                                ALU.mult).then_inc(dve_evacuated, 1)
                add_branch(f"wo{l}", f"gbo{l}")
                batchnorm(f"g1{l}", f"be1{l}")
                dve.wait_ge(last_chunk_ready, 2 * l + 1)
                add_branch(f"f{l}", f"gb2{l}")
                batchnorm(f"g2{l}", f"be2{l}")

            for j in range(4):
                src = two(full(dve, "gT", j))
                for t in (2 * j, 2 * j + 1):
                    row_stats(t, src[:, t % 2, :])
            dve.wait_ge(dve_link, links[0])
            std(TT)
            row_ready(dve, "L1_gnn_ln_g")
            dve.wait_ge(shift_added, TT)
            for j in range(4):
                src = two(slot_of("gT", j))
                for t in (2 * j, 2 * j + 1):
                    tmp = SM[:, t % 2, 0:D]
                    last = nc.vector.scalar_tensor_tensor(tmp, src[:, t % 2, :], mv[:, t, 0:1], row("L1_gnn_ln_g"),
                                                          ALU.subtract, ALU.mult)
                    if t % 2 == 0:
                        link(last)
                    else:
                        last.then_inc(dve_evacuated, 1)
                        dve.wait_ge(*evacuated("gT", j))
                    link(nc.vector.scalar_tensor_tensor(X[:, t, :], tmp, rstd[:, t:t + 1], X[:, t, :], ALU.mult, ALU.add))
            for t in range(TT):
                row_stats(t, X[:, t, :])
            normalise()
            dve.wait_ge(rows_normed, 4 * TT)
            dve.wait_ge(i16_made, 2)
            dve.wait_ge(hid_cleared, 1)
            nc.vector.tensor_scalar(flags[:, :, 0:1], XN[:, :, 0:1], 0.5, None, ALU.is_ge)
            nc.vector.tensor_scalar(flags[:, :, 1:4], XN[:, :, 1:4], 0.5, None, ALU.is_gt)
            link(nc.vector.tensor_scalar(bits, XN[:, :, 16:80].rearrange("p t (j n) -> p t j n", j=4), 0.5, None, ALU.is_gt))
            bf = bits.rearrange("p t j n -> p (t j) n")
            link(nc.vector.tensor_tensor(bf, bf, i16m.unsqueeze(1).broadcast_to([P, TT * 4, 16]), ALU.mult))
            mf = m16.rearrange("p t j -> p (t j)")
            link(nc.vector.tensor_reduce(mf, bf, AX.X, ALU.min))
            b0 = bits[:, :, 0, 0:4]
            link(nc.vector.tensor_scalar(b0, m16, 0.0, None, ALU.is_lt))
            nc.vector.scalar_tensor_tensor(Fx[:, :, :, 0], m16[:, :, 0:2], 16.0, b0[:, :, 0:2], ALU.add, ALU.mult)
            nc.vector.scalar_tensor_tensor(Fx[:, :, :, 1], m16[:, :, 2:4], 16.0, b0[:, :, 2:4], ALU.add, ALU.mult)
            for r in range(2):
                nc.vector.tensor_copy(Fx[:, :, r, 2:4], XN[:, :, 2:4])
                last = nc.vector.tensor_copy(Fx[:, :, r, 4:5], XN[:, :, 1:2])
            last.then_inc(hid_ready, 1)
            for q in range(4):
                src = full(dve, "fT", q)
                nc.vector.tensor_copy(FT[0:6, q * D:(q + 1) * D], src[0:6, 0:D]).then_inc(dve_evacuated, 1)
            dve.wait_ge(nib_loaded, 16 * 13)
            for n in range(16):
                t, r = n // 2, n % 2
                src = full(dve, "hid", n)
                nc.vector.scalar_tensor_tensor(hidb[n % 2], src[:, 0:3 * GE], 0.0, w2bc, ALU.max, ALU.mult).then_inc(dve_evacuated, 1)
                dve.wait_ge(*evacuated("hid", n))
                last = nc.vector.tensor_reduce(yk[:, t, r, :], hidb[n % 2].rearrange("p (k e) -> p k e", k=3), AX.X, ALU.add)
            link(last)
            ykf = yk.rearrange("p t r k -> p (t r) k")
            link(nc.vector.tensor_tensor(ykf, ykf, b2bc.unsqueeze(1).broadcast_to([P, 2 * TT, 3]), ALU.add))
            nc.vector.tensor_copy(pick[:, :, 0:1], flags[:, :, 1:2])
            nc.vector.scalar_tensor_tensor(pick[:, :, 1:2], flags[:, :, 1:2], 0.5, flags[:, :, 2:3], ALU.is_lt, ALU.mult)
            link(nc.vector.tensor_tensor(pick[:, :, 2:3], flags[:, :, 1:2], flags[:, :, 2:3], ALU.max))
            nc.vector.tensor_tensor(act_on.unsqueeze(2), pick[:, :, 2:3], flags[:, :, 3:4], ALU.max)
            link(nc.vector.tensor_scalar(pick[:, :, 2:3], pick[:, :, 2:3], 0.5, None, ALU.is_lt))
            link(nc.vector.tensor_tensor(act_on.unsqueeze(2), act_on.unsqueeze(2), flags[:, :, 0:1], ALU.mult))
            for r in range(2):
                last = nc.vector.tensor_tensor(ysel[:, :, r, :], yk[:, :, r, :], pick, ALU.mult)
            link(last)
            resf = res.rearrange("p t r -> p (t r)")
            link(nc.vector.tensor_reduce(resf, ysel.rearrange("p t r k -> p (t r) k"), AX.X, ALU.add))
            link(nc.vector.tensor_scalar(resf, resf, 0.0, 15.0, ALU.max, ALU.min))
            link(nc.vector.tensor_scalar(resf, resf, MAGIC, MAGIC, ALU.add, ALU.subtract))
            onef = oneh.rearrange("p t r n -> p (t r) n")
            link(nc.vector.tensor_tensor(onef, resf.unsqueeze(2).broadcast_to([P, 2 * TT, 16]),
                                         i16.unsqueeze(1).broadcast_to([P, 2 * TT, 16]), ALU.is_equal))
            onet = oneh.rearrange("p t r n -> p t (r n)")
            link(nc.vector.scalar_tensor_tensor(onet, onet, 2.0, act_on.unsqueeze(2).broadcast_to([P, TT, 32]),
                                                ALU.mult, ALU.mult))
            dve.wait_ge(out_summed, TT)
            nc.vector.tensor_tensor(X[:, :, 80:112], X[:, :, 80:112], onet, ALU.add).then_inc(nibbles_added, 1)

        @block.tensor
        def _(pe):
            waited = {}

            def wait(s, v):
                if waited.get(id(s), 0) < v:
                    pe.wait_ge(s, v)
                    waited[id(s)] = v

            def begin(name, i):
                j = INDEX[(name, i)]
                if j >= 4:
                    wait(*evacuated(*JOBS[j - 4][0]))
                return slot_of(name, i)

            def need(name, *idx):
                for i in idx:
                    wait(*evacuated(name, i))

            def mm(o_, lhsT, rhs, start, stop):
                return nc.tensor.matmul(o_, lhsT, rhs, start=start, stop=stop)

            def end(ins):
                ins.then_inc(psum_full, 1)

            def halves(slot, lhsT_of, rhs_of, n_k):
                for hf in range(2):
                    for k in range(n_k):
                        last = mm(slot[:, hf * D:(hf + 1) * D], lhsT_of(k), rhs_of(k)[:, hf * D:(hf + 1) * D], k == 0, k == n_k - 1)
                return last

            def feature_major(name, w, src, count=FC, n_k=FC, first=0):
                for c in range(first, first + count):
                    slot = begin(name, c)
                    end(halves(slot, lambda k: w[:, k, c * P:(c + 1) * P], lambda k: src[:, k, :], n_k))

            def token_major(name, w, src):
                for j in range(4):
                    slot = begin(name, j)
                    for hf in range(2):
                        t = 2 * j + hf
                        for k in range(FC):
                            last = mm(slot[:, hf * D:(hf + 1) * D], src[:, k, t * P:(t + 1) * P], w[:, k, :], k == 0, k == FC - 1)
                    end(last)

            def turn(slot_part, src):
                rows, n = src.shape[0], src.shape[1]
                return nc.tensor.transpose(slot_part, src, ident[0:rows, 0:rows])

            def xT(n):
                for j in range(4):
                    slot = begin(f"xT{n}", j)
                    pe.wait_ge(rows_normed, TT * n + 2 * j + 2)
                    for c in range(FC):
                        for t in (2 * j, 2 * j + 1):
                            at = (2 * c + t % 2) * P
                            last = turn(slot[:, at:at + P], XN[:, t, c * P:(c + 1) * P])
                    end(last)

            pe.wait_ge(const_made, 7)
            pe.wait_ge(mm_bounds, 1)
            slot = begin("bounds", 0)
            mm(slot[0:1, 0:P], cmin, ident[:], True, True)
            end(mm(slot[0:1, P:2 * P], cmax, ident[:], True, True))
            xT(0)
            pe.sem_inc(onehot_used, GC * SHIFT + GC)
            pe.wait_ge(bounds_made, 1)
            for t in range(TT):
                slot = begin("counts", t)
                first = pe.value_load(bnd_i[0:1, t:t + 1], min_val=0, max_val=NG - 1)
                end_ = pe.value_load(bnd_i[0:1, 8 + t:9 + t], min_val=0, max_val=NG)
                before = pe.value_load(bnd_i[0:1, 24 + t:25 + t], min_val=0, max_val=SHIFT + TT * NG)
                for hf in range(2):
                    mm(slot[:, hf * D:(hf + 1) * D], zeros[:, 0:P], zeros, True, False)
                with pe.Fori(first, end_) as g:
                    for b in range(GC):
                        pe.wait_ge(onehot_ready, (g + before) * GC + b + 1)
                        mm(slot[:, 0:D], dstrow[:, b, :], srcrow[:, b, 0:D], False, False)
                        mm(slot[:, D:N], dstrow[:, b, :], srcrow[:, b, D:N], False, False).then_inc(onehot_used, 1)
                for hf in range(2):
                    last = mm(slot[:, hf * D:(hf + 1) * D], zeros[:, 0:P], zeros, False, True)
                end(last)
            need("counts", *range(TT))
            for t in range(TT):
                slot = begin("adjT", t)
                for s in range(TT):
                    last = turn(slot[:, s * P:(s + 1) * P], MASK[:, s, t * P:(t + 1) * P])
                end(last)
            need("xT0", *range(FC))
            for name, order in (("q0", feature_major), ("k0", feature_major), ("v0", token_major)):
                w_ready(pe, name)
                order(name, wtile(name), XT)
            need("q0", 2, 3)
            need("k0", 2, 3)
            for n in range(TT + LAG + 1):
                if n < TT:
                    slot = begin("score0", n)
                    end(halves(slot, lambda k: QT0[:, k, n * P:(n + 1) * P], lambda k: KT0[:, k, :], FC))
                i = n - LAG
                if 0 <= i < TT:
                    slot = begin("turn0", i)
                    pe.wait_ge(probs0, i + 1)
                    for s in range(TT):
                        last = turn(slot[:, s * P:(s + 1) * P], SM[:, i % 2, s * P:(s + 1) * P])
                    end(last)
                i = n - LAG - 1
                if i >= 0:
                    slot = begin("attn0", i)
                    need("v0", 2, 3)
                    need("turn0", i)
                    for s in range(TT):
                        last = mm(slot[:, 0:D], P0T[:, i % 2, s, :], V0[:, s, :], s == 0, s == TT - 1)
                    end(last)
            w_ready(pe, "winT")
            pe.wait_ge(bd_loaded, 16 * 18)
            wt = wtile("winT")
            slot = begin("wqk", 0)
            for c in range(FC):
                for k in range(FC):
                    last = mm(slot[:, 64 * c:64 * c + 64], wt[:, k, c * P:(c + 1) * P], bdqk[:, k, :], k == 0, k == FC - 1)
            end(last)
            pe.wait_ge(mix_bias, 1)
            slot = begin("bq0", 0)
            for k in range(FC):
                last = mm(slot[:, 0:32], b_bc[:, k, :], bdqk[:, k, 0:32], k == 0, k == FC - 1)
            end(last)
            slot = begin("bk0", 0)
            for k in range(FC):
                last = mm(slot[0:32, 0:1], bdqk[:, k, 32:64], col("b_in", k), k == 0, k == FC - 1)
            end(last)
            need("wqk", 0)
            slot = begin("klog", 0)
            end(halves(slot[0:32, :], lambda k: wqk[:, k, 32:64], lambda k: XT[:, k, :], FC))
            slot = begin("qlog", 0)
            for t in range(TT):
                for k in range(FC):
                    last = mm(slot[:, 32 * t:32 * t + 32], XT[:, k, t * P:(t + 1) * P], wqk[:, k, 0:32], k == 0, k == FC - 1)
            end(last)
            slot = begin("ekt", 0)
            pe.wait_ge(mix_krdy, 1)
            for t in range(TT):
                last = turn(slot[:, 32 * t:32 * t + 32], ekT[:, t * P:(t + 1) * P])
            end(last)
            slot = begin("kx", 0)
            need("ekt", 0)
            for t in range(TT):
                last = mm(slot[0:32, 0:D], ek[:, t, :], XN[:, t, :], t == 0, t == TT - 1)
            end(last)
            slot = begin("kxT", 0)
            need("kx", 0)
            for c in range(FC):
                last = turn(slot[:, 32 * c:32 * c + 32], kx[:, c * P:(c + 1) * P])
            end(last)
            slot = begin("xmT", 0)
            need("kxT", 0)
            w_ready(pe, "win")
            wi = wtile("win")
            for c in range(FC):
                for k in range(FC):
                    last = mm(slot[:, 32 * c:32 * c + 32], wi[:, k, c * P:(c + 1) * P], kxT[:, k, :], k == 0, k == FC - 1)
            end(last)
            slot = begin("kvT", 0)
            need("xmT", 0)
            for c in range(FC):
                last = mm(slot[:, 32 * c:32 * c + 32], bdv, xmT[:, c, :], True, True)
            end(last)
            slot = begin("mixM", 0)
            need("kvT", 0)
            w_ready(pe, "wout")
            for c in range(FC):
                last = mm(slot[0:32, 0:D], kvT[:, c, :], wtile("wout")[:, c, :], c == 0, c == FC - 1)
            end(last)
            slot = begin("qsT", 0)
            pe.wait_ge(mix_kscaled, 1)
            for t in range(TT):
                last = turn(slot[0:32, t * P:(t + 1) * P], ql[:, t, :])
            end(last)
            slot = begin("wsum", 0)
            pe.wait_ge(wstat, 1)
            end(mm(slot[:, 0:2], ones[:], tiny[:, 0:2], True, True))
            for j in range(4):
                slot = begin("mixout", j)
                need("mixM", 0)
                need("qsT", 0)
                for hf in range(2):
                    t = 2 * j + hf
                    last = mm(slot[:, hf * D:(hf + 1) * D], qsT[:, t * P:(t + 1) * P], mixM, True, True)
                end(last)
            xT(1)
            need("xT1", 2, 3)
            pe.wait_ge(wsign, 1)
            token_major("ffn", wtile("ffn"), XT)
            xT(2)
            need("xT2", 2, 3)
            for name in ("k1", "v1"):
                w_ready(pe, name)
                token_major(name, wtile(name), XT)
            pe.wait_ge(blk_made, 1)
            need("k1", 3)
            need("v1", 3)
            slot = begin("kv1", 0)
            for c in range(FC):
                cs = slice(c * P, (c + 1) * P)
                for t in range(TT):
                    mm(slot[:, cs], V1[:, t, cs], K1[:, t, cs], t == 0, t == TT - 1)
                for t in range(TT):
                    last = mm(slot[:, D + 8 * c:D + 8 * (c + 1)], K1[:, t, cs], ones[:, 0:8], t == 0, t == TT - 1)
            end(last)
            w_ready(pe, "q1")
            feature_major("q1", wtile("q1"), XT)
            w_ready(pe, "wout1")
            need("kv1", 0)
            for j in range(2):
                slot = begin("mixM1", j)
                for hf in range(2):
                    c = 2 * j + hf
                    last = mm(slot[:, hf * D:(hf + 1) * D], kvT1[:, c, :], wtile("wout1")[:, c, :], True, True)
                end(last)
            slot = begin("den", 0)
            need("q1", *range(FC))
            end(halves(slot[0:8, :], lambda k: KS1[:, k, :], lambda k: QT1[:, k, :], FC))
            w_ready(pe, "gv0")
            token_major("gv0", wtile("gv0"), XT)
            need("den", 0)
            for c in range(FC):
                slot = begin("zb", c)
                end(halves(slot, lambda k: selh[:, c, :], lambda k: zT, 1))
            need("zb", 3)
            need("mixM1", 0, 1)
            token_major("mixout1", M1, QT1)
            def state(n):
                pe.wait_ge(state_ready, 3 * n)
                pe.wait_ge(last_chunk_ready, n)

            for l in range(L):
                if l:
                    state(2 * l)
                    w_ready(pe, f"gv{l}")
                    token_major(f"gv{l}", wtile(f"gv{l}"), XT)
                w_ready(pe, f"gq{l}")
                w_ready(pe, f"gk{l}")
                for step, n in attention_order():
                    slot = begin(f"{step}{l}g", n)
                    if step in "qk":
                        w = wtile(f"g{step}{l}")
                        end(halves(slot, lambda k: w[:, k, n * P:(n + 1) * P], lambda k: XT[:, k, :], FC))
                    elif step == "score":
                        pair, hf, e, i = n // 16, n // 8 % 2, n // 4 % 2, n % 4
                        need(f"q{l}g", pair)
                        need(f"k{l}g", pair)
                        t = 4 * hf + i
                        end(halves(slot, lambda k: QZ[:, pair % 2, e, t * P:(t + 1) * P], lambda k: KR[:, pair % 2, :], 1))
                    elif step == "turn":
                        wait(probs, UNITS * l + n + 1)
                        for s in range(TT):
                            last = turn(slot[:, s * P:(s + 1) * P], SM[:, n % 2, s * P:(s + 1) * P])
                        end(last)
                    elif step == "rsum":
                        wait(recips, 8 * l + n + 1)
                        end(turn(slot[0:8, 0:P], rl[:]))
                    elif step == "rsum_bc":
                        need(f"rsum{l}g", n)
                        for i in range(4):
                            last = mm(slot[:, i * P:(i + 1) * P], sel[:, i, :], rT, True, True)
                        end(last)
                    elif step == "agg":
                        need(f"gv{l}", 2, 3)
                        need(f"turn{l}g", 8 * n + 6, 8 * n + 7)
                        for s in range(TT):
                            for e in range(2):
                                g = 2 * n + e
                                head = 2 * (n // 2) + e
                                last = mm(slot[e * DH:(e + 1) * DH, 0:D], GV[:, s, head * DH:(head + 1) * DH],
                                          PTr[:, g % 3, s, :], s == 0, s == TT - 1)
                        end(last)
                need(f"agg{l}g", 7)
                w_ready(pe, f"go{l}")
                feature_major(f"wo{l}", wtile(f"go{l}"), AG)
                w_ready(pe, f"w12{l}")
                ws = W[:, WEIGHTS.index(f"w12{l}") % WSLOTS, :]
                state(2 * l + 1)
                feature_major(f"h{l}", ws[:, 0:1024].rearrange("p (k n) -> p k n", k=FC), XT, count=2)
                need(f"h{l}", 0, 1)
                feature_major(f"f{l}", ws[:, 1024:2048].rearrange("p (k n) -> p k n", k=2), KR, n_k=2)
            state(2 * L)
            for j in range(4):
                slot = begin("gT", j)
                for hf in range(2):
                    for c in range(FC):
                        t = 2 * j + hf
                        last = turn(slot[:, hf * D + c * P:hf * D + (c + 1) * P], XT[:, c, t * P:(t + 1) * P])
                end(last)
            pe.wait_ge(hid_ready, 1)
            for q in range(4):
                slot = begin("fT", q)
                for s in range(4):
                    n = 4 * q + s
                    last = turn(slot[0:6, s * P:(s + 1) * P], Fx[:, n // 2, n % 2, 0:6])
                end(last)
            pe.wait_ge(nib_loaded, 16 * 13)
            need("fT", 3)
            for n in range(16):
                slot = begin("hid", n)
                end(mm(slot[:, 0:3 * GE], FT[:, n * P:(n + 1) * P], W1s, True, True))


def kernel(**inputs):
    import concourse.bacc as bacc
    from concourse.bass_utils import run_bass_kernel_spmd

    g = {k: np.asarray(v) for k, v in inputs.items()}

    def chunks(v):
        return v.reshape(-1, P).T

    src, dst = g["src"].reshape(EC, P), g["dst"].reshape(EC, P)
    vec = {"bq": g["L0_gnn_bq"], "bk": g["L0_gnn_bk"], "b_in": g["L0_mix_b_in"]}
    names = {"gbq": "bq", "gbo": "bo", "gb2": "b2", "g1": "g1", "be1": "beta1", "g2": "g2", "be2": "beta2", "gb1": "b1"}
    for l in range(L):
        vec.update({f"{k}{l}": g[f"L1_gnn_{v}"][l] for k, v in names.items()})
    wqkv = g["L1_mix_Wqkv"]
    nets = ("and", "or", "xor")
    arrays = {
        "idx": np.concatenate([dst.T, src.T, dst], axis=1),
        "x": g["x"],
        "cols": np.concatenate([chunks(vec[n]) for n in COLS], axis=1),
        "rows": np.stack([g[n] for n in ROWS]),
        "q0": g["L0_gnn_Wq"], "k0": g["L0_gnn_Wk"], "v0": g["L0_gnn_Wv"],
        "winT": g["L0_mix_W_in"].T, "win": g["L0_mix_W_in"], "wout": g["L0_mix_W_out"],
        "mq": g["L0_mix_W_q"], "mk": g["L0_mix_W_k"], "mv": g["L0_mix_W_v"],
        "ffn": g["L0_ffn_weight"],
        "q1": wqkv[:, 0:D], "k1": wqkv[:, D:2 * D], "v1": wqkv[:, 2 * D:3 * D], "wout1": g["L1_mix_Wout"],
        "nw1": np.stack([g[f"L1_ffn_{k}_w1"] for k in nets]),
        "nb1": np.stack([g[f"L1_ffn_{k}_b1"] for k in nets]),
        "nw2": np.stack([g[f"L1_ffn_{k}_w2"][:, 64] for k in nets]),
        "nb2": np.stack([g[f"L1_ffn_{k}_b2"][64:65] for k in nets], axis=1),
    }
    for l in range(L):
        for k in "qkvo":
            arrays[f"g{k}{l}"] = g[f"L1_gnn_W{k}"][l].T
    fold = lambda w: w.reshape(-1, P, w.shape[1]).transpose(1, 0, 2).reshape(P, -1)
    arrays["w12"] = np.stack([np.concatenate([fold(g["L1_gnn_W1"][l].T), fold(g["L1_gnn_W2"][l].T)], axis=1)
                              for l in range(L)])

    nc = bacc.Bacc("TRN2", target_bir_lowering=False, num_devices=1)
    feed, aps = {}, {}
    for name, v in arrays.items():
        v = np.ascontiguousarray(v)
        feed[f"in_{name}"] = v
        aps[name] = nc.dram_tensor(f"in_{name}", v.shape, mybir.dt.from_np(v.dtype), kind="ExternalInput").ap()
    out = nc.dram_tensor("out_0", (N, D), mybir.dt.float32, kind="ExternalOutput").ap()
    build(nc, aps, out)
    r = run_bass_kernel_spmd(nc, [feed], core_ids=[0])
    return r.results[0]["out_0"]
```

```python
import numpy as np
import concourse.bass as bass
from concourse import mybir
from contextlib import ExitStack

N = 1024
D = 512
E = 16384
P = 128
TT = N // P
FC = D // P
EC = E // P
H = 8
DH = D // H
R = 4
L = 2
F2 = 256
GE = 160
HG = 4
GU = 3 * GE // HG
EPS = 1e-5
NO_EDGE = -1e30
NEG = -1e6
MAGIC = 1.5 * 2.0 ** 23
GC = 4
NG = EC // GC
SHIFT = NG

UNITS = H * TT
LAG = 3
LAG0 = 2
SMB = 4


def unit(n):
    return n // 16, n // 2 % 2, n % 16 // 4 * 2 + n % 2


def attention_order():
    order = [("q", 0), ("q", 1), ("k", 0)]
    for n in range(UNITS + LAG + 3):
        m = n - LAG
        if n < UNITS:
            order.append(("score", n))
            if n % 8 == 5 and 8 <= n < UNITS - 8:
                order.append(("q", n // 8 + 1))
            if n % 16 == 10 and n < UNITS - 16:
                order.append(("k", n // 16 + 1))
        if m >= 5 and m % 4 == 1:
            order.append(("agg", m // 4 - 1))
        if m >= 17 and m % 16 == 2:
            order.append(("rsum_bc", m // 16 - 1))
        if 0 <= m < UNITS:
            order.append(("turn", m))
        if m >= 4 and m % 4 == 0:
            order.append(("agg_start", m // 4 - 1))
        if m >= 17 and m % 16 == 1:
            order.append(("rsum", m // 16 - 1))
    return order


MIXER0_ORDER = [("wqk", 0), ("bq0", 0), ("bk0", 0)] + [("adjT", t) for t in range(4)] + [
    ("klog", 0)] + [("adjT", t) for t in range(4, TT)] + [
    ("qlog", 0), ("v0", 0), ("v0", 1), ("ekt", 0), ("v0", 2), ("kx", 0), ("qsT", 0), ("v0", 3), ("kxT", 0),
    ("k0", 0), ("xmT", 0), ("k0", 1), ("kvT", 0), ("k0", 2), ("mixM", 0), ("k0", 3),
    ("mixout", 0), ("mixout", 1), ("mixout", 2), ("mixout", 3), ("q0", 0), ("q0", 1), ("q0", 2), ("q0", 3)]


def job_table():
    jobs = []

    def add(name, count, engines):
        for i in range(count):
            jobs.append(((name, i), engines[i % len(engines)]))

    A, V = "act", "dve"
    add("bounds", 1, [V])
    add("xT0", FC, [V, A])
    add("counts", TT, [A])
    engine = {"v0": (V, A), "k0": (V, A), "q0": (V, A), "adjT": (V, A)}
    for name, i in MIXER0_ORDER:
        jobs.append(((name, i), engine[name][i % 2] if name in engine else V))
    for n in range(TT + LAG0 + 1):
        if n == 7:
            add("wsum", 1, [V])
        if n < TT:
            jobs.append((("score0", n), V))
        if 0 <= n - LAG0 < TT:
            jobs.append((("turn0", n - LAG0), V))
        if n - LAG0 >= 1:
            jobs.append((("attn0", n - LAG0 - 1), V))
    add("xT1", FC, [V])
    add("ffn", 4, [V])
    add("xT2", FC, [V])
    add("k1", 4, [V])
    add("v1", 4, [A])
    add("kv1", 1, [V])
    add("q1", 4, [V])
    add("mixM1", 2, [V])
    add("den", 1, [V])
    jobs.extend([(("gv0", 0), V), (("gv0", 1), A)])
    add("zb", 4, [V])
    jobs.extend([(("gv0", 2), V), (("gv0", 3), A)])
    add("mixout1", 4, [V])
    for l in range(L):
        if l:
            add(f"gv{l}", 4, [V, A])
        for step, i in attention_order():
            if step == "agg_start":
                continue
            engine = {"q": V, "k": V, "score": V, "turn": (V, A)[i % 2], "rsum": V, "rsum_bc": V, "agg": A}[step]
            jobs.append(((f"{step}{l}g", i), engine))
        add(f"wo{l}", FC, [V])
        add(f"h{l}", 2, [A])
        add(f"f{l}", FC, [V])
    add("gT", 4, [V])
    add("fT", 2, [V, A])
    add("hid", 2 * HG, [V, A])
    add("y", 2, [V, A])
    add("yT", 2, [V])
    return jobs


JOBS = job_table()
INDEX = {name: j for j, (name, _) in enumerate(JOBS)}
EVAC_COUNT = {}
_seen = {"act": 0, "dve": 0}
for _name, _engine in JOBS:
    _seen[_engine] += 1
    EVAC_COUNT[_name] = _seen[_engine]

COLS = {}


def _col(name, n):
    COLS[name] = (sum(w for _, w in COLS.values()), n)


for _n in ("bq", "bk", "b_in"):
    _col(_n, FC)
for _l in range(L):
    for _n in ("gbq", "gbo", "gb2", "g1", "be1", "g2", "be2"):
        _col(f"{_n}{_l}", FC)
    _col(f"gb1{_l}", 2)
NCOL = sum(w for _, w in COLS.values())
ROWS = ["L0_gnn_bv", "L0_mix_b_out", "L0_ffn_bias", "L1_mix_bout", "L1_gnn_ln_g", "L1_gnn_ln_b"]

SPLIT_WEIGHTS = ["k1", "v1", "q1", "gv0"]
NIB_LOADS = 4 * 3 + 6 + 1
WSLOTS = 3
WEIGHTS = [("winT", 0), ("v0", 1), ("k0", 2), ("win", 0), ("wout", 1), ("q0", 0), ("ffn", 0)]
WEIGHTS += [("k1", 1), ("v1", 2), ("q1", 1), ("wout1", 2), ("gv0", 0)]
for _n in [f"{_n}{_l}" for _l in range(L) for _n in ("gv", "gq", "gk", "go", "w12")][1:]:
    WEIGHTS.append((_n, (1, 2, 0)[(len(WEIGHTS) - 12) % WSLOTS]))
WSLOT = dict(WEIGHTS)
W_ROUND, W_BEFORE = {}, {}
for _s in range(WSLOTS):
    _names = [n for n, s in WEIGHTS if s == _s]
    for _i, _n in enumerate(_names):
        W_ROUND[_n], W_BEFORE[_n] = _i + 1, _names[_i - 1] if _i else None


def build(nc, a, out):
    fp32, fp32r, bf16, fp16, i32 = mybir.dt.float32, mybir.dt.float32r, mybir.dt.bfloat16, mybir.dt.float16, mybir.dt.int32
    ALU = mybir.AluOpType
    ACT = mybir.ActivationFunctionType
    AX = mybir.AxisListType
    ctx = ExitStack()
    with ctx:
        def sb(name, shape, dt=fp32):
            return ctx.enter_context(nc.sbuf_tensor(name, shape, dt))

        def sem(name):
            return ctx.enter_context(nc.semaphore(name))

        X = sb("X", [P, TT, D])
        xn_at = nc.sbuf_base
        XN = sb("XN", [P, TT, D])
        xt_at = nc.sbuf_base
        XT = sb("XT", [P, FC, N])
        qs_at = nc.sbuf_base
        QZ = sb("QZ", [P, 2, 2, N])
        QS = nc.alloc_sbuf_tensor_at("QS", [P, 2, 2, 2, D], fp32r, offset=qs_at)
        ks_at = nc.sbuf_base
        KR = sb("KR", [P, 2, N])
        KS0 = nc.alloc_sbuf_tensor_at("KS0", [P, 2, N], fp32r, offset=ks_at)
        ag_at = nc.sbuf_base
        AG = sb("AG", [P, FC, N])
        MASK = sb("MASK", [P, TT, N])
        pt_at = nc.sbuf_base
        PT = sb("PT", [P, 12288])
        KS = [KS0, nc.alloc_sbuf_tensor_at("KS1", [P, 2, N], fp32r, offset=pt_at + 4 * 10240)]
        SM = sb("SM", [P, 2, N])
        w_at = nc.sbuf_base
        W = sb("W", [P, WSLOTS, FC * D])
        BC = sb("BC", [P, 2, D])
        ident = sb("ident", [P, P])
        ones = sb("ones", [P, P])
        QF = sb("QF", [P, D])
        cols = sb("cols", [P, NCOL])
        st = sb("st", [P, TT, 6])
        mv = sb("mv", [P, TT, 2])
        rstd = sb("rstd", [P, TT])
        nm = sb("nm", [P, 8])
        ls = sb("ls", [P, 2, 16])
        rl = sb("rl", [P, 16])
        tiny = sb("tiny", [P, 4])
        bns = sb("bns", [P, 8])

        psum = ctx.enter_context(nc.psum_tensor("slots", [P, 4, N], fp32))

        flat = lambda t: t[:].rearrange("p a b -> p (a b)")
        qz = QZ[:].rearrange("p a b c -> p (a b c)")
        ag, kr = flat(AG), flat(KR)
        iota = PT[:, 0:512].bitcast(fp16)
        srcrow = PT[:, 512:2560].bitcast(bf16).rearrange("p (r n) -> p r n", r=GC)
        dstrow = PT[:, 2560:2816].bitcast(bf16).rearrange("p (r n) -> p r n", r=GC)
        idx_i = PT[:, 2816:3200].bitcast(i32)
        dst_f, src_f, drow_f = PT[:, 3200:3328], PT[:, 3328:3456], PT[:, 3456:3584]
        zeros = PT[:, 3584:3584 + 256].bitcast(bf16)
        cmin, cmax = PT[:, 3840:3841], PT[:, 3841:3842]
        brow = PT[0:1, 3842:3842 + 256]
        lo8, c8, relA, relB = (ag[0:1, 256 * n:256 * n + TT * NG].rearrange("p (t c) -> p t c", t=TT) for n in range(4))
        glow, ghigh = ag[0:1, 1024:1024 + NG], ag[0:1, 1056:1056 + NG]
        bnd = PT[0:1, 4100:4132]
        bnd_i = PT[0:1, 4132:4164].bitcast(i32)
        QT0, KT0 = qz.rearrange("p (c n) -> p c n", c=FC), AG
        V0 = PT[:, 0:4096].rearrange("p (t d) -> p t d", t=TT)
        adj0 = PT[:, 4096:8192].bitcast(bf16).rearrange("p (t n) -> p t n", t=TT)
        negm = PT[:, 8192:10240].rearrange("p (r n) -> p r n", r=2)
        def split_at(name, offset, shape):
            return nc.alloc_sbuf_tensor_at(name, shape, fp32r, offset=offset)

        Q0R, Q0L = split_at("Q0R", xt_at, [P, FC, N]), split_at("Q0L", qs_at, [P, FC, N])
        K0R, K0L = split_at("K0R", w_at + 4 * FC * D, [P, FC, N]), split_at("K0L", ag_at, [P, FC, N])
        V0R, V0L = split_at("V0R", xn_at, [P, TT, D]), split_at("V0L", pt_at, [P, TT, D])
        P0R, P0L = (split_at(f"P0{c}", pt_at + 4 * at, [P, TT, P]) for c, at in (("R", 10240), ("L", 11264)))
        o = [0]

        def part(n, rows=P):
            o[0] += n
            return qz[0:rows, o[0] - n:o[0]]

        bdqk = part(256).rearrange("p (c n) -> p c n", c=FC)
        bdv = part(128)
        wqk = part(256).rearrange("p (c n) -> p c n", c=FC)
        b_bc = part(512).rearrange("p (c n) -> p c n", c=FC)
        bq_bc = part(32)
        bk_col = part(1, 32)
        part(7)
        ql = part(256).rearrange("p (t n) -> p t n", t=TT)
        qm = part(64)
        qr = part(64)
        ek = part(256).rearrange("p (t n) -> p t n", t=TT)
        kx = part(512, 32)
        kxT = part(128).rearrange("p (c n) -> p c n", c=FC)
        xmT = part(128).rearrange("p (c n) -> p c n", c=FC)
        hm = part(128).rearrange("p (c n) -> p c n", c=FC)
        kvT = part(128).rearrange("p (c n) -> p c n", c=FC)
        mixM = part(512, 32)
        kmax, ksum, krec = part(1, 32), part(1, 32), part(1, 32)
        ekT, qsT = KR[0:32, 0, :], KR[0:32, 1, :]
        K1 = PT[:, 0:4096].rearrange("p (t d) -> p t d", t=TT)
        V1 = PT[:, 4096:8192].rearrange("p (t d) -> p t d", t=TT)
        kvT1 = PT[:, 8192:8704].rearrange("p (c n) -> p c n", c=FC)
        KS1 = PT[:, 8704:8736].rearrange("p (c h) -> p c h", c=FC)
        selh = PT[:, 11392:11904].rearrange("p (c n) -> p c n", c=FC)
        blk = PT[:, 11264:11392]
        hm1 = PT[:, 11904:12032].rearrange("p (c n) -> p c n", c=FC)
        XTR, XTL = split_at("XTR", ag_at, [P, FC, N]), split_at("XTL", qs_at, [P, FC, N])
        WL = [split_at(f"WL{s}", w_at + 4 * FC * D * s, [P, FC, D]) for s in range(WSLOTS)]
        WKR = split_at("WKR", ks_at, [P, FC, D])
        ROUNDED = {"k1": WKR, "v1": WL[0], "q1": WKR, "gv0": WKR}
        M1R, M1L = split_at("M1R", w_at + 4 * FC * D * WSLOT["wout1"], [P, FC, D]), split_at("M1L", pt_at + 4 * 9216, [P, FC, D])
        Q1R, Q1L = split_at("Q1R", pt_at + 4 * 4096, [P, FC, N]), split_at("Q1L", pt_at, [P, FC, N])
        QT1 = PT[:, 0:4096].rearrange("p (c n) -> p c n", c=FC)
        zT = SM[:, 0, :]
        PTr = PT[:, 0:8192].rearrange("p (b e s n) -> p b e s n", b=2, e=2, s=TT)
        SMs = [SM[:, 0, :], SM[:, 1, :], PT[:, 8192:9216], PT[:, 9216:10240]]
        GV = XN
        rT = ones[0:16, :]
        sel = BC[0:16, :, :].rearrange("k a n -> k (a n)").rearrange("k (t n) -> k t n", t=TT)
        HT = PT[:, 0:HG * 2 * N].rearrange("p (g n) -> p g n", g=HG)
        W1s = qz[:, 0:3 * GE]
        w2m = qz[:, 1504:1632].rearrange("p (g k) -> p g k", g=HG)
        YS = SM[:].rearrange("p a b -> p (a b)")
        b2bc = qz[:, 992:995]
        F6 = qz[:, 1024:1120].rearrange("p (t r j) -> p t r j", t=TT, r=2)
        Fr = nc.alloc_sbuf_tensor_at("Fr", [P, 2 * TT, P], fp32r, offset=pt_at + 4 * 8192)
        FT = nc.alloc_sbuf_tensor_at("FT", [P, 2 * N], fp32r, offset=qs_at + 4 * 2048)
        W1r = nc.alloc_sbuf_tensor_at("W1r", [P, 3 * GE], fp32r, offset=qs_at + 4 * 512)
        bits = ag[:, 0:512].rearrange("p (t j n) -> p t j n", t=TT, j=4)
        m16 = ag[:, 512:544].rearrange("p (t j) -> p t j", t=TT)
        i16 = ag[:, 544:560]
        i16m = ag[:, 560:576]
        flags = ag[:, 576:608].rearrange("p (t j) -> p t j", t=TT)
        ysel = ag[:, 608:656].rearrange("p (t r k) -> p t r k", t=TT, r=2)
        pick = ag[:, 656:680].rearrange("p (t k) -> p t k", t=TT)
        res = ag[:, 688:704].rearrange("p (t r) -> p t r", t=TT)
        act_on = ag[:, 704:712]
        oneh = ag[:, 768:1024].rearrange("p (t r n) -> p t r n", t=TT, r=2)
        sumc = ag[:, 1024:1040].rearrange("p (c t) -> p c t", c=2)
        yk = ag[:, 2048:2096].rearrange("p (t r k) -> p t r k", t=TT, r=2)

        psum_full, dve_evacuated, act_evacuated = sem("psum_full"), sem("dve_evacuated"), sem("act_evacuated")
        w_loaded = [sem(f"w_loaded{s}") for s in range(WSLOTS)]
        row_loaded = [sem(f"row_loaded{s}") for s in range(2)]
        x_loaded, idx_loaded, cols_loaded, bd_loaded, nib_loaded = (
            sem(n) for n in ("x_loaded", "idx_loaded", "cols_loaded", "bd_loaded", "nib_loaded"))
        const_made, bd_cleared, blk_made, q_cleared, i16_made = (
            sem(n) for n in ("const_made", "bd_cleared", "blk_made", "q_cleared", "i16_made"))
        pool_link, dve_link = sem("pool_link"), sem("dve_link")
        bounds_made, onehot_ready, onehot_used, mm_bounds = (
            sem(n) for n in ("bounds_made", "onehot_ready", "onehot_used", "minmax_made"))
        counts_floored, logs_taken, mask_made = sem("counts_floored"), sem("logs_taken"), sem("mask_made")
        negm_made, masked0, probs0, x_biased = sem("negm_made"), sem("masked0"), sem("probs0"), sem("x_biased")
        rows_normed, var_ready, std_ready = sem("rows_normed"), sem("var_ready"), sem("std_ready")
        bias_spread, keys_max_ready, keys_exp, queries_shifted, queries_exp, queries_normed = (
            sem(n) for n in ("bias_spread", "keys_max_ready", "keys_exp", "queries_shifted", "queries_exp", "queries_normed"))
        wstat, wsign, wmean, ffn_row = sem("w_sums"), sem("w_signs"), sem("w_mean"), sem("ffn_row_used")
        kneg, kexp, x1_biased = sem("min_ready"), sem("elu_exp"), sem("x1_biased")
        probs, recips, bn_ready, state_ready, act_chunk_ready = (
            sem(n) for n in ("probs", "recips", "bn_ready", "state_ready", "act_chunk_ready"))
        q_doubled, q_split, k_rounded, k_split0, sel_made = (sem(n) for n in ("q_doubled", "q_split", "k_rounded", "k_split0", "sel_made"))
        v0_rounded, k0_rounded, q0_rounded, p0_rounded, v0_split, k0_split, q0_split = (
            sem(n) for n in ("v0_rounded", "k0_rounded", "q0_rounded", "p0_rounded", "v0_split", "k0_split", "q0_split"))
        xT_rounded, w_rounded, w_split, x_whole, ffn_made, ffn_added, z_cleared = (
            sem(n) for n in ("xT_rounded", "w_rounded", "w_split", "x_whole", "ffn_made", "ffn_added", "z_cleared"))
        m1_rounded, q1_scaled_rounded, q1_scaled_split = (
            sem(n) for n in ("m1_rounded", "q1_scaled_rounded", "q1_scaled_split"))
        hid_ready, stored = sem("features_ready"), sem("stored")
        shift_added, out_summed, nibbles_added, hid_cleared, w1_split, sum_ready = (
            sem(n) for n in ("shift_added", "out_summed", "nibbles_added", "hid_cleared", "w1_split", "sum_coefficients_ready"))

        slot_of = lambda name, i: psum[:, INDEX[(name, i)] % 4, :]

        def evacuated(name, i):
            engine = JOBS[INDEX[(name, i)]][1]
            return (dve_evacuated if engine == "dve" else act_evacuated), EVAC_COUNT[(name, i)]

        def full(eng, name, i):
            eng.wait_ge(psum_full, INDEX[(name, i)] + 1)
            return slot_of(name, i)

        def done(eng, name, i):
            eng.wait_ge(*evacuated(name, i))

        def col(name, c=None):
            at, w = COLS[name]
            return cols[:, at:at + w] if c is None else cols[:, at + c:at + c + 1]

        def wtile(name):
            return W[:, WSLOT[name], :].rearrange("p (k n) -> p k n", k=FC)

        def w_ready(eng, name):
            eng.wait_ge(w_loaded[WSLOT[name]], 16 * W_ROUND[name])

        def row(name):
            return BC[:, ROWS.index(name) % 2, :]

        def row_ready(eng, name):
            n = ROWS.index(name)
            eng.wait_ge(row_loaded[n % 2], 16 * (n // 2 + 1))

        def turned(eng, copy_out, l, n):
            g = n // 4
            if g >= 2:
                eng.wait_ge(psum_full, INDEX[(f"agg{l}g", g - 2)] + 1)
            else:
                eng.wait_ge(psum_full, INDEX[("mixout1", 3) if l == 0 else ("agg0g", UNITS // 4 - 1)] + 1)
            copy_out(PTr[:, g % 2, n // 2 % 2, :, n % 2 * P:(n % 2 + 1) * P], f"turn{l}g", n,
                     lambda s: s.rearrange("p (s n) -> p s n", s=TT))

        LAST_USE = {
            "q0": ("q0", 3), "k0": ("score0", TT - 1), "v0": ("v0", 3), "winT": ("wqk", 0), "win": ("xmT", 0),
            "wout": ("score0", TT - 1), "ffn": ("v1", 3), "k1": ("k1", 3), "v1": ("v1", 3), "q1": ("q1", 3),
            "wout1": ("mixout1", 3)}
        for l in range(L):
            LAST_USE.update({f"gv{l}": (f"gv{l}", 3), f"gq{l}": (f"q{l}g", H - 1), f"gk{l}": (f"k{l}g", 3),
                             f"go{l}": (f"wo{l}", 3), f"w12{l}": (f"f{l}", 3)})

        block = ctx.enter_context(nc.Block())

        @block.sync
        def _(sp):
            sp.dma_start(idx_i, a["idx"]).then_inc(idx_loaded, 16)
            sp.dma_start(X[:], a["x"].rearrange("(t p) d -> p t d", p=P)).then_inc(x_loaded, 16)
            sp.dma_start(cols[:], a["cols"]).then_inc(cols_loaded, 16)

            def load_row(n):
                sp.dma_start(BC[:, n % 2, :], a["rows"][n:n + 1, :].broadcast_to([P, D])).then_inc(row_loaded[n % 2], 16)

            def load_weight(name):
                s = WSLOT[name]
                if W_BEFORE[name]:
                    sp.wait_ge(psum_full, INDEX[LAST_USE[W_BEFORE[name]]] + 1)
                if name.startswith("w12"):
                    l = int(name[-1])
                    sp.dma_start(W[:, s, :], a["w12"][l]).then_inc(w_loaded[s], 16)
                else:
                    sp.dma_start(wtile(name), a[name].rearrange("(k p) n -> p k n", p=P)).then_inc(w_loaded[s], 16)

            load_row(0)
            load_row(1)
            for name, _ in WEIGHTS[:3]:
                load_weight(name)
            sp.wait_ge(bd_cleared, 1)
            for h in range(H):
                p0, c = (h % 2) * DH, h // 2
                sp.dma_start(bdqk[p0:p0 + DH, c, R * h:R * h + R], a["mq"]).then_inc(bd_loaded, 16)
                sp.dma_start(bdqk[p0:p0 + DH, c, 32 + R * h:32 + R * h + R], a["mk"]).then_inc(bd_loaded, 16)
            for e in range(2):
                sp.dma_start(bdv[e * DH:(e + 1) * DH, e * DH:(e + 1) * DH], a["mv"]).then_inc(bd_loaded, 16)
            sp.wait_ge(x_biased, TT)
            load_row(2)
            load_row(3)
            for name, _ in WEIGHTS[3:]:
                load_weight(name)
            sp.wait_ge(psum_full, INDEX[(f"rsum_bc{L - 1}g", H // 2 - 1)] + 1)
            load_row(4)
            load_row(5)
            sp.wait_ge(hid_cleared, 1)
            for at in range(0, P, 32):
                for r0, n, row0 in ((0, 2, 0), (44, 3, 2)):
                    sp.dma_start(W1s[at + row0:at + row0 + n, :].rearrange("r (k e) -> r k e", k=3),
                                 a["nw1"][:, r0:r0 + n, :].rearrange("k r e -> r k e")).then_inc(nib_loaded, 16)
                sp.dma_start(W1s[at + 5:at + 6, :], a["nb1"]).then_inc(nib_loaded, 16)
            for g in range(HG):
                for k in range(3):
                    h0, h1 = max(GU * g, GE * k), min(GU * (g + 1), GE * (k + 1))
                    if h0 < h1:
                        sp.dma_start(w2m[h0 - GU * g:h1 - GU * g, g, k:k + 1],
                                     a["nw2"][k:k + 1, h0 - GE * k:h1 - GE * k].rearrange("k e -> e k")).then_inc(nib_loaded, 16)
            sp.dma_start(b2bc, a["nb2"].broadcast_to([P, 3])).then_inc(nib_loaded, 16)
            sp.wait_ge(stored, 32)

        @block.gpsimd
        def _(pool):
            links = [0]

            def link(ins):
                links[0] += 1
                ins.then_inc(pool_link, 1)
                pool.wait_ge(pool_link, links[0])

            def head_mask(m):
                link(nc.gpsimd.memset(m, 1.0))
                m4 = m.rearrange("p c (h r) -> p c h r", r=R)
                link(nc.gpsimd.affine_select(out=m4, in_=m4, compare_op=ALU.is_ge, fill=0.0, base=0,
                                             pattern=[[P, FC], [-DH, H], [0, R]], channel_multiplier=1))
                return nc.gpsimd.affine_select(out=m4, in_=m4, compare_op=ALU.is_ge, fill=0.0, base=DH - 1,
                                               pattern=[[-P, FC], [DH, H], [0, R]], channel_multiplier=-1)

            link(nc.gpsimd.memset(ident[:], 0.0))
            nc.gpsimd.affine_select(out=ident[:], in_=ident[:], compare_op=ALU.not_equal, fill=1.0, base=0,
                                    pattern=[[-1, P]], channel_multiplier=1).then_inc(const_made, 1)
            nc.gpsimd.iota(iota, [[1, N]], base=0, channel_multiplier=0,
                           allow_small_or_imprecise_dtypes=True).then_inc(const_made, 1)
            nc.gpsimd.iota(lo8, [[P, TT], [0, NG]], base=0, channel_multiplier=0,
                           allow_small_or_imprecise_dtypes=True).then_inc(const_made, 1)
            nc.gpsimd.iota(c8, [[0, TT], [1, NG]], base=0, channel_multiplier=0,
                           allow_small_or_imprecise_dtypes=True).then_inc(const_made, 1)
            nc.gpsimd.memset(zeros, 0.0).then_inc(const_made, 1)
            nc.gpsimd.memset(ones[:], 1.0).then_inc(const_made, 1)
            nc.gpsimd.memset(bdqk, 0.0)
            link(nc.gpsimd.memset(bdv, 0.0))
            head_mask(hm).then_inc(bd_cleared, 1)
            pool.wait_ge(rows_normed, TT)
            row_ready(pool, "L0_gnn_bv")
            row_ready(pool, "L0_mix_b_out")
            for t in range(TT):
                link(nc.gpsimd.tensor_tensor(X[:, t, :], X[:, t, :], row("L0_gnn_bv"), ALU.add))
                nc.gpsimd.tensor_tensor(X[:, t, :], X[:, t, :], row("L0_mix_b_out"), ALU.add).then_inc(x_biased, 1)
            for i in range(TT + 2):
                if i >= 2:
                    pool.wait_ge(logs_taken, i - 1)
                    nc.gpsimd.tensor_tensor(MASK[:, i - 2, :], MASK[:, i - 2, :], KR[:, i % 2, :],
                                            ALU.add).then_inc(mask_made, 1)
                if i < TT:
                    done(pool, "adjT", 6)
                    done(pool, "adjT", 7)
                    pool.wait_ge(psum_full, INDEX[("mixout", 3)] + 1)
                    if i >= 2:
                        pool.wait_ge(masked0, i - 1)
                        pool.wait_ge(mask_made, i - 1)
                    nc.gpsimd.tensor_scalar(negm[:, i % 2, :], adj0[:, i, :], -NEG, NEG, ALU.mult, ALU.add).then_inc(negm_made, 1)
                    nc.gpsimd.tensor_scalar(KR[:, i % 2, :], MASK[:, i, :], 1.0, None, ALU.max).then_inc(counts_floored, 1)
                    link(nc.gpsimd.tensor_scalar(MASK[:, i, :], MASK[:, i, :], 0.5, NO_EDGE, ALU.is_lt, ALU.mult))
            for j in range(4):
                xs = X[:, 2 * j:2 * j + 2, :]
                pool.wait_ge(ffn_made, j + 1)
                nc.gpsimd.tensor_tensor(xs, xs, SM[:, j % 2, :].rearrange("p (t d) -> p t d", t=2), ALU.add).then_inc(ffn_added, 1)

            def rest_of_weight(n):
                name = SPLIT_WEIGHTS[n]
                pool.wait_ge(w_rounded, n + 1)
                nc.gpsimd.tensor_tensor(WL[WSLOT[name]][:], wtile(name), ROUNDED[name][:].bitcast(fp32),
                                        ALU.subtract).then_inc(w_split, 1)

            rest_of_weight(0)
            rest_of_weight(1)
            pool.wait_ge(rows_normed, 3 * TT)
            link(nc.gpsimd.memset(blk, 0.0))
            link(nc.gpsimd.memset(blk[0:DH, 0:DH], 1.0))
            link(nc.gpsimd.memset(blk[DH:P, DH:P], 1.0))
            link(head_mask(hm1))
            link(nc.gpsimd.memset(selh, 0.0))
            s4 = selh.rearrange("k c (e m) -> k c e m", e=2)
            nc.gpsimd.affine_select(out=s4, in_=s4, compare_op=ALU.not_equal, fill=1.0, base=0,
                                    pattern=[[-2, FC], [-1, 2], [0, DH]], channel_multiplier=1).then_inc(blk_made, 1)
            pool.wait_ge(blk_made, 1)
            for j in range(4):
                done(pool, "xT2", j)
                js = slice(2 * j * P, 2 * (j + 1) * P)
                nc.gpsimd.tensor_tensor(XT[:, :, js], XTR[:, :, js].bitcast(fp32), XTL[:, :, js].bitcast(fp32),
                                        ALU.add).then_inc(x_whole, 1)
            rest_of_weight(2)
            row_ready(pool, "L1_mix_bout")
            for t in range(TT):
                nc.gpsimd.tensor_tensor(X[:, t, :], X[:, t, :], row("L1_mix_bout"), ALU.add).then_inc(x1_biased, 1)
            pool.wait_ge(x1_biased, TT)
            pool.wait_ge(*evacuated("q1", 3))
            nc.gpsimd.memset(zT, 0.0).then_inc(z_cleared, 1)
            rest_of_weight(3)
            link(nc.gpsimd.memset(sel, 0.0))
            sel4 = sel.rearrange("k t (e m) -> k t e m", e=2)
            nc.gpsimd.affine_select(out=sel4, in_=sel4, compare_op=ALU.not_equal, fill=1.0, base=0,
                                    pattern=[[-2, TT], [-1, 2], [0, DH]], channel_multiplier=1).then_inc(sel_made, 1)
            pool.wait_ge(psum_full, INDEX[("mixout1", 3)] + 1)
            for b in range(2):
                link(nc.gpsimd.memset(QS[DH:P, b, 0, 1, :].bitcast(fp32), 0.0))
                nc.gpsimd.memset(QS[0:DH, b, 1, 1, :].bitcast(fp32), 0.0).then_inc(q_cleared, 1)
                pool.wait_ge(q_cleared, b + 1)
            for l in range(L):
                for j in range(H):
                    done(pool, f"q{l}g", j)
                    if j >= 2:
                        pool.wait_ge(psum_full, INDEX[(f"score{l}g", 8 * j - 9)] + 1)
                    own = [slice(0, DH), slice(DH, P)]
                    nc.gpsimd.tensor_scalar(QS[own[0], j % 2, 0, 0, :], QF[own[0], :], 1.0, None, ALU.mult)
                    link(nc.gpsimd.tensor_scalar(QS[own[1], j % 2, 1, 0, :], QF[own[1], :], 1.0, None, ALU.mult))
                    for e in range(2):
                        last = nc.gpsimd.tensor_tensor(QS[own[e], j % 2, e, 1, :], QF[own[e], :],
                                                       QS[own[e], j % 2, e, 0, :].bitcast(fp32), ALU.subtract)
                        last.then_inc(q_split, 1)
            pool.wait_ge(psum_full, INDEX[(f"turn{L - 1}g", UNITS - 1)] + 1)
            link(nc.gpsimd.memset(W1s, 0.0))
            link(nc.gpsimd.memset(w2m, 0.0))
            link(nc.gpsimd.memset(F6, 1.0))
            nc.gpsimd.memset(Fr[:].bitcast(fp32), 0.0).then_inc(hid_cleared, 1)
            pool.wait_ge(hid_cleared, 1)
            row_ready(pool, "L1_gnn_ln_b")
            for t in range(TT):
                nc.gpsimd.tensor_tensor(X[:, t, :], X[:, t, :], row("L1_gnn_ln_b"), ALU.add).then_inc(shift_added, 1)
            pool.wait_ge(shift_added, TT)
            pool.wait_ge(psum_full, INDEX[(f"wo{L - 1}", 3)] + 1)
            nc.gpsimd.iota(i16, [[1, 16]], base=0, channel_multiplier=0,
                           allow_small_or_imprecise_dtypes=True).then_inc(i16_made, 1)
            nc.gpsimd.iota(i16m, [[1, 16]], base=-16, channel_multiplier=0,
                           allow_small_or_imprecise_dtypes=True).then_inc(i16_made, 1)
            pool.wait_ge(nib_loaded, 16 * NIB_LOADS)
            link(nc.gpsimd.tensor_scalar(W1r[:], W1s, 1.0, None, ALU.mult))
            nc.gpsimd.tensor_tensor(W1r[64:P, :], W1s[64:P, :], W1r[64:P, :].bitcast(fp32), ALU.subtract).then_inc(w1_split, 1)

        @block.scalar
        def _(act):
            def copy_out(dst, name, i, view=None):
                src = full(act, name, i)
                src = src if view is None else view(src)
                nc.scalar.activation(dst, src, ACT.Copy).then_inc(act_evacuated, 1)

            def take_std(n, c0=0, c1=TT):
                act.wait_ge(var_ready, n)
                nc.scalar.activation(rstd[:, c0:c1], rstd[:, c0:c1], ACT.Sqrt).then_inc(std_ready, 1)

            def round_xT(n):
                for j in range(4):
                    src = full(act, f"xT{n}", j).rearrange("p (c n) -> p c n", c=FC)
                    if n == 2:
                        act.wait_ge(psum_full, INDEX[("ffn", j)] + 1)
                    nc.scalar.activation(XTR[:, :, 2 * j * P:2 * (j + 1) * P], src, ACT.Copy).then_inc(xT_rounded, 1)

            def round_weight(n):
                name = SPLIT_WEIGHTS[n]
                w_ready(act, name)
                nc.scalar.activation(ROUNDED[name][:], wtile(name), ACT.Copy).then_inc(w_rounded, 1)

            take_std(1)
            for j in (1, 3):
                copy_out(XT[:, :, 2 * j * P:2 * (j + 1) * P], "xT0", j, lambda s: s.rearrange("p (c n) -> p c n", c=FC))
            for t in range(TT):
                copy_out(MASK[:, t, :], "counts", t)
            for name, i in MIXER0_ORDER:
                if name == "adjT" and i % 2:
                    src = full(act, name, i)
                    nc.scalar.activation(adj0[:, i, :], src, ACT.Sign).then_inc(act_evacuated, 1)
                elif name == "v0" and i % 2:
                    copy_out(V0[:, 2 * i:2 * i + 2, :], "v0", i, lambda s: s.rearrange("p (t d) -> p t d", t=2))
                elif name in ("q0", "k0") and i % 2:
                    if (name, i) == ("k0", 1):
                        act.wait_ge(cols_loaded, 16)
                    if (name, i) == ("q0", 1):
                        act.wait_ge(psum_full, INDEX[("mixout", 3)] + 1)
                    src = full(act, name, i)
                    dst = QT0 if name == "q0" else KT0
                    nc.scalar.activation(dst[:, i, :], src, ACT.Identity, bias=col("b" + name[0], i),
                                         scale=1.0).then_inc(act_evacuated, 1)
                elif (name, i) == ("mixout", 0):
                    act.wait_ge(psum_full, INDEX[("mixM", 0)] + 1)
                    for j in range(4):
                        done(act, "v0", j)
                        nc.scalar.activation(V0R[:, 2 * j:2 * j + 2, :], V0[:, 2 * j:2 * j + 2, :], ACT.Copy).then_inc(v0_rounded, 1)
                    act.wait_ge(psum_full, INDEX[("k0", 3)] + 1)
                    for c in range(FC):
                        done(act, "k0", c)
                        nc.scalar.activation(K0R[:, c, :], KT0[:, c, :], ACT.Copy).then_inc(k0_rounded, 1)
                elif name == "klog":
                    act.wait_ge(keys_max_ready, 1)
                    nc.scalar.activation(ekT, ekT, ACT.Exp, bias=kmax, scale=1.0, accum_out=ksum).then_inc(keys_exp, 1)
                elif name == "qlog":
                    act.wait_ge(queries_shifted, 1)
                    nc.scalar.activation(ql, ql, ACT.Exp).then_inc(queries_exp, 1)
            def round_queries(n):
                ns = slice(n * P, (n + 1) * P)
                nc.scalar.activation(Q0R[:, :, ns], QT0[:, :, ns], ACT.Copy).then_inc(q0_rounded, 1)

            act.wait_ge(psum_full, INDEX[("q0", 3)] + 1)
            for c in range(FC):
                done(act, "q0", c)
            for n in range(3):
                round_queries(n)
            for n in range(TT + LAG0 + 1):
                if n + 3 < TT:
                    round_queries(n + 3)
                if n < TT:
                    act.wait_ge(counts_floored, n + 1)
                    nc.scalar.activation(KR[:, n % 2, :], KR[:, n % 2, :], ACT.Ln).then_inc(logs_taken, 1)
                if n >= 1 and n - 1 < TT:
                    i = n - 1
                    act.wait_ge(masked0, i + 1)
                    nc.scalar.activation(SM[:, i % 2, :], SM[:, i % 2, :], ACT.Exp, bias=nm[:, i:i + 1], scale=-1.0,
                                         accum_out=ls[:, 0, i:i + 1]).then_inc(probs0, 1)
                i = n - LAG0
                if 0 <= i < TT:
                    if i >= 1:
                        act.wait_ge(psum_full, INDEX[("attn0", i - 1)] + 1)
                    src = full(act, "turn0", i)
                    nc.scalar.activation(P0R[:].rearrange("p s n -> p (s n)"), src, ACT.Copy).then_inc(p0_rounded, 1)
            act.wait_ge(wmean, 1)
            wf = wtile("ffn")
            nc.scalar.activation(WL[WSLOT["ffn"]][:], wf, ACT.Sign, bias=tiny[:, 2:3], scale=1.0).then_inc(wsign, 1)
            take_std(2)
            round_xT(1)
            act.wait_ge(mask_made, TT)
            round_weight(0)
            act.wait_ge(psum_full, INDEX[("ffn", 3)] + 1)
            round_weight(1)
            take_std(3)
            round_xT(2)
            for j in range(4):
                act.wait_ge(kneg, j + 1)
                nc.scalar.activation(SM[:, j % 2, :], SM[:, j % 2, :], ACT.Exp).then_inc(kexp, 1)
            for j in range(4):
                copy_out(V1[:, 2 * j:2 * j + 2, :], "v1", j, lambda s: s.rearrange("p (t d) -> p t d", t=2))
            act.wait_ge(psum_full, INDEX[("k1", 3)] + 1)
            round_weight(2)
            for j in range(4):
                act.wait_ge(kneg, j + 5)
                nc.scalar.activation(SM[:, j % 2, :], SM[:, j % 2, :], ACT.Exp).then_inc(kexp, 1)
            act.wait_ge(psum_full, INDEX[("q1", 3)] + 1)
            round_weight(3)
            act.wait_ge(psum_full, INDEX[("mixM1", 1)] + 1)
            for j in range(2):
                src = slot_of("mixM1", j).rearrange("p (t d) -> p t d", t=2)
                nc.scalar.activation(M1R[:, 2 * j:2 * j + 2, :], src, ACT.Copy).then_inc(m1_rounded, 1)
            copy_out(GV[:, 2:4, :], "gv0", 1, lambda s: s.rearrange("p (t d) -> p t d", t=2))
            for j in range(FC):
                done(act, "zb", j)
                nc.scalar.activation(Q1R[:, j, :], QT1[:, j, :], ACT.Copy).then_inc(q1_scaled_rounded, 1)
            copy_out(GV[:, 6:8, :], "gv0", 3, lambda s: s.rearrange("p (t d) -> p t d", t=2))

            for l in range(L):
                for j in (1, 3) if l else ():
                    copy_out(GV[:, 2 * j:2 * j + 2, :], f"gv{l}", j, lambda s: s.rearrange("p (t d) -> p t d", t=2))

                def exp_unit(n):
                    act.wait_ge(*evacuated(f"score{l}g", n))
                    pair, e, t = unit(n)
                    if n % 16 == 0 and n >= 32:
                        act.wait_ge(recips, H // 2 * l + pair - 1)
                    nc.scalar.activation(SMs[n % SMB], SMs[n % SMB], ACT.Exp, bias=nm[:, n % 8:n % 8 + 1], scale=-1.0,
                                         accum_out=ls[:, pair % 2, 2 * t + e:2 * t + e + 1]).then_inc(probs, 1)

                def exp_until(n):
                    while taken[0] <= n:
                        exp_unit(taken[0])
                        taken[0] += 1

                pt_free = (psum_full, INDEX[("mixout1", 3) if l == 0 else ("agg0g", UNITS // 4 - 1)] + 1)
                taken = [0]
                for step, n in attention_order():
                    if step == "q":
                        if n >= 2:
                            act.wait_ge(psum_full, INDEX[(f"score{l}g", 8 * n - 9)] + 1)
                        done(act, f"q{l}g", n)
                        nc.scalar.activation(QS[DH:P, n % 2, 0, 0, :], QF[0:DH, :], ACT.Copy)
                        nc.scalar.activation(QS[0:DH, n % 2, 1, 0, :], QF[DH:P, :], ACT.Copy).then_inc(q_doubled, 1)
                    elif step == "k":
                        if n >= 2:
                            act.wait_ge(psum_full, INDEX[(f"score{l}g", 16 * n - 17)] + 1)
                        elif n == 1:
                            act.wait_ge(*pt_free)
                        src = full(act, f"k{l}g", n)
                        for e in range(2):
                            own = slice(e * DH, (e + 1) * DH)
                            nc.scalar.activation(KS[n % 2][own, e, :], src[own, :], ACT.Copy).then_inc(k_rounded, 1)
                    elif step == "score" and n >= 1:
                        exp_until(n - 1)
                    elif step == "turn":
                        exp_until(n)
                        if n % 2 == 1:
                            turned(act, copy_out, l, n)
                    elif step == "agg":
                        copy_out(AG[:, n // 4, n % 4 * 256:(n % 4 + 1) * 256], f"agg{l}g", n, lambda s: s[:, 0:256])

                def bn_third_chunk(n):
                    take_std(2 * n + 4, 0, FC - 1)
                    act.wait_ge(bn_ready, 2 * n + 1)
                    nc.scalar.activation(XT[:, 2, :], XT[:, 2, :], ACT.Identity, bias=bns[:, 6:7],
                                         scale=bns[:, 2:3]).then_inc(act_chunk_ready, 1)
                    take_std(2 * n + 5, FC - 1, FC)

                bn_third_chunk(2 * l)
                for c in range(2):
                    src = full(act, f"h{l}", c)
                    nc.scalar.activation(KR[:, c, :], src, ACT.Relu, bias=col(f"gb1{l}", c), scale=1.0).then_inc(act_evacuated, 1)
                bn_third_chunk(2 * l + 1)
            take_std(4 + 4 * L)
            take_std(5 + 4 * L)
            act.wait_ge(sum_ready, 1)
            for t in range(TT):
                nc.scalar.activation(X[:, t, :], X[:, t, :], ACT.Identity, bias=sumc[:, 1, t:t + 1],
                                     scale=sumc[:, 0, t:t + 1]).then_inc(out_summed, 1)
            o_v = out.rearrange("(t p) d -> p t d", p=P)
            act.wait_ge(out_summed, TT)
            act.dma_start(o_v[:, :, 112:D], X[:, :, 112:D]).then_inc(stored, 16)
            copy_out(FT[:, N:2 * N], "fT", 1)
            for i in range(1, 2 * HG, 2):
                src = full(act, "hid", i)
                nc.scalar.activation(HT[0:GU, i // 2, N:2 * N], src[0:GU, :], ACT.Relu).then_inc(act_evacuated, 1)
            copy_out(YS[:, N:2 * N], "y", 1)
            act.wait_ge(nibbles_added, 1)
            act.dma_start(o_v[:, :, 0:112], X[:, :, 0:112]).then_inc(stored, 16)
            act.wait_ge(stored, 32)

        @block.vector
        def _(dve):
            links = [0]

            def link(ins):
                links[0] += 1
                ins.then_inc(dve_link, 1)
                dve.wait_ge(dve_link, links[0])

            rounds = [0]

            def std(n_cols, first=0):
                rounds[0] += 1
                part = rstd[:, first:n_cols]
                nc.vector.tensor_scalar(part, mv[:, first:n_cols, 1], EPS, None, ALU.add).then_inc(var_ready, 1)
                dve.wait_ge(std_ready, rounds[0])
                link(nc.vector.reciprocal(part, part))

            def row_stats(t, src):
                link(nc.vector.bn_stats(st[:, t, :], src))
                nc.vector.bn_aggr(mv[:, t, :], st[:, t, :]).then_inc(dve_link, 1)
                links[0] += 1

            def stats_of(sources):
                sums = {}
                for t in range(TT + 1):
                    if t < TT:
                        nc.vector.bn_stats(st[:, t, :], sources(t)).then_inc(dve_link, 1)
                        links[0] += 1
                        sums[t] = links[0]
                    if t >= 1:
                        dve.wait_ge(dve_link, sums[t - 1])
                        nc.vector.bn_aggr(mv[:, t - 1, :], st[:, t - 1, :]).then_inc(dve_link, 1)
                        links[0] += 1

            def normalise():
                dve.wait_ge(dve_link, links[0])
                std(TT)
                for t in range(TT):
                    nc.vector.tensor_scalar(XN[:, t, :], X[:, t, :], mv[:, t, 0:1], rstd[:, t:t + 1],
                                            ALU.subtract, ALU.mult).then_inc(rows_normed, 1)

            def copy_out(dst, name, i, view=None):
                src = full(dve, name, i)
                src = src if view is None else view(src)
                nc.vector.tensor_copy(dst, src).then_inc(dve_evacuated, 1)

            two = lambda s: s.rearrange("p (t d) -> p t d", t=2)

            def rest_of_xT(n):
                for j in range(4):
                    js = slice(2 * j * P, 2 * (j + 1) * P)
                    src = full(dve, f"xT{n}", j).rearrange("p (c n) -> p c n", c=FC)
                    dve.wait_ge(xT_rounded, 4 * (n - 1) + j + 1)
                    nc.vector.tensor_tensor(XTL[:, :, js], src, XTR[:, :, js].bitcast(fp32), ALU.subtract).then_inc(dve_evacuated, 1)

            dve.wait_ge(idx_loaded, 16)
            nc.vector.tensor_copy(dst_f, idx_i[:, 0:P])
            nc.vector.tensor_copy(src_f, idx_i[:, P:2 * P])
            link(nc.vector.tensor_copy(drow_f, idx_i[:, 2 * P:3 * P]))
            nc.vector.tensor_reduce(cmin, drow_f, AX.X, ALU.min)
            nc.vector.tensor_reduce(cmax, drow_f, AX.X, ALU.max).then_inc(mm_bounds, 1)
            dve.wait_ge(x_loaded, 16)
            stats_of(lambda t: X[:, t, :])
            normalise()
            src = full(dve, "bounds", 0)
            nc.vector.tensor_copy(brow, src[0:1, 0:2 * P]).then_inc(dve_evacuated, 1)
            dve.wait_ge(*evacuated("bounds", 0))
            dve.wait_ge(const_made, 5)
            nc.vector.tensor_reduce(glow, brow[:, 0:P].rearrange("p (g c) -> p g c", c=GC), AX.X, ALU.min)
            link(nc.vector.tensor_reduce(ghigh, brow[:, P:2 * P].rearrange("p (g c) -> p g c", c=GC), AX.X, ALU.max))
            nc.vector.tensor_tensor(relA, glow.unsqueeze(1).broadcast_to([1, TT, NG]), lo8, ALU.subtract)
            link(nc.vector.tensor_tensor(relB, ghigh.unsqueeze(1).broadcast_to([1, TT, NG]), lo8, ALU.subtract))
            link(nc.vector.tensor_scalar(relB, relB, 0.0, None, ALU.is_ge))
            link(nc.vector.scalar_tensor_tensor(relA, relA, float(P - 1), relB, ALU.is_le, ALU.mult))
            nc.vector.scalar_tensor_tensor(relB, c8, float(NG - 1), relA, ALU.subtract, ALU.mult)
            link(nc.vector.tensor_tensor(relA, c8, relA, ALU.mult))
            nc.vector.tensor_reduce(bnd[:, 0:8], relB, AX.X, ALU.min)
            link(nc.vector.tensor_reduce(bnd[:, 8:16], relA, AX.X, ALU.max))
            link(nc.vector.tensor_scalar(bnd[:, 0:8], bnd[:, 0:8], float(NG - 1), None, ALU.add))
            link(nc.vector.tensor_tensor(bnd[:, 8:16], bnd[:, 8:16], bnd[:, 0:8], ALU.max))
            link(nc.vector.tensor_scalar(bnd[:, 8:16], bnd[:, 8:16], 1.0, None, ALU.add))
            link(nc.vector.tensor_tensor(bnd[:, 16:24], bnd[:, 8:16], bnd[:, 0:8], ALU.subtract))
            link(nc.vector.memset(bnd[:, 24:25], float(SHIFT)))
            for t in range(1, TT):
                link(nc.vector.tensor_tensor(bnd[:, 24 + t:25 + t], bnd[:, 23 + t:24 + t], bnd[:, 15 + t:16 + t], ALU.add))
            link(nc.vector.tensor_tensor(bnd[:, 24:32], bnd[:, 24:32], bnd[:, 0:8], ALU.subtract))
            nc.vector.tensor_copy(bnd_i, bnd).then_inc(bounds_made, 1)
            for j in (0, 2):
                copy_out(XT[:, :, 2 * j * P:2 * (j + 1) * P], "xT0", j, lambda s: s.rearrange("p (c n) -> p c n", c=FC))
            dve.wait_ge(bounds_made, 1)
            dve.sem_inc(onehot_ready, GC * SHIFT)
            for t in range(TT):
                first = dve.value_load(bnd_i[0:1, t:t + 1], min_val=0, max_val=NG - 1)
                end = dve.value_load(bnd_i[0:1, 8 + t:9 + t], min_val=0, max_val=NG)
                before = dve.value_load(bnd_i[0:1, 24 + t:25 + t], min_val=0, max_val=SHIFT + TT * NG)
                with dve.Fori(first, end) as g:
                    for b in range(GC):
                        dve.wait_ge(onehot_used, (g + before) * GC + b + 1)
                        nc.vector.tensor_scalar(dstrow[:, b, :], iota[:, t * P:(t + 1) * P],
                                                dst_f[:, bass.ds(g * GC + b, 1)], None, ALU.is_equal)
                        nc.vector.tensor_scalar(srcrow[:, b, :], iota, src_f[:, bass.ds(g * GC + b, 1)], None,
                                                ALU.is_equal).then_inc(onehot_ready, 1)
            def mixer_step(name):
                if name == "wqk":
                    dve.wait_ge(cols_loaded, 16)
                    dve.wait_ge(bd_cleared, 1)
                    nc.vector.tensor_copy(b_bc, col("b_in").unsqueeze(2).broadcast_to([P, FC, P])).then_inc(bias_spread, 1)
                    copy_out(wqk, "wqk", 0, quarter)
                elif name == "bq0":
                    copy_out(bq_bc, "bq0", 0, lambda s: s[:, 0:32])
                elif name == "bk0":
                    copy_out(bk_col, "bk0", 0, lambda s: s[0:32, 0:1])
                elif name == "klog":
                    src = full(dve, "klog", 0)
                    dve.wait_ge(*evacuated("bk0", 0))
                    nc.vector.tensor_scalar(ekT, src[0:32, :], bk_col, None, ALU.add).then_inc(dve_evacuated, 1)
                    dve.wait_ge(*evacuated("klog", 0))
                    nc.vector.tensor_reduce(kmax, ekT, AX.X, ALU.max, negate=True).then_inc(keys_max_ready, 1)
                elif name == "qlog":
                    src = full(dve, "qlog", 0)
                    nc.vector.tensor_tensor(ql, src[:, 0:256].rearrange("p (t n) -> p t n", t=TT),
                                            bq_bc.unsqueeze(1).broadcast_to([P, TT, 32]), ALU.add).then_inc(dve_evacuated, 1)
                    dve.wait_ge(*evacuated("qlog", 0))
                    link(nc.vector.tensor_reduce(qm, qlf, AX.X, ALU.max))
                    nc.vector.tensor_tensor(qlf, qlf, qm.unsqueeze(2).broadcast_to([P, TT * H, R]),
                                            ALU.subtract).then_inc(queries_shifted, 1)
                elif name == "ekt":
                    dve.wait_ge(queries_exp, 1)
                    link(nc.vector.tensor_reduce(qr, qlf, AX.X, ALU.add))
                    link(nc.vector.reciprocal(qr, qr))
                    nc.vector.tensor_tensor(qlf, qlf, qr.unsqueeze(2).broadcast_to([P, TT * H, R]),
                                            ALU.mult).then_inc(queries_normed, 1)
                    dve.wait_ge(keys_exp, 1)
                    link(nc.vector.reciprocal(krec, ksum))
                    copy_out(ek, "ekt", 0, lambda s: s[:, 0:256].rearrange("p (t n) -> p t n", t=TT))
                elif name == "kx":
                    src = full(dve, "kx", 0)
                    nc.vector.tensor_scalar(kx, src[0:32, 0:D], krec, None, ALU.mult).then_inc(dve_evacuated, 1)
                elif name == "kxT":
                    copy_out(kxT, "kxT", 0, four32)
                elif name == "xmT":
                    src = four32(full(dve, "xmT", 0))
                    link(nc.vector.tensor_tensor(xmT, src, col("b_in").unsqueeze(2).broadcast_to([P, FC, 32]), ALU.add))
                    nc.vector.tensor_tensor(xmT, xmT, hm, ALU.mult).then_inc(dve_evacuated, 1)
                elif name == "kvT":
                    copy_out(kvT, "kvT", 0, four32)
                elif name == "mixM":
                    copy_out(mixM, "mixM", 0, lambda s: s[0:32, 0:D])
                elif name == "qsT":
                    copy_out(qsT, "qsT", 0, lambda s: s[0:32, :])

            quarter = lambda s: s[:, 0:256].rearrange("p (c n) -> p c n", c=FC)
            four32 = lambda s: s[:, 0:128].rearrange("p (c n) -> p c n", c=FC)
            qlf = ql.rearrange("p t (h r) -> p (t h) r", r=R)
            for name, i in MIXER0_ORDER:
                if (name, i) == ("q0", 0):
                    for j in range(4):
                        dve.wait_ge(v0_rounded, j + 1)
                        nc.vector.tensor_tensor(V0L[:, 2 * j:2 * j + 2, :], V0[:, 2 * j:2 * j + 2, :],
                                                V0R[:, 2 * j:2 * j + 2, :].bitcast(fp32), ALU.subtract).then_inc(v0_split, 1)
                    for c in range(FC):
                        dve.wait_ge(k0_rounded, c + 1)
                        nc.vector.tensor_tensor(K0L[:, c, :], KT0[:, c, :], K0R[:, c, :].bitcast(fp32),
                                                ALU.subtract).then_inc(k0_split, 1)
                if name == "adjT":
                    if i % 2 == 0:
                        src = full(dve, "adjT", i)
                        nc.vector.tensor_scalar(adj0[:, i, :], src, 1.0, None, ALU.min).then_inc(dve_evacuated, 1)
                elif name == "v0":
                    if i % 2 == 0:
                        copy_out(V0[:, 2 * i:2 * i + 2, :], "v0", i, two)
                elif name in ("q0", "k0"):
                    if i % 2 == 0:
                        src = full(dve, name, i)
                        dst = QT0 if name == "q0" else KT0
                        nc.vector.tensor_scalar(dst[:, i, :], src, col("b" + name[0], i), None,
                                                ALU.add).then_inc(dve_evacuated, 1)
                elif name == "mixout":
                    dve.wait_ge(x_biased, TT)
                    src = two(full(dve, "mixout", i))
                    nc.vector.tensor_tensor(X[:, 2 * i:2 * i + 2, :], src, X[:, 2 * i:2 * i + 2, :], ALU.add).then_inc(dve_evacuated, 1)
                else:
                    mixer_step(name)
            dve.wait_ge(*evacuated("mixout", 3))

            def rest_of_queries(n):
                ns = slice(n * P, (n + 1) * P)
                dve.wait_ge(q0_rounded, n + 1)
                nc.vector.tensor_tensor(Q0L[:, :, ns], QT0[:, :, ns], Q0R[:, :, ns].bitcast(fp32), ALU.subtract).then_inc(q0_split, 1)

            for n in range(3):
                rest_of_queries(n)
            for n in range(TT + LAG0 + 1):
                if n == 6:
                    w_ready(dve, "ffn")
                    wfl = W[:, WSLOT["ffn"], :]
                    nc.vector.tensor_reduce(tiny[:, 0:1], wfl, AX.X, ALU.add)
                    nc.vector.tensor_reduce(tiny[:, 1:2], wfl, AX.X, ALU.add, apply_absolute_value=True).then_inc(wstat, 1)
                if n == 7:
                    src = full(dve, "wsum", 0)
                    nc.vector.tensor_scalar(tiny[:, 2:3], src[:, 0:1], -1.0 / (D * D), None, ALU.mult).then_inc(wmean, 1)
                    nc.vector.tensor_scalar(tiny[:, 3:4], src[:, 1:2], 1.0 / (D * D), None, ALU.mult).then_inc(dve_evacuated, 1)
                if n < TT:
                    src = full(dve, "score0", n)
                    if n >= 2:
                        dve.wait_ge(psum_full, INDEX[("turn0", n - 2)] + 1)
                    else:
                        dve.wait_ge(*evacuated("adjT", 7))
                    nc.vector.scalar_tensor_tensor(SM[:, n % 2, :], src, float(D) ** -0.5, adj0[:, n, :],
                                                   ALU.mult, ALU.mult).then_inc(dve_evacuated, 1)
                    dve.wait_ge(*evacuated("score0", n))
                    dve.wait_ge(negm_made, n + 1)
                    nc.vector.tensor_tensor_reduce(out=SM[:, n % 2, :], in0=SM[:, n % 2, :], in1=negm[:, n % 2, :],
                                                   scale=-1.0, scalar=3e38, op0=ALU.add, op1=ALU.min,
                                                   accum_out=nm[:, n:n + 1]).then_inc(masked0, 1)
                    if n + 3 < TT:
                        rest_of_queries(n + 3)
                i = n - LAG0
                if 0 <= i < TT:
                    src = full(dve, "turn0", i)
                    dve.wait_ge(p0_rounded, i + 1)
                    nc.vector.tensor_tensor(P0L[:].rearrange("p s n -> p (s n)"), src,
                                            P0R[:].rearrange("p s n -> p (s n)").bitcast(fp32), ALU.subtract).then_inc(dve_evacuated, 1)
                i = n - LAG0 - 1
                if i >= 0:
                    dve.wait_ge(probs0, i + 1)
                    link(nc.vector.reciprocal(rl[:, i:i + 1], ls[:, 0, i:i + 1]))
                    src = full(dve, "attn0", i)
                    nc.vector.scalar_tensor_tensor(X[:, i, :], src[:, 0:D], rl[:, i:i + 1], X[:, i, :],
                                                   ALU.mult, ALU.add).then_inc(dve_evacuated, 1)
                    dve.wait_ge(*evacuated("attn0", i))
                    row_stats(i, X[:, i, :])
            normalise()
            rest_of_xT(1)
            row_ready(dve, "L0_ffn_bias")
            fb = row("L0_ffn_bias").unsqueeze(1).broadcast_to([P, 2, D])

            def ffn_stats(j):
                dve.wait_ge(ffn_added, j + 1)
                for t in (2 * j, 2 * j + 1):
                    row_stats(t, X[:, t, :])

            for j in range(4):
                y = two(SM[:, j % 2, :])
                src = two(full(dve, "ffn", j))
                if j == 0:
                    dve.wait_ge(*evacuated("wsum", 0))
                if j >= 2:
                    dve.wait_ge(ffn_added, j - 1)
                nc.vector.scalar_tensor_tensor(y, src, tiny[:, 3:4], fb, ALU.mult, ALU.add).then_inc(dve_evacuated, 1)
                dve.wait_ge(*evacuated("ffn", j))
                link(nc.vector.tensor_scalar(y, y, -1.0, 1.0, ALU.max, ALU.min))
                link(nc.vector.tensor_scalar(y, y, 7.0, MAGIC, ALU.mult, ALU.add))
                nc.vector.tensor_scalar(y, y, MAGIC, 1.0 / 7.0, ALU.subtract, ALU.mult).then_inc(ffn_made, 1)
                if j >= 1:
                    ffn_stats(j - 1)
            ffn_stats(3)
            normalise()
            rest_of_xT(2)

            def elu1(dst, name, j, n):
                src = full(dve, name, j)
                nc.vector.tensor_scalar(SM[:, n % 2, :], src, 0.0, None, ALU.min).then_inc(kneg, 1)
                dve.wait_ge(kexp, n + 1)
                nc.vector.scalar_tensor_tensor(dst, src, 0.0, SM[:, n % 2, :], ALU.max, ALU.add).then_inc(dve_evacuated, 1)

            for j in range(4):
                elu1(K1[:, 2 * j:2 * j + 2, :].rearrange("p t d -> p (t d)"), "k1", j, j)
            dve.wait_ge(blk_made, 1)
            src = full(dve, "kv1", 0)
            blk4 = blk.unsqueeze(1).broadcast_to([P, FC, P])
            nc.vector.tensor_tensor(kvT1, src[:, 0:D].rearrange("p (c n) -> p c n", c=FC), blk4, ALU.mult)
            hm8 = hm1.rearrange("p c (h r) -> p c h r", r=R)[:, :, :, 0]
            nc.vector.tensor_tensor(KS1, src[:, D:D + 32].rearrange("p (c h) -> p c h", c=FC), hm8, ALU.mult).then_inc(dve_evacuated, 1)
            for j in range(4):
                if j == 0:
                    dve.wait_ge(psum_full, INDEX[("kv1", 0)] + 1)
                elu1(QT1[:, j, :], "q1", j, 4 + j)
            for j in range(2):
                src = two(full(dve, "mixM1", j))
                dve.wait_ge(m1_rounded, j + 1)
                nc.vector.tensor_tensor(M1L[:, 2 * j:2 * j + 2, :], src, M1R[:, 2 * j:2 * j + 2, :].bitcast(fp32),
                                        ALU.subtract).then_inc(dve_evacuated, 1)
            src = full(dve, "den", 0)
            dve.wait_ge(z_cleared, 1)
            link(nc.vector.tensor_scalar(zT[0:8, :], src[0:8, :], 1e-6, None, ALU.add))
            nc.vector.reciprocal(zT[0:8, :], zT[0:8, :]).then_inc(dve_evacuated, 1)
            copy_out(GV[:, 0:2, :], "gv0", 0, two)
            for j in range(4):
                src = full(dve, "zb", j)
                nc.vector.tensor_tensor(QT1[:, j, :], QT1[:, j, :], src, ALU.mult).then_inc(dve_evacuated, 1)
            for j in range(4):
                dve.wait_ge(q1_scaled_rounded, j + 1)
                nc.vector.tensor_tensor(Q1L[:, j, :], QT1[:, j, :], Q1R[:, j, :].bitcast(fp32), ALU.subtract).then_inc(q1_scaled_split, 1)
            copy_out(GV[:, 4:6, :], "gv0", 2, two)
            dve.wait_ge(x1_biased, TT)
            for j in range(4):
                src = two(full(dve, "mixout1", j))
                nc.vector.tensor_tensor(X[:, 2 * j:2 * j + 2, :], src, X[:, 2 * j:2 * j + 2, :], ALU.add).then_inc(dve_evacuated, 1)

            def branch_and_norm(name, bias, g, be):
                for c in range(FC):
                    src = full(dve, name, c)
                    nc.vector.scalar_tensor_tensor(XT[:, c, :], src, col(bias, c), XT[:, c, :],
                                                   ALU.add, ALU.add).then_inc(dve_evacuated, 1)
                    done(dve, name, c)
                    nc.vector.bn_stats(st[:, 2 * c, :], XT[:, c, 0:D])
                    link(nc.vector.bn_stats(st[:, 2 * c + 1, :], XT[:, c, D:N]))
                    link(nc.vector.bn_aggr(mv[:, c, :], st[:, 2 * c:2 * c + 2, :]))
                    if c == FC - 2:
                        batchnorm(g, be, 0, FC - 1)
                batchnorm(g, be, FC - 1, FC)

            def batchnorm(g, be, c0, c1):
                std(c1, c0)
                scale, shift = bns[:, c0:c1], bns[:, FC + c0:FC + c1]
                link(nc.vector.tensor_tensor(scale, rstd[:, c0:c1], col(g)[:, c0:c1], ALU.mult))
                link(nc.vector.tensor_tensor(shift, mv[:, c0:c1, 0], scale, ALU.mult))
                nc.vector.tensor_tensor(shift, col(be)[:, c0:c1], shift, ALU.subtract).then_inc(bn_ready, 1)
                bn_rounds[0] += 1
                dve.wait_ge(bn_ready, bn_rounds[0])
                for c in range(c0, c1):
                    if c != FC - 2:
                        nc.vector.tensor_scalar(XT[:, c, :], XT[:, c, :], bns[:, c:c + 1], bns[:, 4 + c:5 + c],
                                                ALU.mult, ALU.add).then_inc(state_ready, 1)

            bn_rounds = [0]
            for l in range(L):
                if l:
                    for j in (0, 2):
                        copy_out(GV[:, 2 * j:2 * j + 2, :], f"gv{l}", j, two)
                for step, n in attention_order():
                    if step == "q":
                        if n or l:
                            dve.wait_ge(q_doubled, H * l + n)
                            dve.wait_ge(q_split, 2 * (H * l + n))
                        src = full(dve, f"q{l}g", n)
                        nc.vector.tensor_scalar(QF[:], src[:, 0:D], col(f"gbq{l}", n // 2), DH ** -0.5,
                                                ALU.add, ALU.mult).then_inc(dve_evacuated, 1)
                    elif step == "k":
                        src = full(dve, f"k{l}g", n)
                        for e in range(2):
                            own, other = slice(e * DH, (e + 1) * DH), slice((1 - e) * DH, (2 - e) * DH)
                            dve.wait_ge(k_rounded, 2 * (H // 2 * l + n) + e + 1)
                            last = nc.vector.tensor_tensor(KS[n % 2][other, e, :], src[own, :], KS[n % 2][own, e, :].bitcast(fp32),
                                                           ALU.subtract)
                            last.then_inc((k_split0, dve_evacuated)[e], 1)
                    elif step == "score":
                        src = full(dve, f"score{l}g", n)
                        if n >= SMB:
                            dve.wait_ge(psum_full, INDEX[(f"turn{l}g", n - SMB)] + 1)
                        elif n >= 2:
                            dve.wait_ge(psum_full, INDEX[("mixout1", 3) if l == 0 else ("turn0g", UNITS - 1)] + 1)
                        nc.vector.tensor_tensor_reduce(out=SMs[n % SMB], in0=src, in1=MASK[:, unit(n)[2], :],
                                                       scale=-1.0, scalar=-0.1 * NO_EDGE, op0=ALU.add, op1=ALU.min,
                                                       accum_out=nm[:, n % 8:n % 8 + 1]).then_inc(dve_evacuated, 1)
                    elif step == "turn":
                        if n % 2 == 0:
                            turned(dve, copy_out, l, n)
                    elif step == "rsum":
                        src = full(dve, f"rsum{l}g", n)
                        if n or l:
                            before = (f"rsum_bc{l}g", n - 1) if n else ("rsum_bc0g", H // 2 - 1)
                            dve.wait_ge(psum_full, INDEX[before] + 1)
                        nc.vector.tensor_copy(rT, src[0:16, 0:P]).then_inc(dve_evacuated, 1)
                    elif step == "rsum_bc":
                        done(dve, f"agg{l}g", 4 * n + 3)
                        src = full(dve, f"rsum_bc{l}g", n)
                        nc.vector.tensor_tensor(AG[:, n, :], AG[:, n, :], src, ALU.mult).then_inc(dve_evacuated, 1)
                    if step == "turn" and n % 16 == 15:
                        dve.wait_ge(probs, UNITS * l + n + 1)
                        if n > 16 or l:
                            dve.wait_ge(psum_full, INDEX[(f"rsum{l}g", n // 16 - 1) if n > 16 else ("rsum0g", H // 2 - 1)] + 1)
                        link(nc.vector.tensor_scalar(rl[:], ls[:, n // 16 % 2, :], 1e-16, None, ALU.add))
                        nc.vector.reciprocal(rl[:], rl[:]).then_inc(recips, 1)
                branch_and_norm(f"wo{l}", f"gbo{l}", f"g1{l}", f"be1{l}")
                dve.wait_ge(act_chunk_ready, 2 * l + 1)
                branch_and_norm(f"f{l}", f"gb2{l}", f"g2{l}", f"be2{l}")

            stats_of(lambda t: two(full(dve, "gT", t // 2) if t % 2 == 0 else slot_of("gT", t // 2))[:, t % 2, :])
            dve.wait_ge(dve_link, links[0])
            std(TT)
            row_ready(dve, "L1_gnn_ln_g")
            dve.wait_ge(shift_added, TT)
            made = {}

            def step(key, ins):
                ins.then_inc(dve_link, 1)
                links[0] += 1
                made[key] = links[0]

            for n in range(TT + 3):
                t = n
                if t < TT:
                    if t >= 2:
                        dve.wait_ge(dve_link, made["sum", t - 2])
                    src = two(slot_of("gT", t // 2))[:, t % 2, :]
                    ins = nc.vector.scalar_tensor_tensor(SM[:, t % 2, 0:D], src, mv[:, t, 0:1], row("L1_gnn_ln_g"),
                                                         ALU.subtract, ALU.mult)
                    if t % 2 == 0:
                        step(("scaled", t), ins)
                    else:
                        ins.then_inc(dve_evacuated, 1)
                t = n - 1
                if 0 <= t < TT:
                    if t % 2 == 0:
                        dve.wait_ge(dve_link, made["scaled", t])
                    else:
                        dve.wait_ge(*evacuated("gT", t // 2))
                    step(("sum", t), nc.vector.scalar_tensor_tensor(X[:, t, :], SM[:, t % 2, 0:D], rstd[:, t:t + 1],
                                                                     X[:, t, :], ALU.mult, ALU.add))
                t = n - 2
                if 0 <= t < TT:
                    dve.wait_ge(dve_link, made["sum", t])
                    step(("stats", t), nc.vector.bn_stats(st[:, t, :], X[:, t, :]))
                t = n - 3
                if 0 <= t < TT:
                    dve.wait_ge(dve_link, made["stats", t])
                    step(("moments", t), nc.vector.bn_aggr(mv[:, t, :], st[:, t, :]))
            dve.wait_ge(dve_link, links[0])
            std(TT)
            for t in range(TT):
                last = nc.vector.tensor_scalar(XN[:, t, 0:80], X[:, t, 0:80], mv[:, t, 0:1], rstd[:, t:t + 1],
                                               ALU.subtract, ALU.mult)
            link(last)
            nc.vector.tensor_scalar(sumc[:, 0, :], rstd[:], 1.0, None, ALU.add)
            nc.vector.scalar_tensor_tensor(sumc[:, 1, :], mv[:, :, 0], -1.0, rstd[:], ALU.mult, ALU.mult).then_inc(sum_ready, 1)
            dve.wait_ge(i16_made, 2)
            dve.wait_ge(hid_cleared, 1)
            nc.vector.tensor_scalar(flags[:, :, 0:1], XN[:, :, 0:1], 0.5, None, ALU.is_ge)
            nc.vector.tensor_scalar(flags[:, :, 1:4], XN[:, :, 1:4], 0.5, None, ALU.is_gt)
            link(nc.vector.tensor_scalar(bits, XN[:, :, 16:80].rearrange("p t (j n) -> p t j n", j=4), 0.5, None, ALU.is_gt))
            bf = bits.rearrange("p t j n -> p (t j) n")
            link(nc.vector.tensor_tensor(bf, bf, i16m.unsqueeze(1).broadcast_to([P, TT * 4, 16]), ALU.mult))
            mf = m16.rearrange("p t j -> p (t j)")
            link(nc.vector.tensor_reduce(mf, bf, AX.X, ALU.min))
            b0 = bits[:, :, 0, 0:4]
            link(nc.vector.tensor_scalar(b0, m16, 0.0, None, ALU.is_lt))
            nc.vector.scalar_tensor_tensor(F6[:, :, :, 0], m16[:, :, 0:2], 16.0, b0[:, :, 0:2], ALU.add, ALU.mult)
            nc.vector.scalar_tensor_tensor(F6[:, :, :, 1], m16[:, :, 2:4], 16.0, b0[:, :, 2:4], ALU.add, ALU.mult)
            for r in range(2):
                nc.vector.tensor_copy(F6[:, :, r, 2:4], XN[:, :, 2:4])
                last = nc.vector.tensor_copy(F6[:, :, r, 4:5], XN[:, :, 1:2])
            link(last)
            f6 = F6.rearrange("p t r j -> p (t r) j")
            nc.vector.tensor_copy(Fr[:, :, 64:70], f6)
            link(nc.vector.tensor_copy(Fr[:, :, 0:6], f6))
            nc.vector.tensor_tensor(Fr[:, :, 32:38], f6, Fr[:, :, 0:6].bitcast(fp32), ALU.subtract)
            nc.vector.tensor_tensor(Fr[:, :, 96:102], f6, Fr[:, :, 0:6].bitcast(fp32), ALU.subtract).then_inc(hid_ready, 1)
            copy_out(FT[:, 0:N], "fT", 0)
            nc.vector.tensor_copy(pick[:, :, 0:1], flags[:, :, 1:2])
            nc.vector.scalar_tensor_tensor(pick[:, :, 1:2], flags[:, :, 1:2], 0.5, flags[:, :, 2:3], ALU.is_lt, ALU.mult)
            link(nc.vector.tensor_tensor(pick[:, :, 2:3], flags[:, :, 1:2], flags[:, :, 2:3], ALU.max))
            nc.vector.tensor_tensor(act_on.unsqueeze(2), pick[:, :, 2:3], flags[:, :, 3:4], ALU.max)
            link(nc.vector.tensor_scalar(pick[:, :, 2:3], pick[:, :, 2:3], 0.5, None, ALU.is_lt))
            link(nc.vector.tensor_tensor(act_on.unsqueeze(2), act_on.unsqueeze(2), flags[:, :, 0:1], ALU.mult))
            for i in range(0, 2 * HG, 2):
                src = full(dve, "hid", i)
                nc.vector.tensor_scalar(HT[0:GU, i // 2, 0:N], src[0:GU, :], 0.0, None, ALU.max).then_inc(dve_evacuated, 1)
            copy_out(YS[:, 0:N], "y", 0)
            ykf = yk.rearrange("p t r k -> p (t r) k")
            for j in range(2):
                src = full(dve, "yT", j)
                nc.vector.tensor_reduce(ykf[:, j * TT:(j + 1) * TT, :],
                                        src.rearrange("p (n g k) -> p n k g", n=TT, g=HG)[:, :, 0:3, :],
                                        AX.X, ALU.add).then_inc(dve_evacuated, 1)
            dve.wait_ge(nib_loaded, 16 * NIB_LOADS)
            done(dve, "yT", 1)
            link(nc.vector.tensor_tensor(ykf, ykf, b2bc.unsqueeze(1).broadcast_to([P, 2 * TT, 3]), ALU.add))
            for r in range(2):
                last = nc.vector.tensor_tensor(ysel[:, :, r, :], yk[:, :, r, :], pick, ALU.mult)
            link(last)
            resf = res.rearrange("p t r -> p (t r)")
            link(nc.vector.tensor_reduce(resf, ysel.rearrange("p t r k -> p (t r) k"), AX.X, ALU.add))
            link(nc.vector.tensor_scalar(resf, resf, 0.0, 15.0, ALU.max, ALU.min))
            link(nc.vector.tensor_scalar(resf, resf, MAGIC, MAGIC, ALU.add, ALU.subtract))
            onef = oneh.rearrange("p t r n -> p (t r) n")
            link(nc.vector.tensor_tensor(onef, resf.unsqueeze(2).broadcast_to([P, 2 * TT, 16]),
                                         i16.unsqueeze(1).broadcast_to([P, 2 * TT, 16]), ALU.is_equal))
            onet = oneh.rearrange("p t r n -> p t (r n)")
            link(nc.vector.scalar_tensor_tensor(onet, onet, 2.0, act_on.unsqueeze(2).broadcast_to([P, TT, 32]),
                                                ALU.mult, ALU.mult))
            dve.wait_ge(out_summed, TT)
            nc.vector.tensor_tensor(X[:, :, 80:112], X[:, :, 80:112], onet, ALU.add).then_inc(nibbles_added, 1)

        @block.tensor
        def _(pe):
            waited = {}

            def wait(s, v):
                if waited.get(id(s), 0) < v:
                    pe.wait_ge(s, v)
                    waited[id(s)] = v

            def begin(name, i):
                j = INDEX[(name, i)]
                if j >= 4:
                    wait(*evacuated(*JOBS[j - 4][0]))
                return slot_of(name, i)

            def need(name, *idx):
                for i in idx:
                    wait(*evacuated(name, i))

            def mm(o_, lhsT, rhs, start, stop):
                return nc.tensor.matmul(o_, lhsT, rhs, start=start, stop=stop)

            def end(ins):
                ins.then_inc(psum_full, 1)

            def halves(slot, lhsT_of, rhs_of, n_k):
                for hf in range(2):
                    for k in range(n_k):
                        last = mm(slot[:, hf * D:(hf + 1) * D], lhsT_of(k), rhs_of(k)[:, hf * D:(hf + 1) * D], k == 0, k == n_k - 1)
                return last

            def parts(dst, lhsT_of, rhs_of, n_k):
                for k in range(n_k):
                    (a, al), (b, bl) = lhsT_of(k), rhs_of(k)
                    mm(dst, a, b, k == 0, False)
                    mm(dst, a, bl, False, False)
                    last = mm(dst, al, b, False, k == n_k - 1)
                return last

            def feature_major(name, w, src, count=FC, n_k=FC, first=0, ready=lambda k: None):
                for c in range(first, first + count):
                    slot = begin(name, c)
                    for k in range(n_k):
                        ready(k)
                        for hf in range(2):
                            hs = slice(hf * D, (hf + 1) * D)
                            last = mm(slot[:, hs], w[:, k, c * P:(c + 1) * P], src[:, k, hs], k == 0, k == n_k - 1)
                    end(last)

            def token_major(name, w, src, only=None, ready=lambda k: None):
                for j in range(4) if only is None else (only,):
                    slot = begin(name, j)
                    for k in range(FC):
                        ready(k)
                        for hf in range(2):
                            t = 2 * j + hf
                            last = mm(slot[:, hf * D:(hf + 1) * D], src[:, k, t * P:(t + 1) * P], w[:, k, :], k == 0, k == FC - 1)
                    end(last)

            def split_token_major(name, wr, wl, jobs=range(4)):
                xt = "xT1" if name == "ffn" else "xT2"
                for j in jobs:
                    slot = begin(name, j)
                    need(xt, j)
                    for hf in range(2):
                        ts = slice((2 * j + hf) * P, (2 * j + hf + 1) * P)
                        dst = slot[:, hf * D:(hf + 1) * D]
                        if wl is None:
                            for k in range(FC):
                                mm(dst, XTR[:, k, ts], wr[:, k, :], k == 0, False)
                                last = mm(dst, XTL[:, k, ts], wr[:, k, :], False, k == FC - 1)
                        else:
                            last = parts(dst, lambda k: (XTR[:, k, ts], XTL[:, k, ts]), lambda k: (wr[:, k, :], wl[:, k, :]), FC)
                    end(last)

            def split_weight(name):
                wait(w_split, SPLIT_WEIGHTS.index(name) + 1)
                return ROUNDED[name], WL[WSLOT[name]]

            def turn(slot_part, src):
                rows, n = src.shape[0], src.shape[1]
                return nc.tensor.transpose(slot_part, src, ident[0:rows, 0:rows])

            def xT(n):
                for j in range(4):
                    slot = begin(f"xT{n}", j)
                    pe.wait_ge(rows_normed, TT * n + 2 * j + 2)
                    for c in range(FC):
                        for t in (2 * j, 2 * j + 1):
                            at = (2 * c + t % 2) * P
                            last = turn(slot[:, at:at + P], XN[:, t, c * P:(c + 1) * P])
                    end(last)

            pe.wait_ge(const_made, 6)
            pe.wait_ge(mm_bounds, 1)
            slot = begin("bounds", 0)
            mm(slot[0:1, 0:P], cmin, ident[:], True, True)
            end(mm(slot[0:1, P:2 * P], cmax, ident[:], True, True))
            xT(0)
            pe.sem_inc(onehot_used, GC * SHIFT + GC)
            pe.wait_ge(bounds_made, 1)
            for t in range(TT):
                slot = begin("counts", t)
                first = pe.value_load(bnd_i[0:1, t:t + 1], min_val=0, max_val=NG - 1)
                end_ = pe.value_load(bnd_i[0:1, 8 + t:9 + t], min_val=0, max_val=NG)
                before = pe.value_load(bnd_i[0:1, 24 + t:25 + t], min_val=0, max_val=SHIFT + TT * NG)
                for hf in range(2):
                    mm(slot[:, hf * D:(hf + 1) * D], zeros[:, 0:P], zeros, True, False)
                with pe.Fori(first, end_) as g:
                    for b in range(GC):
                        pe.wait_ge(onehot_ready, (g + before) * GC + b + 1)
                        mm(slot[:, 0:D], dstrow[:, b, :], srcrow[:, b, 0:D], False, False)
                        mm(slot[:, D:N], dstrow[:, b, :], srcrow[:, b, D:N], False, False).then_inc(onehot_used, 1)
                for hf in range(2):
                    last = mm(slot[:, hf * D:(hf + 1) * D], zeros[:, 0:P], zeros, False, True)
                end(last)
            need("counts", *range(TT))
            need("xT0", *range(FC))
            pe.wait_ge(bd_loaded, 16 * 18)

            def mixer_step(name):
                if name == "wqk":
                    w_ready(pe, "winT")
                    wt = wtile("winT")
                    slot = begin("wqk", 0)
                    for c in range(FC):
                        for k in range(FC):
                            last = mm(slot[:, 64 * c:64 * c + 64], wt[:, k, c * P:(c + 1) * P], bdqk[:, k, :], k == 0, k == FC - 1)
                elif name == "bq0":
                    pe.wait_ge(bias_spread, 1)
                    slot = begin("bq0", 0)
                    for k in range(FC):
                        last = mm(slot[:, 0:32], b_bc[:, k, :], bdqk[:, k, 0:32], k == 0, k == FC - 1)
                elif name == "bk0":
                    slot = begin("bk0", 0)
                    for k in range(FC):
                        last = mm(slot[0:32, 0:1], bdqk[:, k, 32:64], col("b_in", k), k == 0, k == FC - 1)
                elif name == "klog":
                    need("wqk", 0)
                    slot = begin("klog", 0)
                    last = halves(slot[0:32, :], lambda k: wqk[:, k, 32:64], lambda k: XT[:, k, :], FC)
                elif name == "qlog":
                    slot = begin("qlog", 0)
                    for t in range(TT):
                        for k in range(FC):
                            last = mm(slot[:, 32 * t:32 * t + 32], XT[:, k, t * P:(t + 1) * P], wqk[:, k, 0:32], k == 0, k == FC - 1)
                elif name == "ekt":
                    slot = begin("ekt", 0)
                    pe.wait_ge(keys_exp, 1)
                    for t in range(TT):
                        last = turn(slot[:, 32 * t:32 * t + 32], ekT[:, t * P:(t + 1) * P])
                elif name == "kx":
                    slot = begin("kx", 0)
                    need("ekt", 0)
                    for t in range(TT):
                        last = mm(slot[0:32, 0:D], ek[:, t, :], XN[:, t, :], t == 0, t == TT - 1)
                elif name == "kxT":
                    slot = begin("kxT", 0)
                    need("kx", 0)
                    for c in range(FC):
                        last = turn(slot[:, 32 * c:32 * c + 32], kx[:, c * P:(c + 1) * P])
                elif name == "xmT":
                    slot = begin("xmT", 0)
                    need("kxT", 0)
                    w_ready(pe, "win")
                    wi = wtile("win")
                    for c in range(FC):
                        for k in range(FC):
                            last = mm(slot[:, 32 * c:32 * c + 32], wi[:, k, c * P:(c + 1) * P], kxT[:, k, :], k == 0, k == FC - 1)
                elif name == "kvT":
                    slot = begin("kvT", 0)
                    need("xmT", 0)
                    for c in range(FC):
                        last = mm(slot[:, 32 * c:32 * c + 32], bdv, xmT[:, c, :], True, True)
                elif name == "mixM":
                    slot = begin("mixM", 0)
                    need("kvT", 0)
                    w_ready(pe, "wout")
                    for c in range(FC):
                        last = mm(slot[0:32, 0:D], kvT[:, c, :], wtile("wout")[:, c, :], c == 0, c == FC - 1)
                elif name == "qsT":
                    slot = begin("qsT", 0)
                    pe.wait_ge(queries_normed, 1)
                    for t in range(TT):
                        last = turn(slot[0:32, t * P:(t + 1) * P], ql[:, t, :])
                end(last)

            for name, i in MIXER0_ORDER:
                if name == "adjT":
                    slot = begin("adjT", i)
                    for s in range(TT):
                        last = turn(slot[:, s * P:(s + 1) * P], MASK[:, s, i * P:(i + 1) * P])
                    end(last)
                elif name in ("v0", "k0", "q0"):
                    if i == 0:
                        w_ready(pe, name)
                    if name == "v0":
                        token_major(name, wtile(name), XT, only=i)
                    else:
                        feature_major(name, wtile(name), XT, count=1, first=i)
                elif name == "mixout":
                    need("mixM", 0)
                    need("qsT", 0)
                    slot = begin("mixout", i)
                    for hf in range(2):
                        t = 2 * i + hf
                        last = mm(slot[:, hf * D:(hf + 1) * D], qsT[:, t * P:(t + 1) * P], mixM, True, True)
                    end(last)
                else:
                    mixer_step(name)
            need("q0", 2, 3)
            pe.wait_ge(k0_split, FC)
            for n in range(TT + LAG0 + 1):
                if n == 7:
                    slot = begin("wsum", 0)
                    pe.wait_ge(wstat, 1)
                    end(mm(slot[:, 0:2], ones[:], tiny[:, 0:2], True, True))
                if n < TT:
                    slot = begin("score0", n)
                    pe.wait_ge(q0_split, n + 1)
                    ns = slice(n * P, (n + 1) * P)
                    for hf in range(2):
                        hs = slice(hf * D, (hf + 1) * D)
                        last = parts(slot[:, hs], lambda k: (Q0R[:, k, ns], Q0L[:, k, ns]),
                                     lambda k: (K0R[:, k, hs], K0L[:, k, hs]), FC)
                    end(last)
                i = n - LAG0
                if 0 <= i < TT:
                    slot = begin("turn0", i)
                    pe.wait_ge(probs0, i + 1)
                    for s in range(TT):
                        last = turn(slot[:, s * P:(s + 1) * P], SM[:, i % 2, s * P:(s + 1) * P])
                    end(last)
                i = n - LAG0 - 1
                if i >= 0:
                    slot = begin("attn0", i)
                    wait(v0_split, 4)
                    need("turn0", i)
                    end(parts(slot[:, 0:D], lambda s: (P0R[:, s, :], P0L[:, s, :]), lambda s: (V0R[:, s, :], V0L[:, s, :]), TT))
            xT(1)
            pe.wait_ge(wsign, 1)
            split_token_major("ffn", WL[WSLOT["ffn"]], None)
            xT(2)
            for name in ("k1", "v1"):
                split_token_major(name, *split_weight(name))
            pe.wait_ge(blk_made, 1)
            need("k1", 3)
            need("v1", 3)
            slot = begin("kv1", 0)
            for c in range(FC):
                cs = slice(c * P, (c + 1) * P)
                for t in range(TT):
                    mm(slot[:, cs], V1[:, t, cs], K1[:, t, cs], t == 0, t == TT - 1)
                for t in range(TT):
                    last = mm(slot[:, D + 8 * c:D + 8 * (c + 1)], K1[:, t, cs], ones[:, 0:8], t == 0, t == TT - 1)
            end(last)
            wr, wl = split_weight("q1")
            for c in range(FC):
                slot = begin("q1", c)
                cs = slice(c * P, (c + 1) * P)
                for hf in range(2):
                    hs = slice(hf * D, (hf + 1) * D)
                    last = parts(slot[:, hs], lambda k: (wr[:, k, cs], wl[:, k, cs]), lambda k: (XTR[:, k, hs], XTL[:, k, hs]), FC)
                end(last)
            w_ready(pe, "wout1")
            need("kv1", 0)
            for j in range(2):
                slot = begin("mixM1", j)
                for hf in range(2):
                    c = 2 * j + hf
                    last = mm(slot[:, hf * D:(hf + 1) * D], kvT1[:, c, :], wtile("wout1")[:, c, :], True, True)
                end(last)
            slot = begin("den", 0)
            need("q1", *range(FC))
            end(halves(slot[0:8, :], lambda k: KS1[:, k, :], lambda k: QT1[:, k, :], FC))
            split_token_major("gv0", *split_weight("gv0"), jobs=(0, 1))
            need("den", 0)
            for c in range(FC):
                slot = begin("zb", c)
                end(halves(slot, lambda k: selh[:, c, :], lambda k: zT, 1))
            split_token_major("gv0", *split_weight("gv0"), jobs=(2, 3))
            need("mixM1", 0, 1)
            wait(q1_scaled_split, 4)
            for j in range(4):
                slot = begin("mixout1", j)
                for hf in range(2):
                    ts = slice((2 * j + hf) * P, (2 * j + hf + 1) * P)
                    last = parts(slot[:, hf * D:(hf + 1) * D], lambda k: (Q1R[:, k, ts], Q1L[:, k, ts]),
                                 lambda k: (M1R[:, k, :], M1L[:, k, :]), FC)
                end(last)
            def state(n, c):
                if c == FC - 2:
                    wait(act_chunk_ready, n)
                else:
                    wait(state_ready, 3 * n - 2 + min(c, 2))

            def aggregate(slot, l, g, tiles):
                for s in tiles:
                    for e in range(2):
                        head = 2 * (g // 4) + e
                        last = mm(slot[e * DH:(e + 1) * DH, 0:2 * P], GV[:, s, head * DH:(head + 1) * DH],
                                  PTr[:, g % 2, e, s, :], s == 0, s == TT - 1)
                return last

            def project(slot, l, chunks):
                for k in chunks:
                    need(f"rsum_bc{l}g", k)
                    for hf in range(2):
                        hs = slice(hf * D, (hf + 1) * D)
                        last = mm(slot[:, hs], wtile(f"go{l}")[:, k, 0:P], AG[:, k, hs], k == 0, k == FC - 1)
                return last

            for l in range(L):
                if l:
                    w_ready(pe, f"gv{l}")
                    token_major(f"gv{l}", wtile(f"gv{l}"), XT, ready=lambda k: state(2 * l, k))
                w_ready(pe, f"gq{l}")
                wait(x_whole, 4)
                for step, n in attention_order():
                    if step == "agg_start":
                        slot = begin(f"agg{l}g", n)
                        need(f"gv{l}", 2, 3)
                        need(f"turn{l}g", 4 * n + 2, 4 * n + 3)
                        aggregate(slot, l, n, range(0, TT // 2))
                        continue
                    slot = begin(f"{step}{l}g", n) if step != "agg" else slot_of(f"agg{l}g", n)
                    if step == "q":
                        pair, hf = n // 2, n % 2
                        w = wtile(f"gq{l}")
                        for k in range(FC):
                            last = mm(slot[:, 0:D], w[:, k, pair * P:(pair + 1) * P], XT[:, k, hf * D:(hf + 1) * D],
                                      k == 0, k == FC - 1)
                        end(last)
                    elif step == "k":
                        if n == 0:
                            w_ready(pe, f"gk{l}")
                        w = wtile(f"gk{l}")
                        end(halves(slot, lambda k: w[:, k, n * P:(n + 1) * P], lambda k: XT[:, k, :], FC))
                    elif step == "score":
                        pair, e, t = unit(n)
                        b = n // 8
                        wait(q_doubled, H * l + b + 1)
                        wait(q_split, 2 * (H * l + b + 1))
                        wait(q_cleared, 2)
                        if e == 0:
                            wait(k_split0, H // 2 * l + pair + 1)
                        else:
                            need(f"k{l}g", pair)
                        end(halves(slot, lambda k: QS[:, b % 2, e, k, t % 4 * P:(t % 4 + 1) * P],
                                   lambda k: KS[pair % 2][:, e, :], 2))
                    elif step == "turn":
                        wait(probs, UNITS * l + n + 1)
                        for s in range(TT):
                            last = turn(slot[:, s * P:(s + 1) * P], SMs[n % SMB][:, s * P:(s + 1) * P])
                        end(last)
                    elif step == "rsum":
                        wait(recips, H // 2 * l + n + 1)
                        end(turn(slot[0:16, 0:P], rl[:]))
                        if n == H // 2 - 1:
                            w_ready(pe, f"go{l}")
                            wo_slot = begin(f"wo{l}", 0)
                            project(wo_slot, l, (0, 1))
                    elif step == "rsum_bc":
                        need(f"rsum{l}g", n)
                        wait(sel_made, 1)
                        for t in range(TT):
                            last = mm(slot[:, t * P:(t + 1) * P], sel[:, t, :], rT, True, True)
                        end(last)
                    elif step == "agg":
                        end(aggregate(slot, l, n, range(TT // 2, TT)))
                end(project(wo_slot, l, (2, 3)))
                feature_major(f"wo{l}", wtile(f"go{l}"), AG, count=FC - 1, first=1)
                w_ready(pe, f"w12{l}")
                ws = W[:, WSLOT[f"w12{l}"], :]
                feature_major(f"h{l}", ws[:, 0:1024].rearrange("p (k n) -> p k n", k=FC), XT, count=2,
                              ready=lambda k: state(2 * l + 1, k))
                need(f"h{l}", 0, 1)
                feature_major(f"f{l}", ws[:, 1024:2048].rearrange("p (k n) -> p k n", k=2), KR, n_k=2)
            def turn_chunks(j, chunks):
                for c in chunks:
                    state(2 * L, c)
                    for hf in range(2):
                        t = 2 * j + hf
                        last = turn(slot_of("gT", j)[:, hf * D + c * P:hf * D + (c + 1) * P], XT[:, c, t * P:(t + 1) * P])
                return last

            for j in range(4):
                begin("gT", j)
                turn_chunks(j, range(FC - 1))
            for j in range(4):
                end(turn_chunks(j, [FC - 1]))
            pe.wait_ge(hid_ready, 1)
            for q in range(2):
                slot = begin("fT", q)
                for n in range(TT):
                    last = turn(slot[:, n * P:(n + 1) * P], Fr[:, q * TT + n, :].bitcast(fp32))
                end(last)
            pe.wait_ge(w1_split, 1)
            for i in range(2 * HG):
                slot = begin("hid", i)
                need("fT", i % 2)
                for hf in range(2):
                    at = i % 2 * N + hf * D
                    last = mm(slot[0:GU, hf * D:(hf + 1) * D], W1r[:, i // 2 * GU:(i // 2 + 1) * GU], FT[:, at:at + D], True, True)
                end(last)
            for j in range(2):
                slot = begin("y", j)
                for g in range(HG):
                    need("hid", 2 * g + j)
                for hf in range(2):
                    at = j * N + hf * D
                    for g in range(HG):
                        last = mm(slot[32 * g:32 * g + 32, hf * D:(hf + 1) * D], w2m[0:GU, g, :], HT[0:GU, g, at:at + D], True, True)
                end(last)
            for j in range(2):
                slot = begin("yT", j)
                need("y", j)
                for n in range(TT):
                    last = turn(slot[:, n * P:(n + 1) * P], YS[:, (j * TT + n) * P:(j * TT + n + 1) * P])
                end(last)


def kernel(**inputs):
    import concourse.bacc as bacc
    from concourse.bass_utils import run_bass_kernel_spmd

    g = {k: np.asarray(v) for k, v in inputs.items()}

    def chunks(v):
        return v.reshape(-1, P).T

    src, dst = g["src"].reshape(EC, P), g["dst"].reshape(EC, P)
    vec = {"bq": g["L0_gnn_bq"], "bk": g["L0_gnn_bk"], "b_in": g["L0_mix_b_in"]}
    names = {"gbq": "bq", "gbo": "bo", "gb2": "b2", "g1": "g1", "be1": "beta1", "g2": "g2", "be2": "beta2", "gb1": "b1"}
    for l in range(L):
        vec.update({f"{k}{l}": g[f"L1_gnn_{v}"][l] for k, v in names.items()})
    wqkv = g["L1_mix_Wqkv"]
    nets = ("and", "or", "xor")
    arrays = {
        "idx": np.concatenate([dst.T, src.T, dst], axis=1),
        "x": g["x"],
        "cols": np.concatenate([chunks(vec[n]) for n in COLS], axis=1),
        "rows": np.stack([g[n] for n in ROWS]),
        "q0": g["L0_gnn_Wq"], "k0": g["L0_gnn_Wk"], "v0": g["L0_gnn_Wv"],
        "winT": g["L0_mix_W_in"].T, "win": g["L0_mix_W_in"], "wout": g["L0_mix_W_out"],
        "mq": g["L0_mix_W_q"], "mk": g["L0_mix_W_k"], "mv": g["L0_mix_W_v"],
        "ffn": g["L0_ffn_weight"],
        "q1": wqkv[:, 0:D], "k1": wqkv[:, D:2 * D], "v1": wqkv[:, 2 * D:3 * D], "wout1": g["L1_mix_Wout"],
        "nw1": np.stack([g[f"L1_ffn_{k}_w1"] for k in nets]),
        "nb1": np.concatenate([g[f"L1_ffn_{k}_b1"] for k in nets])[None],
        "nw2": np.stack([g[f"L1_ffn_{k}_w2"][:, 64] for k in nets]),
        "nb2": np.stack([g[f"L1_ffn_{k}_b2"][64:65] for k in nets], axis=1),
    }
    for l in range(L):
        for k in "qkvo":
            arrays[f"g{k}{l}"] = g[f"L1_gnn_W{k}"][l].T
    fold = lambda w: w.reshape(-1, P, w.shape[1]).transpose(1, 0, 2).reshape(P, -1)
    arrays["w12"] = np.stack([np.concatenate([fold(g["L1_gnn_W1"][l].T), fold(g["L1_gnn_W2"][l].T)], axis=1)
                              for l in range(L)])

    nc = bacc.Bacc("TRN2", target_bir_lowering=False, num_devices=1)
    feed, aps = {}, {}
    for name, v in arrays.items():
        v = np.ascontiguousarray(v)
        feed[f"in_{name}"] = v
        aps[name] = nc.dram_tensor(f"in_{name}", v.shape, mybir.dt.from_np(v.dtype), kind="ExternalInput").ap()
    out = nc.dram_tensor("out_0", (N, D), mybir.dt.float32, kind="ExternalOutput").ap()
    build(nc, aps, out)
    r = run_bass_kernel_spmd(nc, [feed], core_ids=[0])
    return r.results[0]["out_0"]
```
